# Optimizing a Trainium2 kernel written in Bass

```python
import numpy as np
import jax
import jax.numpy as jnp

def _softmax(x, axis=-1):
    return jax.nn.softmax(x, axis=axis)

def _gelu(x):
    return jax.nn.gelu(x, approximate=True)

def _silu(x):
    return jax.nn.silu(x)

def _sigmoid(x):
    return jax.nn.sigmoid(x)

def _layernorm(x, axis=-1, eps=1e-05):
    m = jnp.mean(x, axis=axis, keepdims=True)
    v = jnp.var(x, axis=axis, keepdims=True)
    return (x - m) / jnp.sqrt(v + eps)

def _scatter_add(tgt, idx, src, axis=0):
    return tgt.at[idx].add(src)

def _segment_sum(src, seg, n):
    return jax.ops.segment_sum(src, seg, n)
kernel_name = 'mk_decoder_postln_d2_seqx_r8_4f7d73'

def setup_inputs(seed: int=0):
    np.random.seed(seed)
    _w = jnp.asarray

    def _rec_inputs():
        import jax
        import jax.numpy as jnp
        _rk = jax.random.key(seed)
        x = 7.22e-05 + 1 * jax.random.normal(jax.random.fold_in(_rk, 1), (32, 128, 128), jnp.float32)
        _lenS = 128 - jax.random.randint(jax.random.fold_in(_rk, 7), (32,), 0, max(1, 128 // 4) + 1, jnp.int32)
        _lenS2 = 77 - jax.random.randint(jax.random.fold_in(_rk, 8), (32,), 0, max(1, 77 // 4) + 1, jnp.int32)
        _ctx_768P = jax.random.normal(jax.random.fold_in(_rk, 11), (32, 16, 96), jnp.float32)
        _ctx_768c = jax.random.dirichlet(jax.random.fold_in(_rk, 511), 0.3 * jnp.ones((16,), jnp.float32), (32, 77))
        _ctx_768t = jnp.einsum('bsk,bkd->bsd', _ctx_768c, _ctx_768P)
        _ctx_768t = _ctx_768t * jax.lax.rsqrt(jnp.mean(jnp.square(_ctx_768t)) + 1e-12) * 0.953939
        ctx_768 = -0.000191848 + 0.999787 * (_ctx_768t + 0.3 * jax.random.normal(jax.random.fold_in(_rk, 611), (32, 77, 96), jnp.float32))
        return (x, ctx_768)
    x, ctx_768 = _rec_inputs()

    def _L0_attn_setup():
        import jax, jax.numpy as jnp
        import numpy as np
        from jax import lax
        L, B, S, D, H = (2, 8, 256, 128, 128)
        LOG_H0 = float(np.log(0.5))

        def _log_g(x):
            return jnp.where(x >= 0, jnp.log(jnp.where(x >= 0, x + 0.5, 1.0)), -jax.nn.softplus(-x))

        def _mingru_layer(x, Wz, bz, Wh, bh):
            k = jnp.einsum('bsd,hd->bsh', x, Wz) + bz
            log_z = -jax.nn.softplus(-k)
            log_coeffs = -jax.nn.softplus(k)
            pre_h = jnp.einsum('bsd,hd->bsh', x, Wh) + bh
            log_values = log_z + _log_g(pre_h)
            Bq = x.shape[0]
            log_coeffs = jnp.pad(log_coeffs, ((0, 0), (1, 0), (0, 0)))
            log_values = jnp.concatenate([jnp.full((Bq, 1, log_values.shape[-1]), LOG_H0, dtype=log_values.dtype), log_values], axis=1)
            a_star = jnp.cumsum(log_coeffs, axis=1)
            log_h = a_star + lax.cumlogsumexp(log_values - a_star, axis=1)
            return jnp.exp(log_h)[:, 1:]
        key = jax.random.key(seed)
        ks = jax.random.split(key, 5)
        stdv = 1.0 / np.sqrt(D)
        u = lambda k, shp: jax.random.uniform(k, shp, jnp.float32, -stdv, stdv)
        return {'x': jax.random.normal(ks[0], (B, S, D), jnp.float32), 'Wz': u(ks[1], (L, H, D)), 'bz': u(ks[2], (L, H)), 'Wh': u(ks[3], (L, H, D)), 'bh': u(ks[4], (L, H))}
    _L0_attn_all = _L0_attn_setup()
    _L0_attn_in = {k: v for k, v in _L0_attn_all.items() if k in ('Wz', 'bz', 'Wh', 'bh')}
    del _L0_attn_all

    def _L0_xattn_setup():
        import jax, jax.numpy as jnp
        import numpy as np
        NUM_HEADS = 16
        CLAMP = 10000.0
        key = jax.random.key(seed)
        ks = jax.random.split(key, 8)
        B, Nq, Nkv, Cq, Ckv = (4, 256, 256, 128, 96)
        s_q = 1.0 / np.sqrt(Cq)
        s_kv = 1.0 / np.sqrt(Ckv)
        return {'query': jax.random.normal(ks[0], (B, Nq, Cq), jnp.float32), 'key_value': jax.random.normal(ks[1], (B, Nkv, Ckv), jnp.float32), 'Wq': jax.random.normal(ks[2], (Cq, Cq), jnp.float32) * s_q, 'bq': jnp.zeros((Cq,), jnp.float32), 'Wk': jax.random.normal(ks[3], (Ckv, Cq), jnp.float32) * s_kv, 'bk': jnp.zeros((Cq,), jnp.float32), 'Wv': jax.random.normal(ks[4], (Ckv, Cq), jnp.float32) * s_kv, 'bv': jnp.zeros((Cq,), jnp.float32), 'Wo': jax.random.normal(ks[5], (Cq, Cq), jnp.float32) * s_q, 'bo': jnp.zeros((Cq,), jnp.float32)}
    _L0_xattn_all = _L0_xattn_setup()
    _L0_xattn_in = {k: v for k, v in _L0_xattn_all.items() if k in ('Wq', 'bq', 'Wk', 'bk', 'Wv', 'bv', 'Wo', 'bo')}
    del _L0_xattn_all

    def _L0_ffn_setup():
        import jax, jax.numpy as jnp
        import numpy as np
        E = 16
        K = 2
        LOAD = 1.0

        def _dispatch(xb, pb, cap):
            T, C = xb.shape
            top_k_probs, ei = jax.lax.top_k(pb, K)
            flat = ei.swapaxes(0, 1).ravel()
            one_hot = jax.nn.one_hot(flat, E, dtype=jnp.int32)
            pos = jnp.cumsum(one_hot, axis=0) * one_hot
            pos = pos.reshape(K, T, E).swapaxes(0, 1)
            pos = jnp.max(pos, axis=-1) - 1
            ei2 = flat.reshape(K, T).swapaxes(0, 1)
            xr = jnp.repeat(xb, K, axis=0)
            buf = jnp.zeros((E, cap, C), xb.dtype)
            buf = buf.at[ei2.ravel(), pos.ravel()].set(xr, mode='drop')
            return (top_k_probs, pos, ei2, buf)

        def _collect(eo_b, ei_b, pos_b, tk_b):
            out = eo_b[ei_b, pos_b]
            return jnp.sum(tk_b[..., None] * out, axis=1)
        key = jax.random.key(seed)
        k1, k2, k3, k4, k5 = jax.random.split(key, 5)
        B, T, C, H = (8, 512, 128, 64)
        n_layer = 12
        x = jax.random.normal(k1, (B, T, C), dtype=jnp.float32)
        w_router = jax.random.normal(k2, (C, E), dtype=jnp.float32) * 0.02
        w_fc = jax.random.normal(k3, (E, C, H), dtype=jnp.float32) * 0.02
        w_gate = jax.random.normal(k4, (E, C, H), dtype=jnp.float32) * 0.02
        w_proj = jax.random.normal(k5, (E, H, C), dtype=jnp.float32) * (0.02 * (2 * n_layer) ** (-0.5))
        return {'x': x, 'w_router': w_router, 'w_fc': w_fc, 'w_gate': w_gate, 'w_proj': w_proj}
    _L0_ffn_all = _L0_ffn_setup()
    _L0_ffn_in = {k: v for k, v in _L0_ffn_all.items() if k in ('w_router', 'w_fc', 'w_gate', 'w_proj')}
    del _L0_ffn_all

    def _L1_attn_setup():
        import jax, jax.numpy as jnp
        import numpy as np
        D_MODEL = 128
        N_HEADS = 16
        D_HEAD = D_MODEL // N_HEADS
        BLOCK = 128
        B, T = (2, 256)

        def _flash_attention(Q, K, V, block_size, scale):
            Bb, H, Tt, d = Q.shape
            n_blocks = Tt // block_size
            Kb = K.reshape(Bb, H, n_blocks, block_size, d).transpose(2, 0, 1, 3, 4)
            Vb = V.reshape(Bb, H, n_blocks, block_size, d).transpose(2, 0, 1, 3, 4)
            starts = jnp.arange(n_blocks) * block_size
            q_pos = jnp.arange(Tt)

            def step(carry, xs):
                m, l, acc = carry
                kb, vb, st = xs
                scores = scale * jnp.einsum('bhtd,bhsd->bhts', Q, kb)
                kv_pos = st + jnp.arange(block_size)
                future = kv_pos[None, :] > q_pos[:, None]
                scores = jnp.where(future[None, None], -jnp.inf, scores)
                m_new = jnp.maximum(m, jnp.max(scores, axis=-1, keepdims=True))
                p = jnp.exp(scores - m_new)
                corr = jnp.exp(m - m_new)
                l = corr * l + jnp.sum(p, axis=-1, keepdims=True)
                acc = corr * acc + jnp.einsum('bhts,bhsd->bhtd', p, vb)
                return ((m_new, l, acc), None)
            m0 = jnp.full((Bb, H, Tt, 1), -jnp.inf, dtype=jnp.float32)
            l0 = jnp.zeros((Bb, H, Tt, 1), dtype=jnp.float32)
            a0 = jnp.zeros((Bb, H, Tt, d), dtype=jnp.float32)
            (m, l, acc), _ = jax.lax.scan(step, (m0, l0, a0), (Kb, Vb, starts))
            return acc / jnp.maximum(l, 1e-12)
        key = jax.random.key(seed)
        ks = jax.random.split(key, 5)
        x = jax.random.normal(ks[0], (B, T, D_MODEL), dtype=jnp.float32)

        def init_w(k):
            return jax.random.normal(k, (D_MODEL, D_MODEL), dtype=jnp.float32) / np.sqrt(D_MODEL).astype(np.float32)
        return {'x': x, 'Wq': init_w(ks[1]), 'Wk': init_w(ks[2]), 'Wv': init_w(ks[3]), 'Wo': init_w(ks[4])}
    _L1_attn_all = _L1_attn_setup()
    _L1_attn_in = {k: v for k, v in _L1_attn_all.items() if k in ('Wq', 'Wk', 'Wv', 'Wo')}
    del _L1_attn_all

    def _L1_xattn_setup():
        import jax, jax.numpy as jnp
        import numpy as np
        HEADS = 16
        DIM_HEAD = 64
        SCALE = DIM_HEAD ** (-0.5)
        QUERY_DIM = 128
        CONTEXT_DIM = 96
        INNER_DIM = HEADS * DIM_HEAD
        key = jax.random.key(seed)
        ks = jax.random.split(key, 7)
        B, Nq, Nk = (8, 512, 77)
        x = jax.random.normal(ks[0], (B, Nq, QUERY_DIM), dtype=jnp.float32)
        context = jax.random.normal(ks[1], (B, Nk, CONTEXT_DIM), dtype=jnp.float32)
        Wq = jax.random.normal(ks[2], (QUERY_DIM, INNER_DIM), dtype=jnp.float32) * QUERY_DIM ** (-0.5)
        Wk = jax.random.normal(ks[3], (CONTEXT_DIM, INNER_DIM), dtype=jnp.float32) * CONTEXT_DIM ** (-0.5)
        Wv = jax.random.normal(ks[4], (CONTEXT_DIM, INNER_DIM), dtype=jnp.float32) * CONTEXT_DIM ** (-0.5)
        Wo = jax.random.normal(ks[5], (INNER_DIM, QUERY_DIM), dtype=jnp.float32) * INNER_DIM ** (-0.5)
        bo = jnp.zeros((QUERY_DIM,), dtype=jnp.float32)
        return {'x': x, 'context': context, 'Wq': Wq, 'Wk': Wk, 'Wv': Wv, 'Wo': Wo, 'bo': bo}
    _L1_xattn_all = _L1_xattn_setup()
    _L1_xattn_in = {k: v for k, v in _L1_xattn_all.items() if k in ('Wq', 'Wk', 'Wv', 'Wo', 'bo')}
    del _L1_xattn_all

    def _L1_ffn_setup():
        import jax, jax.numpy as jnp
        import numpy as np
        N_HEADS = 16
        NUM_EXPERTS = 4
        TOP_K = 2
        D_MODEL = 128
        GATE_HID = 128
        key = jax.random.key(seed)
        ks = jax.random.split(key, 12)
        B, T, C, E = (2, 128, D_MODEL, NUM_EXPERTS)
        s = 1.0 / np.sqrt(C)
        return {'hidden_states': jax.random.normal(ks[0], (B, T, C), jnp.float32), 'Wq': jax.random.normal(ks[1], (E, C, C), jnp.float32) * s, 'bq': jnp.zeros((E, C), jnp.float32), 'Wk': jax.random.normal(ks[2], (E, C, C), jnp.float32) * s, 'bk': jnp.zeros((E, C), jnp.float32), 'Wv': jax.random.normal(ks[3], (E, C, C), jnp.float32) * s, 'bv': jnp.zeros((E, C), jnp.float32), 'Wg1': jax.random.normal(ks[4], (C, GATE_HID), jnp.float32) * s, 'bg1': jnp.zeros((GATE_HID,), jnp.float32), 'Wg2': jax.random.normal(ks[5], (GATE_HID, E), jnp.float32) / np.sqrt(GATE_HID), 'bg2': jnp.zeros((E,), jnp.float32), 'Wo': jax.random.normal(ks[6], (C, C), jnp.float32) * s, 'bo': jnp.zeros((C,), jnp.float32)}
    _L1_ffn_all = _L1_ffn_setup()
    _L1_ffn_in = {k: v for k, v in _L1_ffn_all.items() if k in ('Wq', 'bq', 'Wk', 'bk', 'Wv', 'bv', 'Wg1', 'bg1', 'Wg2', 'bg2', 'Wo', 'bo')}
    del _L1_ffn_all
    return {'x': x, 'ctx_768': ctx_768, 'L0_attn_Wz': _L0_attn_in['Wz'], 'L0_attn_bz': _L0_attn_in['bz'], 'L0_attn_Wh': _L0_attn_in['Wh'], 'L0_attn_bh': _L0_attn_in['bh'], 'L0_xattn_Wq': _L0_xattn_in['Wq'], 'L0_xattn_bq': _L0_xattn_in['bq'], 'L0_xattn_Wk': _L0_xattn_in['Wk'], 'L0_xattn_bk': _L0_xattn_in['bk'], 'L0_xattn_Wv': _L0_xattn_in['Wv'], 'L0_xattn_bv': _L0_xattn_in['bv'], 'L0_xattn_Wo': _L0_xattn_in['Wo'], 'L0_xattn_bo': _L0_xattn_in['bo'], 'L0_ffn_w_router': _L0_ffn_in['w_router'], 'L0_ffn_w_fc': _L0_ffn_in['w_fc'], 'L0_ffn_w_gate': _L0_ffn_in['w_gate'], 'L0_ffn_w_proj': _L0_ffn_in['w_proj'], 'L1_attn_Wq': _L1_attn_in['Wq'], 'L1_attn_Wk': _L1_attn_in['Wk'], 'L1_attn_Wv': _L1_attn_in['Wv'], 'L1_attn_Wo': _L1_attn_in['Wo'], 'L1_xattn_Wq': _L1_xattn_in['Wq'], 'L1_xattn_Wk': _L1_xattn_in['Wk'], 'L1_xattn_Wv': _L1_xattn_in['Wv'], 'L1_xattn_Wo': _L1_xattn_in['Wo'], 'L1_xattn_bo': _L1_xattn_in['bo'], 'L1_ffn_Wq': _L1_ffn_in['Wq'], 'L1_ffn_bq': _L1_ffn_in['bq'], 'L1_ffn_Wk': _L1_ffn_in['Wk'], 'L1_ffn_bk': _L1_ffn_in['bk'], 'L1_ffn_Wv': _L1_ffn_in['Wv'], 'L1_ffn_bv': _L1_ffn_in['bv'], 'L1_ffn_Wg1': _L1_ffn_in['Wg1'], 'L1_ffn_bg1': _L1_ffn_in['bg1'], 'L1_ffn_Wg2': _L1_ffn_in['Wg2'], 'L1_ffn_bg2': _L1_ffn_in['bg2'], 'L1_ffn_Wo': _L1_ffn_in['Wo'], 'L1_ffn_bo': _L1_ffn_in['bo']}

def reference(x, ctx_768, L0_attn_Wz, L0_attn_bz, L0_attn_Wh, L0_attn_bh, L0_xattn_Wq, L0_xattn_bq, L0_xattn_Wk, L0_xattn_bk, L0_xattn_Wv, L0_xattn_bv, L0_xattn_Wo, L0_xattn_bo, L0_ffn_w_router, L0_ffn_w_fc, L0_ffn_w_gate, L0_ffn_w_proj, L1_attn_Wq, L1_attn_Wk, L1_attn_Wv, L1_attn_Wo, L1_xattn_Wq, L1_xattn_Wk, L1_xattn_Wv, L1_xattn_Wo, L1_xattn_bo, L1_ffn_Wq, L1_ffn_bq, L1_ffn_Wk, L1_ffn_bk, L1_ffn_Wv, L1_ffn_bv, L1_ffn_Wg1, L1_ffn_bg1, L1_ffn_Wg2, L1_ffn_bg2, L1_ffn_Wo, L1_ffn_bo):
    import jax
    import jax.numpy as jnp

    def _L0_attn_ref(x, Wz, bz, Wh, bh):
        import jax, jax.numpy as jnp
        import numpy as np
        from jax import lax
        L, B, S, D, H = (2, 8, 256, 128, 128)
        LOG_H0 = float(np.log(0.5))

        def _log_g(x):
            return jnp.where(x >= 0, jnp.log(jnp.where(x >= 0, x + 0.5, 1.0)), -jax.nn.softplus(-x))

        def _mingru_layer(x, Wz, bz, Wh, bh):
            k = jnp.einsum('bsd,hd->bsh', x, Wz) + bz
            log_z = -jax.nn.softplus(-k)
            log_coeffs = -jax.nn.softplus(k)
            pre_h = jnp.einsum('bsd,hd->bsh', x, Wh) + bh
            log_values = log_z + _log_g(pre_h)
            Bq = x.shape[0]
            log_coeffs = jnp.pad(log_coeffs, ((0, 0), (1, 0), (0, 0)))
            log_values = jnp.concatenate([jnp.full((Bq, 1, log_values.shape[-1]), LOG_H0, dtype=log_values.dtype), log_values], axis=1)
            a_star = jnp.cumsum(log_coeffs, axis=1)
            log_h = a_star + lax.cumlogsumexp(log_values - a_star, axis=1)
            return jnp.exp(log_h)[:, 1:]
        h = x
        for l in range(Wz.shape[0]):
            h = _mingru_layer(h, Wz[l], bz[l], Wh[l], bh[l])
        return h

    def _L0_xattn_ref(query, key_value, Wq, bq, Wk, bk, Wv, bv, Wo, bo):
        import jax, jax.numpy as jnp
        import numpy as np
        NUM_HEADS = 16
        CLAMP = 10000.0
        B, Nq, Cq = query.shape
        Nkv = key_value.shape[1]
        H = NUM_HEADS
        D = Cq // H
        scale = D ** (-0.5)
        q = (query @ Wq + bq).reshape(B, Nq, H, D).transpose(0, 2, 1, 3)
        k = (key_value @ Wk + bk).reshape(B, Nkv, H, D).transpose(0, 2, 1, 3)
        v = (key_value @ Wv + bv).reshape(B, Nkv, H, D).transpose(0, 2, 1, 3)
        attn = jnp.einsum('bhqd,bhkd->bhqk', q, k) * scale
        attn = jnp.clip(attn, -CLAMP, CLAMP)
        attn = jax.nn.softmax(attn, axis=-1)
        attn = jnp.where(jnp.any(jnp.isnan(attn)), jnp.asarray(1.0 / Nkv, attn.dtype), attn)
        x = jnp.einsum('bhqk,bhkd->bqhd', attn, v).reshape(B, Nq, Cq)
        return x @ Wo + bo

    def _L0_ffn_ref(x, w_router, w_fc, w_gate, w_proj):
        import jax, jax.numpy as jnp
        import numpy as np
        E = 16
        K = 2
        LOAD = 1.0

        def _dispatch(xb, pb, cap):
            T, C = xb.shape
            top_k_probs, ei = jax.lax.top_k(pb, K)
            flat = ei.swapaxes(0, 1).ravel()
            one_hot = jax.nn.one_hot(flat, E, dtype=jnp.int32)
            pos = jnp.cumsum(one_hot, axis=0) * one_hot
            pos = pos.reshape(K, T, E).swapaxes(0, 1)
            pos = jnp.max(pos, axis=-1) - 1
            ei2 = flat.reshape(K, T).swapaxes(0, 1)
            xr = jnp.repeat(xb, K, axis=0)
            buf = jnp.zeros((E, cap, C), xb.dtype)
            buf = buf.at[ei2.ravel(), pos.ravel()].set(xr, mode='drop')
            return (top_k_probs, pos, ei2, buf)

        def _collect(eo_b, ei_b, pos_b, tk_b):
            out = eo_b[ei_b, pos_b]
            return jnp.sum(tk_b[..., None] * out, axis=1)
        B, T, C = x.shape
        cap = int(LOAD * K * max(1, T / E))
        g = jnp.einsum('btc,ce->bte', x, w_router)
        gate_probs = jax.nn.softmax(g, axis=-1)
        top_k_probs, positions, indices, expert_inputs = jax.vmap(lambda xb, pb: _dispatch(xb, pb, cap))(x, gate_probs)
        expert_inputs = jnp.swapaxes(expert_inputs, 0, 1).reshape(E, B * cap, C)
        gg = jnp.einsum('enc,ech->enh', expert_inputs, w_gate)
        h = jnp.einsum('enc,ech->enh', expert_inputs, w_fc)
        h = jax.nn.silu(gg) * h
        o = jnp.einsum('enh,ehc->enc', h, w_proj)
        expert_outputs = jnp.swapaxes(o.reshape(E, B, cap, C), 0, 1)
        y = jax.vmap(_collect)(expert_outputs, indices, positions, top_k_probs)
        return y

    def _L1_attn_ref(x, Wq, Wk, Wv, Wo):
        import jax, jax.numpy as jnp
        import numpy as np
        D_MODEL = 128
        N_HEADS = 16
        D_HEAD = D_MODEL // N_HEADS
        BLOCK = 128
        B, T = (2, 256)

        def _flash_attention(Q, K, V, block_size, scale):
            Bb, H, Tt, d = Q.shape
            n_blocks = Tt // block_size
            Kb = K.reshape(Bb, H, n_blocks, block_size, d).transpose(2, 0, 1, 3, 4)
            Vb = V.reshape(Bb, H, n_blocks, block_size, d).transpose(2, 0, 1, 3, 4)
            starts = jnp.arange(n_blocks) * block_size
            q_pos = jnp.arange(Tt)

            def step(carry, xs):
                m, l, acc = carry
                kb, vb, st = xs
                scores = scale * jnp.einsum('bhtd,bhsd->bhts', Q, kb)
                kv_pos = st + jnp.arange(block_size)
                future = kv_pos[None, :] > q_pos[:, None]
                scores = jnp.where(future[None, None], -jnp.inf, scores)
                m_new = jnp.maximum(m, jnp.max(scores, axis=-1, keepdims=True))
                p = jnp.exp(scores - m_new)
                corr = jnp.exp(m - m_new)
                l = corr * l + jnp.sum(p, axis=-1, keepdims=True)
                acc = corr * acc + jnp.einsum('bhts,bhsd->bhtd', p, vb)
                return ((m_new, l, acc), None)
            m0 = jnp.full((Bb, H, Tt, 1), -jnp.inf, dtype=jnp.float32)
            l0 = jnp.zeros((Bb, H, Tt, 1), dtype=jnp.float32)
            a0 = jnp.zeros((Bb, H, Tt, d), dtype=jnp.float32)
            (m, l, acc), _ = jax.lax.scan(step, (m0, l0, a0), (Kb, Vb, starts))
            return acc / jnp.maximum(l, 1e-12)
        Bx, Tx, _ = x.shape
        scale = 1.0 / np.sqrt(D_HEAD).astype(np.float32)

        def proj(W):
            y = jnp.einsum('btm,nm->btn', x, W)
            return y.reshape(Bx, Tx, N_HEADS, D_HEAD).transpose(0, 2, 1, 3)
        Q, K, V = (proj(Wq), proj(Wk), proj(Wv))
        O = _flash_attention(Q.astype(jnp.float32), K.astype(jnp.float32), V.astype(jnp.float32), BLOCK, scale)
        O = O.astype(x.dtype).transpose(0, 2, 1, 3).reshape(Bx, Tx, D_MODEL)
        return jnp.einsum('btm,nm->btn', O, Wo)

    def _L1_xattn_ref(x, context, Wq, Wk, Wv, Wo, bo):
        import jax, jax.numpy as jnp
        import numpy as np
        HEADS = 16
        DIM_HEAD = 64
        SCALE = DIM_HEAD ** (-0.5)
        QUERY_DIM = 128
        CONTEXT_DIM = 96
        INNER_DIM = HEADS * DIM_HEAD
        B, Nq, _ = x.shape
        Nk = context.shape[1]
        q = x @ Wq
        k = context @ Wk
        v = context @ Wv
        q = q.reshape(B, Nq, HEADS, DIM_HEAD).transpose(0, 2, 1, 3)
        k = k.reshape(B, Nk, HEADS, DIM_HEAD).transpose(0, 2, 1, 3)
        v = v.reshape(B, Nk, HEADS, DIM_HEAD).transpose(0, 2, 1, 3)
        sim = jnp.einsum('bhid,bhjd->bhij', q, k) * SCALE
        attn = jax.nn.softmax(sim, axis=-1)
        out = jnp.einsum('bhij,bhjd->bhid', attn, v)
        out = out.transpose(0, 2, 1, 3).reshape(B, Nq, INNER_DIM)
        return out @ Wo + bo

    def _L1_ffn_ref(hidden_states, Wq, bq, Wk, bk, Wv, bv, Wg1, bg1, Wg2, bg2, Wo, bo):
        import jax, jax.numpy as jnp
        import numpy as np
        N_HEADS = 16
        NUM_EXPERTS = 4
        TOP_K = 2
        D_MODEL = 128
        GATE_HID = 128
        B, T, C = hidden_states.shape
        H = N_HEADS
        D = C // H
        pooled = hidden_states.mean(axis=1)
        logits = jax.nn.relu(pooled @ Wg1 + bg1) @ Wg2 + bg2
        vals, idx = jax.lax.top_k(logits, TOP_K)
        sm = jax.nn.softmax(vals, axis=-1)
        weights = jnp.zeros_like(logits).at[jnp.arange(B)[:, None], idx].set(sm)

        def moe_proj(W, b):
            Wc = jnp.einsum('be,ecd->bcd', weights, W)
            bc = weights @ b
            return jnp.einsum('btc,bcd->btd', hidden_states, Wc) + bc[:, None, :]
        q = moe_proj(Wq, bq).reshape(B, T, H, D)
        k = moe_proj(Wk, bk).reshape(B, T, H, D)
        v = moe_proj(Wv, bv).reshape(B, T, H, D)
        scores = jnp.einsum('bthd,bshd->bhts', q, k) / np.sqrt(D).astype(np.float32)
        attn = jax.nn.softmax(scores, axis=-1)
        out = jnp.einsum('bhts,bshd->bthd', attn, v).reshape(B, T, C)
        return out @ Wo + bo
    x = _layernorm(x + _L0_attn_ref(x, L0_attn_Wz, L0_attn_bz, L0_attn_Wh, L0_attn_bh), axis=-1)
    x = _layernorm(x + _L0_xattn_ref(x, ctx_768, L0_xattn_Wq, L0_xattn_bq, L0_xattn_Wk, L0_xattn_bk, L0_xattn_Wv, L0_xattn_bv, L0_xattn_Wo, L0_xattn_bo), axis=-1)
    x = _layernorm(x + _L0_ffn_ref(x, L0_ffn_w_router, L0_ffn_w_fc, L0_ffn_w_gate, L0_ffn_w_proj), axis=-1)
    x = _layernorm(x + _L1_attn_ref(x, L1_attn_Wq, L1_attn_Wk, L1_attn_Wv, L1_attn_Wo), axis=-1)
    x = _layernorm(x + _L1_xattn_ref(x, ctx_768, L1_xattn_Wq, L1_xattn_Wk, L1_xattn_Wv, L1_xattn_Wo, L1_xattn_bo), axis=-1)
    x = _layernorm(x + _L1_ffn_ref(x, L1_ffn_Wq, L1_ffn_bq, L1_ffn_Wk, L1_ffn_bk, L1_ffn_Wv, L1_ffn_bv, L1_ffn_Wg1, L1_ffn_bg1, L1_ffn_Wg2, L1_ffn_bg2, L1_ffn_Wo, L1_ffn_bo), axis=-1)
    return x

_drawn_inputs = setup_inputs


def setup_inputs(seed=0):
    import zlib

    import numpy as np

    out = dict(_drawn_inputs(seed))
    spreads = {'L0_xattn_bq': (0.0, 0.306),
     'L0_xattn_bk': (0.0, 2.0),
     'L0_xattn_bv': (0.0, 0.1),
     'L0_xattn_bo': (0.0, 0.1),
     'L1_xattn_bo': (0.0, 0.1),
     'L1_ffn_bq': (0.0, 2.0),
     'L1_ffn_bk': (0.0, 2.0),
     'L1_ffn_bv': (0.0, 0.1),
     'L1_ffn_bg1': (0.0, 0.546),
     'L1_ffn_bg2': (0.0, 0.1),
     'L1_ffn_bo': (0.0, 0.1)}
    factors = {'L0_attn_Wz': 3.483,
     'L0_attn_bz': 8.0,
     'L0_ffn_w_router': 8.0,
     'L0_ffn_w_fc': 8.0,
     'L0_ffn_w_gate': 8.0,
     'L0_ffn_w_proj': 8.0}
    for name, (base, spread) in spreads.items():
        noise = np.random.default_rng([zlib.crc32(name.encode()), seed]).standard_normal(out[name].shape)
        drawn = base * np.exp(spread * noise) if base else spread * noise
        out[name] = jnp.asarray(drawn.astype(out[name].dtype))
    for name, factor in factors.items():
        out[name] = (out[name] * factor).astype(out[name].dtype)
    return out
```

```python
from contextlib import ExitStack

import concourse.bass as bass
from concourse import mybir

F32 = mybir.dt.float32
BF16 = mybir.dt.bfloat16
U32 = mybir.dt.uint32
ALU = mybir.AluOpType
ACT = mybir.ActivationFunctionType
X_AXIS = mybir.AxisListType.X

B = 32
T = 128
C = 128
NCTX = 77
CC = 96
H = 16
D8 = C // H
D64 = 64
QUAD = 4
NU = H // QUAD
GB = 4
NG = B // GB
E16 = 16
CAP = 16
SLOTS = E16 * CAP
HID = 64
EPS = 1e-5
CLAMP = 10000.0
NEG = -3.0e38

INS = ['x', 'ctx_768', 'L0_attn_Wz', 'L0_attn_bz', 'L0_attn_Wh', 'L0_attn_bh', 'L0_xattn_Wq', 'L0_xattn_bq',
       'L0_xattn_Wk', 'L0_xattn_bk', 'L0_xattn_Wv', 'L0_xattn_bv', 'L0_xattn_Wo', 'L0_xattn_bo',
       'L0_ffn_w_router', 'L0_ffn_w_fc', 'L0_ffn_w_gate', 'L0_ffn_w_proj', 'L1_attn_Wq', 'L1_attn_Wk',
       'L1_attn_Wv', 'L1_attn_Wo', 'L1_xattn_Wq', 'L1_xattn_Wk', 'L1_xattn_Wv', 'L1_xattn_Wo', 'L1_xattn_bo',
       'L1_ffn_Wq', 'L1_ffn_bq', 'L1_ffn_Wk', 'L1_ffn_bk', 'L1_ffn_Wv', 'L1_ffn_bv', 'L1_ffn_Wg1', 'L1_ffn_bg1',
       'L1_ffn_Wg2', 'L1_ffn_bg2', 'L1_ffn_Wo', 'L1_ffn_bo']


class Core:

    def __init__(self, nc, ctx, inp, out):
        self.nc, self.ctx, self.inp, self.out = nc, ctx, inp, out
        self.retired = []
        self.psum = ctx.enter_context(nc.psum_tensor("psum", [128, 8, 512], F32))
        self.x = self.sb("x", [T, B, C])
        self.xT = self.sb("xT", [C, B, T])
        self.branch = self.sb("branch", [128, B, 128])
        self.ctxT = self.sb("ctxT", [CC, B, NCTX])
        self.ident = self.sb("ident", [128, 128])
        self.ones = self.sb("ones", [128, 128])
        self.zeros = self.sb("zeros", [128, 512])
        self.pow_half = self.sb("pow_half", [128, GB])
        self.quad_mask = self.sb("quad_mask", [128, QUAD])
        self.wT = self.sb("wT", [128, 8, 128])

    def sb(self, name, shape, dt=F32):
        return self.ctx.enter_context(self.nc.sbuf_tensor(name, shape, dt))

    def bank(self, n):
        return self.psum[:, n, :]


class Stage:

    def __init__(self, core, name):
        self.core, self.name, self.ctx, self.sems = core, name, ExitStack(), []

    def __enter__(self):
        return self

    def __exit__(self, *_):
        self.ctx.close()
        for handle in self.core.retired:
            self.core.nc.release_semaphore(handle)
        self.core.retired = self.sems

    def sb(self, name, shape, dt=F32):
        return self.ctx.enter_context(self.core.nc.sbuf_tensor(f"{self.name}_{name}", shape, dt))

    def sem(self, name):
        self.sems.append(self.core.nc.alloc_semaphore(name=f"{self.name}_{name}"))
        return self.sems[-1]

    def clear_retired(self, engine):
        numbers = sorted(handle.num for handle in self.core.retired)
        while numbers:
            run = 1
            while run < len(numbers) and numbers[run] == numbers[0] + run:
                run += 1
            engine.sem_clear(range(numbers[0], numbers[0] + run))
            numbers = numbers[run:]


def stand_alone(engine, passed):
    engine.sem_inc(passed, 1)


def row(ap):
    return ap.rearrange("(a n) -> a n", a=1)


def col(ap):
    return ap.rearrange("(n a) -> n a", a=1)


def build_setup(core):
    nc, inp = core.nc, core.inp
    with Stage(core, "setup") as st:
        wn = st.sb("w_natural", [128, 8, 128])
        xin = st.sb("xin", [T, 2, GB, C])
        cin = st.sb("cin", [NCTX, 2, GB, CC])
        loaded_w, loaded_x, loaded_res = st.sem("loaded_w"), [st.sem("loaded_x0"), st.sem("loaded_x1")], st.sem("loaded_res")
        zeroed, ident_ready, consts = st.sem("zeroed"), st.sem("ident_ready"), st.sem("consts")
        tr_ready, xT_done, cT_done, w_ready, w_done = (st.sem(n) for n in ("tr_ready", "xT_done", "cT_done", "w_ready", "w_done"))
        x_g = inp['x'].rearrange("(n g) t c -> n t g c", g=GB)
        c_g = inp['ctx_768'].rearrange("(n g) t c -> n t g c", g=GB)

        passed = st.sem("passed")
        with nc.Block() as block:
            @block.sync
            def _(sp):
                for k, (name, l) in enumerate([('L0_attn_Wz', 0), ('L0_attn_Wz', 1), ('L0_attn_Wh', 0), ('L0_attn_Wh', 1)]):
                    sp.dma_start(wn[:, k, :], inp[name][l]).then_inc(loaded_w, 16)
                for k, name in enumerate(['L1_attn_Wq', 'L1_attn_Wk', 'L1_attn_Wv', 'L1_attn_Wo']):
                    sp.dma_start(wn[:, 4 + k, :], inp[name][:, :]).then_inc(loaded_w, 16)
                sp.dma_start(core.x[:, :, :], inp['x'].rearrange("b t c -> t b c")).then_inc(loaded_res, 16)
                for par in range(2):
                    sp.dma_start(xin[:, par, :, :], x_g[par]).then_inc(loaded_x[par], 16)
                    sp.dma_start(cin[:, par, :, :], c_g[par]).then_inc(loaded_x[par], 16)
                with sp.Fori(1, NG // 2) as i:
                    for par in range(2):
                        sp.wait_ge(tr_ready, 4 * i + 2 * par - 2)
                        sp.dma_start(xin[:, par, :, :], x_g[2 * i + par]).then_inc(loaded_x[par], 16)
                        sp.dma_start(cin[:, par, :, :], c_g[2 * i + par]).then_inc(loaded_x[par], 16)
                sp.wait_ge(loaded_res, 16)

            @block.gpsimd
            def _(pool):
                st.clear_retired(pool)
                nc.gpsimd.memset(core.ones[:, :], 1.0).then_inc(consts, 1)
                nc.gpsimd.memset(core.zeros[:, :], 0.0).then_inc(consts, 1)
                nc.gpsimd.memset(core.pow_half[:, :], -0.5).then_inc(consts, 1)
                pool.wait_ge(consts, 3)
                nc.gpsimd.affine_select(out=core.ident[:, :], in_=core.zeros[:, 0:128], compare_op=ALU.not_equal, fill=1.0,
                                        base=0, pattern=[[-1, 128]], channel_multiplier=1).then_inc(ident_ready, 1)
                for g in range(4):
                    sl = slice(32 * g, 32 * g + 32)
                    nc.gpsimd.affine_select(out=core.quad_mask[sl, :], in_=core.ones[sl, 0:QUAD], compare_op=ALU.is_ge, fill=0.0,
                                            base=0, pattern=[[-D8, QUAD]], channel_multiplier=1).then_inc(zeroed, 1)
                    pool.wait_ge(zeroed, 2 * g + 1)
                    nc.gpsimd.affine_select(out=core.quad_mask[sl, :], in_=core.quad_mask[sl, :], compare_op=ALU.is_ge, fill=0.0,
                                            base=D8 - 1, pattern=[[D8, QUAD]], channel_multiplier=-1).then_inc(zeroed, 1)

            @block.tensor
            def _(pe):
                pe.wait_ge(ident_ready, 1)
                pe.wait_ge(loaded_w, 16 * 8)
                for k in range(8):
                    nc.tensor.transpose(core.psum[:, 4 + k // 4, (k % 4) * 128:(k % 4 + 1) * 128], wn[:, k, :], core.ident[:, :]).then_inc(w_ready, 1)
                with pe.Fori(0, NG // 2) as i:
                    for par in range(2):
                        pe.wait_ge(loaded_x[par], 32 * i + 32)
                        pe.wait_ge(xT_done, 2 * i + par + 1)
                        for j in range(GB):
                            last = nc.tensor.transpose(core.psum[:, 0, j * T:(j + 1) * T], xin[:, par, j, :], core.ident[:, :])
                        last.then_inc(tr_ready, 1)
                        pe.wait_ge(cT_done, 2 * i + par + 1)
                        for j in range(GB):
                            last = nc.tensor.transpose(core.psum[0:CC, 1, j * NCTX:(j + 1) * NCTX], cin[:, par, j, :],
                                                       core.ident[0:NCTX, 0:NCTX])
                        last.then_inc(tr_ready, 1)

            @block.scalar
            def _(act):
                act.sem_inc(xT_done, 1)
                with act.Fori(0, NG) as n:
                    act.wait_ge(tr_ready, 2 * n + 1)
                    nc.scalar.activation(core.xT[:, bass.ts(n, GB), :], core.psum[:, 0, :].rearrange("p (g t) -> p g t", g=GB),
                                         ACT.Identity).then_inc(xT_done, 1)

            @block.vector
            def _(dve):
                dve.sem_inc(cT_done, 1)
                dve.wait_ge(w_ready, 8)
                nc.vector.tensor_copy(core.wT[:, :, :], core.psum[:, 4:6, :].rearrange("p a (k n) -> p (a k) n", k=4)).then_inc(w_done, 1)
                with dve.Fori(0, NG) as n:
                    dve.wait_ge(tr_ready, 2 * n + 2)
                    nc.vector.tensor_copy(core.ctxT[:, bass.ts(n, GB), :],
                                          core.psum[0:CC, 1, 0:GB * NCTX].rearrange("p (g t) -> p g t", g=GB)).then_inc(cT_done, 1)


def build_gru(core):
    nc, inp = core.nc, core.inp
    with Stage(core, "gru") as st:
        h1 = st.sb("h1", [C, B, T])
        bias = st.sb("bias", [128, 4, 2])
        keep = st.sb("keep", [128, 2, 512])
        z = st.sb("z", [128, 2, 512])
        sg = st.sb("sg", [128, 2, 512])
        g = st.sb("g", [128, 2, 512])
        v = st.sb("v", [128, 2, 512])
        loaded, bias_ready = st.sem("loaded"), st.sem("bias_ready")
        passed = st.sem("passed")
        with nc.Block() as block:
            @block.sync
            def _(sp):
                st.clear_retired(sp)
                for l in range(2):
                    sp.dma_start(bias[:, 0, l:l + 1], col(inp['L0_attn_bz'][l])).then_inc(loaded, 16)
                    sp.dma_start(bias[:, 1, l:l + 1], col(inp['L0_attn_bh'][l])).then_inc(loaded, 16)

            for l, (src, dst) in enumerate([(core.xT, h1), (h1, core.branch)]):
                pre_ready, gates_ready, cand, value, scanned = (
                    st.sem(f"{n}{l}") for n in ("pre_ready", "gates_ready", "cand", "value", "scanned"))
                lay = [pre_ready, gates_ready, cand, value, scanned]
                gru_layer(core, block, l, src, dst, bias, keep, z, sg, g, v, loaded, bias_ready, *lay,
                          prev_scanned=prev if l else None)
                prev = scanned


def gru_layer(core, block, l, src, dst, bias, keep, z, sg, g, v, loaded, bias_ready, pre_ready, gates_ready, cand, value,
              scanned, prev_scanned):
    nc = core.nc
    groups = [(lambda i, par=par: 2 * i + par) for par in range(2)]

    @block.tensor
    def _(pe):
        if prev_scanned is not None:
            pe.wait_ge(prev_scanned, GB * (NG + 1) + 1)
        with pe.Fori(0, NG // 2) as i:
            for par in range(2):
                n = groups[par](i)
                pe.wait_ge(cand, n + 1)
                rhs = src[:, bass.ds(n * GB, GB), :]
                nc.tensor.matmul(core.bank(2 * par), core.wT[:, l, :], rhs, start=True, stop=True).then_inc(pre_ready, 1)
                nc.tensor.matmul(core.bank(2 * par + 1), core.wT[:, 2 + l, :], rhs, start=True, stop=True).then_inc(pre_ready, 1)

    @block.scalar
    def _(act):
        act.wait_ge(bias_ready, 2)
        with act.Fori(0, NG // 2) as i:
            for par in range(2):
                n = groups[par](i)
                act.wait_ge(pre_ready, 2 * n + 1)
                act.wait_ge(value, n + 1)
                nc.scalar.activation(z[:, par, :], core.bank(2 * par), ACT.Sigmoid, bias=bias[:, 0, l:l + 1]).then_inc(gates_ready, 1)
                act.wait_ge(scanned, GB * n + 1)
                nc.scalar.activation(keep[:, par, :], core.bank(2 * par), ACT.Sigmoid, bias=bias[:, 2, l:l + 1],
                                     scale=-1.0).then_inc(gates_ready, 1)
                act.wait_ge(pre_ready, 2 * n + 2)
                nc.scalar.activation(sg[:, par, :], core.bank(2 * par + 1), ACT.Sigmoid, bias=bias[:, 1, l:l + 1]).then_inc(gates_ready, 1)

    @block.vector
    def _(dve):
        if l == 0:
            dve.wait_ge(loaded, 64)
            nc.vector.tensor_scalar(bias[:, 2, :], bias[:, 0, :], -1.0, None, ALU.mult).then_inc(bias_ready, 1)
            nc.vector.tensor_scalar(bias[:, 3, :], bias[:, 1, :], 0.5, None, ALU.add).then_inc(bias_ready, 1)
            dve.wait_ge(bias_ready, 2)
        dve.sem_inc(cand, 2)
        dve.sem_inc(value, 2)
        dve.sem_inc(scanned, GB + 1)
        with dve.Fori(0, NG // 2) as i:
            for par in range(2):
                n = groups[par](i)
                dve.wait_ge(gates_ready, 3 * n + 3)
                nc.vector.scalar_tensor_tensor(out=g[:, par, :], in0=core.bank(2 * par + 1), scalar=bias[:, 3, l:l + 1],
                                               in1=sg[:, par, :], op0=ALU.add, op1=ALU.max).then_inc(cand, 1)
                dve.wait_ge(cand, n + 3)
                nc.vector.tensor_tensor(v[:, par, :], g[:, par, :], z[:, par, :], ALU.mult).then_inc(value, 1)
                dve.wait_ge(value, n + 3)
                for j in range(GB):
                    nc.vector.tensor_tensor_scan(dst[:, n * GB + j, :], keep[:, par, j * T:(j + 1) * T],
                                                 v[:, par, j * T:(j + 1) * T], 0.5, ALU.mult, ALU.add).then_inc(scanned, 1)


def build_close(core, name, wo=None, v_bias=None, v_bias_by_batch=None, out_bias=None, turned=False, nan_guard=None, last=False):
    nc, inp = core.nc, core.inp
    with_pe = turned or wo is not None
    with Stage(core, name) as st:
        cur = st.sb("cur", [128, 2, GB, 128])
        oT = st.sb("oT", [128, 2, GB, 128])
        z = st.sb("z", [128, 2, GB, C])
        xn = st.sb("xn", [128, 2, GB, C])
        stats = st.sb("stats", [128, GB, 6])
        mv = st.sb("mv", [128, 2, GB, 2])
        rstd = st.sb("rstd", [128, 2, GB])
        ve = st.sb("ve", [128, 2, GB])
        w_o = st.sb("w_o", [128, 128])
        b_v = st.sb("b_v", [128, 1])
        b_o = st.sb("b_o", [128, 128])
        loaded = st.sem("loaded")
        cur_ready, turned_ready, oT_done, y_ready, summed = (st.sem(n) for n in ("cur_ready", "turned_ready", "oT_done", "y_ready", "summed"))
        stat_step, ve_done, rstd_done, normed, xT_ready, xT_done = (
            st.sem(n) for n in ("stat_step", "ve_done", "rstd_done", "normed", "xT_ready", "xT_done"))
        stored = [st.sem("stored0"), st.sem("stored1")]
        x_copied, bo_added = st.sem("x_copied"), st.sem("bo_added")
        guard_step, guard_mm, mean_copied, oT_final = (st.sem(n) for n in ("guard_step", "guard_mm", "mean_copied", "oT_final"))
        if nan_guard:
            recip_all, w_v = nan_guard
            wv = st.sb("wv", [CC, C])
            csum = st.sb("csum", [CC, B])
            vmean = st.sb("vmean", [C, B])
            mean4 = st.sb("mean4", [C, 2, GB])
            rsum = st.sb("rsum", [T, 2])
            mask = st.sb("mask", [T, 1], U32)
            isnan = st.sb("isnan", [T, 1])
        n_load = (wo is not None) + (v_bias is not None) + (out_bias is not None) + (nan_guard is not None)
        Y = 4
        y_bank = (lambda par: 0 + par) if turned else (lambda par: 2 + par)

        passed = st.sem("passed")
        with nc.Block() as block:
            @block.sync
            def _(sp):
                if wo is not None:
                    sp.dma_start(w_o[:, :], wo).then_inc(loaded, 16)
                if v_bias is not None:
                    sp.dma_start(b_v[:, :], col(v_bias)).then_inc(loaded, 16)
                if nan_guard:
                    sp.dma_start(wv[:, :], w_v).then_inc(loaded, 16)
                if out_bias is not None:
                    sp.dma_start(b_o[:, :], row(out_bias).broadcast_to([128, 128])).then_inc(loaded, 16)
                if last:
                    with sp.Fori(0, NG // 2) as i:
                        for par in range(2):
                            n = 2 * i + par
                            sp.wait_ge(normed, GB * (n + 2))
                            sp.dma_start(core.out.rearrange("(n g) t c -> n t g c", g=GB)[n], xn[:, par, :, :]).then_inc(stored[par], 16)
                    for par in range(2):
                        sp.wait_ge(stored[par], 16 * (NG // 2))

            @block.gpsimd
            def _(pool):
                st.clear_retired(pool)
                if out_bias is not None:
                    pool.wait_ge(loaded, 16 * n_load)
                with pool.Fori(0, NG // 2) as i:
                    for par in range(2):
                        n = 2 * i + par
                        xs = core.x[:, bass.ds(n * GB, GB), :]
                        if with_pe:
                            pool.wait_ge(turned_ready, n + 1)
                            nc.gpsimd.tensor_copy(cur[:, par, :, :], core.branch[:, bass.ds(n * GB, GB), :]).then_inc(cur_ready, 1)
                        if out_bias is not None:
                            nc.gpsimd.tensor_tensor(xs, xs, b_o[:, :].rearrange("p (a c) -> p a c", a=1).broadcast_to([128, GB, C]),
                                                    ALU.add).then_inc(bo_added, 1)
                        pool.wait_ge(ve_done, n + 1)
                        nc.gpsimd.tensor_tensor(rstd[:, par, :], ve[:, par, :], core.pow_half[:, :], ALU.pow).then_inc(rstd_done, 1)

            @block.tensor
            def _(pe):
                if wo is not None:
                    pe.wait_ge(loaded, 16 * n_load)
                pe.sem_inc(turned_ready, 2)

                def turn_x(n, par):
                    pe.wait_ge(normed, GB * (n + 2))
                    pe.wait_ge(xT_done, n)
                    for j in range(GB):
                        mm = nc.tensor.transpose(core.psum[:, 4 + par, j * T:(j + 1) * T], xn[:, par, j, :], core.ident[:, :])
                    mm.then_inc(xT_ready, 1)

                def front(n, par):
                    if not with_pe:
                        return
                    pe.wait_ge(cur_ready, n + 1)
                    if turned:
                        pe.wait_ge(summed, n)
                    else:
                        pe.wait_ge(oT_done, n)
                    for j in range(GB):
                        mm = nc.tensor.transpose(core.psum[:, par, j * T:(j + 1) * T], cur[:, par, j, :], core.ident[:, :])
                    mm.then_inc(turned_ready, 1)
                    if wo is not None:
                        if nan_guard:
                            pe.wait_ge(oT_final, n + 1)
                        else:
                            pe.wait_ge(oT_done, n + 2)
                        pe.wait_ge(summed, n)
                        for j in range(GB):
                            mm = nc.tensor.matmul(core.psum[:, 2 + par, j * C:(j + 1) * C], oT[:, par, j, :], w_o[:, :], start=True, stop=True)
                        mm.then_inc(y_ready, 1)

                def pair(i, first):
                    for par in range(2):
                        n = 2 * i + par
                        front(n, par)
                        if not last and not (first and par == 0):
                            turn_x(n - 1, 1 - par)

                if nan_guard:
                    pe.wait_ge(guard_step, 1)
                    nc.tensor.matmul(core.psum[:, 6, 0:1], core.ones[:, :], rsum[:, 0:1], start=True, stop=True).then_inc(guard_mm, 1)
                    pe.wait_ge(guard_step, 2)
                    nc.tensor.matmul(core.psum[:, 7, 0:B], wv[:, :], csum[:, :], start=True, stop=True).then_inc(guard_mm, 1)
                pair(0, True)
                with pe.Fori(1, NG // 2) as i:
                    pair(i, False)
                if not last:
                    turn_x(NG - 1, (NG - 1) % 2)

            @block.scalar
            def _(act):
                act.sem_inc(oT_done, 1)
                act.sem_inc(xT_done, 1)

                def copy_oT(n, par):
                    act.wait_ge(turned_ready, n + 3)
                    src = core.psum[:, par, :].rearrange("p (g t) -> p g t", g=GB)
                    if v_bias is not None:
                        ins = nc.scalar.activation(oT[:, par, :, :], src, ACT.Identity, bias=b_v[:, :])
                        ins.then_inc(oT_done, 1)
                    elif v_bias_by_batch is not None:
                        for j in range(GB):
                            ins = nc.scalar.activation(oT[:, par, j, :], src[:, j, :], ACT.Identity,
                                                       bias=v_bias_by_batch[:, bass.ds(n * GB + j, 1)])
                        ins.then_inc(oT_done, 1)
                    else:
                        nc.scalar.activation(oT[:, par, :, :], src, ACT.Identity).then_inc(oT_done, 1)

                def copy_xT(n, par):
                    act.wait_ge(xT_ready, n + 1)
                    nc.scalar.activation(core.xT[:, bass.ds(n * GB, GB), :],
                                         core.psum[:, 4 + par, :].rearrange("p (g t) -> p g t", g=GB), ACT.Identity).then_inc(xT_done, 1)

                if v_bias is not None:
                    act.wait_ge(loaded, 16 * n_load)

                def pair(i, first):
                    for par in range(2):
                        n = 2 * i + par
                        if wo is not None:
                            copy_oT(n, par)
                        if not last and not (first and par == 0):
                            copy_xT(n - 1, 1 - par)

                pair(0, True)
                with act.Fori(1, NG // 2) as i:
                    pair(i, False)
                if not last:
                    copy_xT(NG - 1, (NG - 1) % 2)

            @block.vector
            def _(dve):
                dve.sem_inc(summed, 1)
                dve.sem_inc(normed, GB)
                if nan_guard:
                    nc.vector.tensor_reduce(rsum[:, 0:1], recip_all[:, :, :].rearrange("p b h -> p (b h)"), X_AXIS, ALU.add).then_inc(guard_step, 1)
                    nc.vector.tensor_reduce(csum[:, :], core.ctxT[:, :, :], X_AXIS, ALU.add).then_inc(guard_step, 1)
                    dve.wait_ge(guard_mm, 1)
                    nc.vector.tensor_copy(rsum[:, 1:2], core.psum[:, 6, 0:1]).then_inc(guard_step, 1)
                    dve.wait_ge(guard_step, 3)
                    nc.vector.tensor_tensor(isnan[:, :], rsum[:, 1:2], rsum[:, 1:2], ALU.not_equal).then_inc(guard_step, 1)
                    dve.wait_ge(guard_step, 4)
                    nc.vector.tensor_copy(mask[:, :], isnan[:, :]).then_inc(guard_step, 1)
                    dve.wait_ge(guard_mm, 2)
                    dve.wait_ge(loaded, 16 * n_load)
                    nc.vector.tensor_scalar(vmean[:, :], core.psum[:, 7, 0:B], 1.0 / NCTX, b_v[:, :], ALU.mult, ALU.add).then_inc(guard_step, 1)
                    dve.wait_ge(guard_step, 6)

                def blend(n, par):
                    nc.vector.tensor_copy(mean4[:, par, :], vmean[:, bass.ds(n * GB, GB)]).then_inc(mean_copied, 1)
                    dve.wait_ge(mean_copied, n + 1)
                    dve.wait_ge(oT_done, n + 2)
                    stand_alone(dve, passed)
                    nc.vector.copy_predicated(oT[:, par, :, :], mask[:, :].rearrange("p (a b) -> p a b", a=1).broadcast_to([C, GB, T]),
                                              mean4[:, par, :].rearrange("p (g a) -> p g a", a=1).broadcast_to([C, GB, T])).then_inc(oT_final, 1)

                def add_up(n, par):
                    xs = core.x[:, bass.ds(n * GB, GB), :]
                    if out_bias is not None:
                        dve.wait_ge(bo_added, n + 1)
                    if turned:
                        dve.wait_ge(turned_ready, n + 3)
                        y = core.psum[:, par, :].rearrange("p (g c) -> p g c", g=GB)
                    elif wo is not None:
                        if nan_guard:
                            blend(n, par)
                        dve.wait_ge(y_ready, n + 1)
                        y = core.psum[:, 2 + par, :].rearrange("p (g c) -> p g c", g=GB)
                    else:
                        y = core.branch[:, bass.ds(n * GB, GB), :]
                    nc.vector.tensor_tensor(z[:, par, :, :], y, xs, ALU.add).then_inc(summed, 1)
                    dve.wait_ge(summed, n + 2)
                    for j in range(GB):
                        nc.vector.bn_stats(stats[:, j, :], z[:, par, j, :]).then_inc(stat_step, 1)
                    dve.wait_ge(stat_step, 8 * n + 4)
                    stand_alone(dve, passed)
                    for j in range(GB):
                        nc.vector.bn_aggr(mv[:, par, j, :], stats[:, j, :]).then_inc(stat_step, 1)
                    dve.wait_ge(stat_step, 8 * n + 8)
                    nc.vector.tensor_scalar(ve[:, par, :], mv[:, par, :, 1], EPS, None, ALU.add).then_inc(ve_done, 1)

                def norm(n, par, earlier):
                    dve.wait_ge(rstd_done, n + 1)
                    if last and not (isinstance(earlier, int) and earlier == 0):
                        dve.wait_ge(stored[par], 16 * earlier)
                    if not last and not (isinstance(n, int) and n < 2):
                        dve.wait_ge(xT_ready, n - 1)
                    for j in range(GB):
                        nc.vector.tensor_scalar(xn[:, par, j, :], z[:, par, j, :], mv[:, par, j, 0:1], rstd[:, par, j:j + 1],
                                                ALU.subtract, ALU.mult).then_inc(normed, 1)
                    dve.wait_ge(normed, GB * (n + 2))
                    if not last:
                        stand_alone(dve, passed)
                        nc.vector.tensor_copy(core.x[:, bass.ds(n * GB, GB), :], xn[:, par, :, :]).then_inc(x_copied, 1)

                def pair(i, first):
                    for par in range(2):
                        n = 2 * i + par
                        add_up(n, par)
                        if not (first and par == 0):
                            norm(n - 1, 1 - par, i - (1 - par))

                pair(0, True)
                with dve.Fori(1, NG // 2) as i:
                    pair(i, False)
                norm(NG - 1, 1, NG // 2 - 1)


def build_attention8(core, name, nk, w_q, w_k, w_v, cross=False, b_q=None, b_k=None, transposed=None, causal=False,
                     clip=False, guard=False, mixed=None, recip_all=None):
    nc, inp = core.nc, core.inp
    scale = float(D8) ** -0.5
    ck = CC if cross else C
    S_BANK, T_BANK, O_BANK, Q_BANK, K_BANK, V_BANK = 0, 2, 4, 5, 6, 7
    with Stage(core, name) as st:
        xc = st.sb("xc", [C, 2, T])
        cc = st.sb("cc", [CC, 2, NCTX])
        qT = st.sb("qT", [C, 2, T])
        keys_q = st.sb("keys_q", [C, 2, QUAD, nk])
        va = st.sb("va", [nk, 2, H, D8 + 1])
        sc = st.sb("sc", [T, 2, QUAD, nk])
        clipped = st.sb("clipped", [T, 2, QUAD, nk])
        pT = st.sb("pT", [nk, 2, QUAD, T])
        negmax = st.sb("negmax", [T, 2, QUAD])
        den = st.sb("den", [T, 2, H])
        rden = st.sb("rden", [T, 2, H])
        wq, wk, wv = (st.sb(n, [128, C]) for n in ("wq", "wk", "wv"))
        bq, bk = st.sb("bq", [C, 1]), st.sb("bk", [C, 1])
        wmix = st.sb("wmix", [C, 2, 3, C]) if mixed else None
        future = st.sb("future", [T, T], BF16) if causal else None
        identb = st.sb("identb", [T, T], BF16) if causal else None
        loaded, consts, src_ready, projected = (st.sem(n) for n in ("loaded", "consts", "src_ready", "projected"))
        q_done, k_done, v_done, mix_step = (st.sem(n) for n in ("q_done", "k_done", "v_done", "mix_step"))
        scored, clip_step, max_step, shifted, p_ready, turned, pT_ready, o_ready, norm_step, o_done = (st.sem(n) for n in (
            "scored", "clip_step", "max_step", "shifted", "p_ready", "turned", "pT_ready", "o_ready", "norm_step", "o_done"))
        biased = b_q is not None
        n_load = 0
        weights = []
        if mixed is None and transposed is None:
            weights = [(wq[:, :], w_q), (wk[0:ck, :], w_k), (wv[0:ck, :], w_v)]
        if biased:
            weights += [(bq[:, :], col(b_q)), (bk[:, :], col(b_k))]
        n_load = len(weights)
        NORM = 1 + guard + (recip_all is not None)

        passed = st.sem("passed")
        with nc.Block() as block:
            @block.sync
            def _(sp):
                for dst, src in weights:
                    sp.dma_start(dst, src).then_inc(loaded, 16)
                if n_load:
                    sp.wait_ge(loaded, 16 * n_load)

            @block.gpsimd
            def _(pool):
                st.clear_retired(pool)
                nc.gpsimd.memset(va[:, :, :, D8:D8 + 1], 1.0).then_inc(consts, 1)
                if causal:
                    nc.gpsimd.tensor_copy(identb[:, :], core.ident[:, :]).then_inc(consts, 1)
                    nc.gpsimd.affine_select(out=future[:, :], in_=core.zeros[:, 0:T], compare_op=ALU.is_ge, fill=NEG, base=0,
                                            pattern=[[-1, T]], channel_multiplier=1).then_inc(consts, 1)
                with pool.Fori(0, B // 2) as i:
                    for par in range(2):
                        b = 2 * i + par
                        pool.wait_ge(projected, 3 * b + 1)
                        nc.gpsimd.tensor_copy(xc[:, par, :], core.xT[:, b, :]).then_inc(src_ready, 1)
                        if cross:
                            nc.gpsimd.tensor_copy(cc[:, par, :], core.ctxT[:, b, :]).then_inc(src_ready, 1)

            @block.tensor
            def _(pe):
                pe.sem_inc(projected, 4)
                if n_load:
                    pe.wait_ge(loaded, 16 * n_load)
                pe.wait_ge(consts, 3 if causal else 1)

                def project(b, par):
                    pe.wait_ge(src_ready, (2 if cross else 1) * (b + 1))
                    if mixed is not None:
                        pe.wait_ge(mix_step, 4 * b + 4)
                        ws = [wmix[:, par, k, :] for k in range(3)]
                    elif transposed is not None:
                        ws = [core.wT[:, k, :] for k in transposed]
                    else:
                        ws = [wq[:, :], wk[0:ck, :], wv[0:ck, :]]
                    kv = cc[:, par, :] if cross else xc[:, par, :]
                    pe.wait_ge(q_done, b)
                    nc.tensor.matmul(core.psum[:, Q_BANK, 0:T], ws[0], xc[:, par, :], start=True, stop=True).then_inc(projected, 1)
                    pe.wait_ge(k_done, b)
                    nc.tensor.matmul(core.psum[:, K_BANK, 0:nk], ws[1], kv, start=True, stop=True).then_inc(projected, 1)
                    pe.wait_ge(v_done, b)
                    nc.tensor.matmul(core.psum[0:nk, V_BANK, 0:C], kv, ws[2], start=True, stop=True).then_inc(projected, 1)

                def score(b, par, g):
                    u = NU * b + g
                    if g == 0:
                        pe.wait_ge(q_done, b + 1)
                        pe.wait_ge(k_done, b + 1)
                    pe.wait_ge(shifted, u)
                    rows = slice(32 * g, 32 * g + 32)
                    out = core.psum[:, S_BANK + g % 2, 0:QUAD * nk]
                    mm = nc.tensor.matmul(out, qT[rows, par, :], keys_q[rows, par, :, :], start=True, stop=not causal)
                    if causal:
                        for j in range(QUAD):
                            mm = nc.tensor.matmul(out[:, j * nk:(j + 1) * nk], identb[:, :], future[:, :], start=False, stop=(j == QUAD - 1))
                    mm.then_inc(scored, 1)

                def turn(b, g):
                    u = NU * b + g
                    pe.wait_ge(p_ready, u + 1)
                    pe.wait_ge(pT_ready, u)
                    for j in range(QUAD):
                        mm = nc.tensor.transpose(core.psum[0:nk, T_BANK + g % 2, j * T:(j + 1) * T], sc[:, g % 2, j, :], core.ident[:, :])
                    mm.then_inc(turned, 1)

                def weigh(b, par, g):
                    u = NU * b + g
                    if g == 0:
                        pe.wait_ge(v_done, b + 1)
                        pe.wait_ge(o_done, b)
                    pe.wait_ge(pT_ready, u + 2)
                    for j in range(QUAD):
                        h = QUAD * g + j
                        mm = nc.tensor.matmul(core.psum[:, O_BANK, h * (D8 + 1):(h + 1) * (D8 + 1)], pT[:, g % 2, j, :], va[:, par, h, :],
                                              start=True, stop=True)
                    if g == NU - 1:
                        mm.then_inc(o_ready, 1)

                def before(b, par, g, back):
                    k = g - back
                    return (b, par, k) if k >= 0 else (b - 1, 1 - par, k + NU)

                def pair(i, first, last):
                    for par in range(2):
                        b = 2 * i + par
                        for g in range(NU):
                            score(b, par, g)
                            if not (first and par == 0 and g < 1):
                                bb, _, gg = before(b, par, g, 1)
                                turn(bb, gg)
                            if not (first and par == 0 and g < 2):
                                weigh(*before(b, par, g, 2))
                            if g == 1 and not (last and par == 1):
                                project(b + 1, 1 - par)

                project(0, 0)
                pair(0, True, False)
                with pe.Fori(1, B // 2 - 1) as i:
                    pair(i, False, False)
                pair(B // 2 - 1, False, True)
                turn(B - 1, NU - 1)
                weigh(B - 1, 1, NU - 2)
                weigh(B - 1, 1, NU - 1)

            @block.scalar
            def _(act):
                act.sem_inc(pT_ready, 1)
                if n_load:
                    act.wait_ge(loaded, 16 * n_load)
                act.wait_ge(consts, 3 if causal else 1)

                def copy_projected(b, par):
                    act.wait_ge(projected, 3 * b + 5)
                    q_bias = bq[:, :] if biased else (mixed[1][:, 0, bass.ds(b, 1)] if mixed else 0.0)
                    nc.scalar.activation(qT[:, par, :], core.psum[:, Q_BANK, 0:T], ACT.Identity, bias=q_bias).then_inc(q_done, 1)
                    act.wait_ge(projected, 3 * b + 7)
                    nc.scalar.activation(va[:, par, :, 0:D8], core.psum[0:nk, V_BANK, 0:C].rearrange("p (h d) -> p h d", h=H),
                                         ACT.Identity).then_inc(v_done, 1)

                def exponential(u, g):
                    act.wait_ge(shifted, u + 2)
                    nc.scalar.activation(sc[:, g % 2, :, :], sc[:, g % 2, :, :], ACT.Exp, scale=scale).then_inc(p_ready, 1)

                def copy_pT(u, g):
                    act.wait_ge(turned, u + 1)
                    nc.scalar.activation(pT[:, g % 2, :, :], core.psum[0:nk, T_BANK + g % 2, :].rearrange("p (j t) -> p j t", j=QUAD),
                                         ACT.Identity).then_inc(pT_ready, 1)

                def pair(i, first, last):
                    for par in range(2):
                        b = 2 * i + par
                        for g in range(NU):
                            exponential(NU * b + g, g)
                            if not (first and par == 0 and g == 0):
                                copy_pT(NU * b + g - 1, (g - 1) % 2)
                            if g == 2 and not (last and par == 1):
                                copy_projected(b + 1, 1 - par)

                copy_projected(0, 0)
                pair(0, True, False)
                with act.Fori(1, B // 2 - 1) as i:
                    pair(i, False, False)
                pair(B // 2 - 1, False, True)
                copy_pT(NU * B - 1, (NU - 1) % 2)

            @block.vector
            def _(dve):
                dve.sem_inc(shifted, 1)
                if n_load:
                    dve.wait_ge(loaded, 16 * n_load)

                def mix(b, par):
                    gate, _, experts = mixed
                    dve.wait_ge(projected, 3 * b + 1)
                    out = wmix[:, par, :, :].rearrange("p k n -> p (k n)")
                    nc.vector.tensor_scalar(out, experts[:, 0, :], gate[:, bass.ds(4 * b, 1)], None, ALU.mult).then_inc(mix_step, 1)
                    for e in range(1, 4):
                        dve.wait_ge(mix_step, 4 * b + e)
                        nc.vector.scalar_tensor_tensor(out=out, in0=experts[:, e, :], scalar=gate[:, bass.ds(4 * b + e, 1)], in1=out,
                                                       op0=ALU.mult, op1=ALU.add).then_inc(mix_step, 1)

                def spread_keys(b, par):
                    dve.wait_ge(projected, 3 * b + 6)
                    k_in = core.psum[:, K_BANK, 0:nk].rearrange("p (a n) -> p a n", a=1).broadcast_to([C, QUAD, nk])
                    k_bias = bk[:, :] if biased else (mixed[1][:, 1, bass.ds(b, 1)] if mixed else 0.0)
                    mask = core.quad_mask[:, :].rearrange("p (q a) -> p q a", a=1).broadcast_to([C, QUAD, nk])
                    nc.vector.scalar_tensor_tensor(out=keys_q[:, par, :, :], in0=k_in, scalar=k_bias, in1=mask,
                                                   op0=ALU.add, op1=ALU.mult).then_inc(k_done, 1)

                def shift(u, g, no_turned_wait):
                    dve.wait_ge(scored, u + 1)
                    s = core.psum[:, S_BANK + g % 2, 0:QUAD * nk].rearrange("p (j n) -> p j n", j=QUAD)
                    if clip:
                        nc.vector.tensor_scalar(clipped[:, g % 2, :, :], s, CLAMP / scale, -CLAMP / scale, ALU.min, ALU.max).then_inc(clip_step, 1)
                        dve.wait_ge(clip_step, u + 1)
                        s = clipped[:, g % 2, :, :]
                    nc.vector.tensor_reduce(negmax[:, g % 2, :], s, X_AXIS, ALU.max, negate=True).then_inc(max_step, 1)
                    dve.wait_ge(max_step, u + 1)
                    if not no_turned_wait:
                        dve.wait_ge(turned, u - 1)
                    nm = negmax[:, g % 2, :].rearrange("p (q a) -> p q a", a=1).broadcast_to([T, QUAD, nk])
                    nc.vector.tensor_tensor(sc[:, g % 2, :, :], s, nm, ALU.add).then_inc(shifted, 1)

                def norm(b, par):
                    k = NORM * b
                    dve.wait_ge(o_ready, b + 1)
                    o = core.psum[:, O_BANK, 0:H * (D8 + 1)].rearrange("p (h d) -> p h d", h=H)
                    rd = rden[:, par, :]
                    if guard:
                        nc.vector.tensor_scalar(den[:, par, :], o[:, :, D8], 1e-12, None, ALU.max).then_inc(norm_step, 1)
                        dve.wait_ge(norm_step, k + 1)
                        k = k + 1
                        nc.vector.reciprocal(rd, den[:, par, :]).then_inc(norm_step, 1)
                    else:
                        nc.vector.reciprocal(rd, o[:, :, D8]).then_inc(norm_step, 1)
                    dve.wait_ge(norm_step, k + 1)
                    out = core.branch[:, b, :].rearrange("p (h d) -> p h d", h=H)
                    nc.vector.tensor_tensor(out, o[:, :, 0:D8], rd.rearrange("p (h a) -> p h a", a=1).broadcast_to([T, H, D8]),
                                            ALU.mult).then_inc(o_done, 1)
                    if recip_all is not None:
                        nc.vector.tensor_copy(recip_all[:, b, :], rd).then_inc(norm_step, 1)

                def pair(i, first, last):
                    for par in range(2):
                        b = 2 * i + par
                        for g in range(NU):
                            shift(NU * b + g, g, first and par == 0 and g < 2)
                            if g == 1 and not (first and par == 0):
                                norm(b - 1, 1 - par)
                            if g == 0 and mixed is not None and not (last and par == 1):
                                mix(b + 1, 1 - par)
                            if g == 2 and not (last and par == 1):
                                spread_keys(b + 1, 1 - par)

                if mixed is not None:
                    mix(0, 0)
                spread_keys(0, 0)
                pair(0, True, False)
                with dve.Fori(1, B // 2 - 1) as i:
                    pair(i, False, False)
                pair(B // 2 - 1, False, True)
                norm(B - 1, 1)


def build_route(core, taken, slot_read, prob):
    nc, inp = core.nc, core.inp
    LOGITS, COUNTS, XE = 0, 2, 4
    with Stage(core, "route") as st:
        w_r = st.sb("w_r", [C, E16])
        xt = st.sb("xt", [C, 2, GB, T])
        xs = st.sb("xs", [T, 2, GB, C])
        iota16 = st.sb("iota16", [T, E16])
        iota256 = st.sb("iota256", [T, SLOTS])
        upto = st.sb("upto", [T, T], BF16)
        onesb = st.sb("onesb", [T, T], BF16)
        mx = st.sb("mx", [T, GB])
        lg = st.sb("lg", [T, 2, GB, E16])
        rs = st.sb("rs", [T, GB])
        rr = st.sb("rr", [T, GB])
        pr = st.sb("pr", [T, 2, GB, E16])
        top = st.sb("top", [T, GB, 8])
        idx = st.sb("idx", [T, GB, 8], U32)
        idf = st.sb("idf", [T, GB, 2])
        chosen = st.sb("chosen", [T, 2, GB, 2, E16], BF16)
        ranks = st.sb("ranks", [T, GB, 2, E16])
        pos = st.sb("pos", [T, GB, 2])
        capped = st.sb("capped", [T, GB, 2])
        first_slot = st.sb("first_slot", [T, GB, 2])
        over = st.sb("over", [T, GB, 2])
        slot_in = st.sb("slot_in", [T, GB, 2])
        d1 = st.sb("d1", [T, 2, SLOTS])
        disp = st.sb("disp", [T, 2, SLOTS])
        loaded, consts, src_ready, logit_ready, counted, xe_ready, xe_done = (st.sem(n) for n in (
            "loaded", "consts", "src_ready", "logit_ready", "counted", "xe_ready", "xe_done"))
        shifted, exp_done, step, chosen_done, half, disp_ready = (st.sem(n) for n in (
            "shifted", "exp_done", "step", "chosen_done", "half", "disp_ready"))
        passed = st.sem("passed")
        with nc.Block() as block:
            @block.sync
            def _(sp):
                sp.dma_start(w_r[:, :], inp['L0_ffn_w_router'][:, :]).then_inc(loaded, 16)
                sp.wait_ge(loaded, 16)

            @block.gpsimd
            def _(pool):
                st.clear_retired(pool)
                nc.gpsimd.iota(iota16[:, :], pattern=[[1, E16]], base=0, channel_multiplier=0, allow_small_or_imprecise_dtypes=True).then_inc(consts, 1)
                nc.gpsimd.iota(iota256[:, :], pattern=[[1, SLOTS]], base=0, channel_multiplier=0, allow_small_or_imprecise_dtypes=True).then_inc(consts, 1)
                nc.gpsimd.tensor_copy(onesb[:, :], core.ones[:, :]).then_inc(consts, 1)
                nc.gpsimd.affine_select(out=upto[:, :], in_=core.ones[:, 0:T], compare_op=ALU.is_ge, fill=0.0, base=0,
                                        pattern=[[1, T]], channel_multiplier=-1).then_inc(consts, 1)
                with pool.Fori(0, NG // 2) as i:
                    for par in range(2):
                        n = 2 * i + par
                        pool.wait_ge(xe_ready, GB * n + 1)
                        nc.gpsimd.tensor_copy(xt[:, par, :, :], core.xT[:, bass.ds(n * GB, GB), :]).then_inc(src_ready, 1)
                        nc.gpsimd.tensor_copy(xs[:, par, :, :], core.x[:, bass.ds(n * GB, GB), :]).then_inc(src_ready, 1)

            @block.tensor
            def _(pe):
                pe.wait_ge(loaded, 16)
                pe.wait_ge(consts, 4)
                pe.sem_inc(xe_ready, GB + 1)

                def logits(n, par):
                    pe.wait_ge(src_ready, 2 * n + 1)
                    pe.wait_ge(shifted, n)
                    for j in range(GB):
                        mm = nc.tensor.matmul(core.psum[:, LOGITS + par, j * E16:(j + 1) * E16], xt[:, par, j, :], w_r[:, :], start=True, stop=True)
                    mm.then_inc(logit_ready, 1)

                def dispatch(n, par):
                    pe.wait_ge(chosen_done, n + 1)
                    counts = core.psum[:, COUNTS + par, 0:GB * 2 * E16].rearrange("p (g k e) -> p g k e", g=GB, k=2)
                    nc.tensor.matmul(counts, upto[:, :], chosen[:, par, :, :, :], start=True, stop=False)
                    nc.tensor.matmul(counts[:, :, 1, :], onesb[:, :], chosen[:, par, :, 0, :], start=False, stop=True).then_inc(counted, 1)
                    pe.wait_ge(src_ready, 2 * n + 2)
                    for j in range(GB):
                        pe.wait_ge(disp_ready, GB * n + j + 1)
                        pe.wait_ge(xe_done, GB * n + j + 1)
                        nc.tensor.matmul(core.psum[:, XE + j % 2, 0:SLOTS], xs[:, par, j, :], disp[:, j % 2, :], start=True,
                                         stop=True).then_inc(xe_ready, 1)

                def pair(i, last):
                    for par in range(2):
                        n = 2 * i + par
                        if not (last and par == 1):
                            logits(n + 1, 1 - par)
                        dispatch(n, par)

                logits(0, 0)
                with pe.Fori(0, NG // 2 - 1) as i:
                    pair(i, False)
                pair(NG // 2 - 1, True)

            @block.scalar
            def _(act):
                act.sem_inc(xe_done, 2)
                with act.Fori(0, NG // 2) as i:
                    for par in range(2):
                        n = 2 * i + par
                        act.wait_ge(shifted, n + 2)
                        nc.scalar.activation(pr[:, par, :, :], lg[:, par, :, :], ACT.Exp).then_inc(exp_done, 1)
                        for j in range(GB):
                            act.wait_ge(xe_ready, GB * n + j + 2 + GB)
                            nc.scalar.activation(taken[:, :, bass.ds(n * GB + j, 1), :],
                                                 core.psum[:, XE + j % 2, 0:SLOTS].rearrange("p (e a s) -> p e a s", e=E16, a=1),
                                                 ACT.Identity).then_inc(xe_done, 1)

            @block.vector
            def _(dve):
                dve.wait_ge(consts, 4)
                dve.sem_inc(shifted, 1)
                K = 18
                with dve.Fori(0, NG // 2) as i:
                    for par in range(2):
                        n = 2 * i + par
                        s = K * n
                        wide = lambda t, w: t.rearrange("p (g a) -> p g a", a=1).broadcast_to([T, GB, w])
                        dve.wait_ge(logit_ready, n + 1)
                        lp = core.psum[:, LOGITS + par, 0:GB * E16].rearrange("p (g e) -> p g e", g=GB)
                        nc.vector.tensor_reduce(mx[:, :], lp, X_AXIS, ALU.max, negate=True).then_inc(step, 1)
                        dve.wait_ge(step, s + 1)
                        nc.vector.tensor_tensor(lg[:, par, :, :], lp, wide(mx[:, :], E16), ALU.add).then_inc(shifted, 1)
                        dve.wait_ge(exp_done, n + 1)
                        p = pr[:, par, :, :]
                        nc.vector.tensor_reduce(rs[:, :], p, X_AXIS, ALU.add).then_inc(step, 1)
                        dve.wait_ge(step, s + 2)
                        nc.vector.reciprocal(rr[:, :], rs[:, :]).then_inc(step, 1)
                        dve.wait_ge(step, s + 3)
                        nc.vector.tensor_tensor(p, p, wide(rr[:, :], E16), ALU.mult).then_inc(step, 1)
                        dve.wait_ge(step, s + 4)
                        stand_alone(dve, passed)
                        for j in range(GB):
                            nc.vector.max(top[:, j, :], pr[:, par, j, :]).then_inc(step, 1)
                        dve.wait_ge(step, s + 8)
                        stand_alone(dve, passed)
                        for j in range(GB):
                            nc.vector.max_index(idx[:, j, :], top[:, j, :], pr[:, par, j, :]).then_inc(step, 1)
                        nc.vector.tensor_copy(prob[:, bass.ds(n * GB, GB), :], top[:, :, 0:2]).then_inc(step, 1)
                        dve.wait_ge(step, s + 13)
                        nc.vector.tensor_copy(idf[:, :, :], idx[:, :, 0:2]).then_inc(step, 1)
                        dve.wait_ge(step, s + 14)
                        e_of = idf[:, :, :].rearrange("p g k -> p (g k)")
                        flat = lambda t: t.rearrange("p g k -> p (g k)")
                        nc.vector.tensor_tensor(chosen[:, par, :, :, :].rearrange("p g k e -> p (g k) e"),
                                                iota16[:, :].rearrange("p (a e) -> p a e", a=1).broadcast_to([T, 2 * GB, E16]),
                                                e_of.rearrange("p (q a) -> p q a", a=1).broadcast_to([T, 2 * GB, E16]),
                                                ALU.is_equal).then_inc(chosen_done, 1)
                        dve.wait_ge(chosen_done, n + 1)
                        dve.wait_ge(counted, n + 1)
                        nc.vector.tensor_tensor(ranks[:, :, :, :].rearrange("p g k e -> p (g k) e"),
                                                core.psum[:, COUNTS + par, 0:GB * 2 * E16].rearrange("p (q e) -> p q e", e=E16),
                                                chosen[:, par, :, :, :].rearrange("p g k e -> p (g k) e"), ALU.mult).then_inc(step, 1)
                        dve.wait_ge(step, s + 15)
                        nc.vector.tensor_reduce(flat(pos[:, :, :]), ranks[:, :, :, :].rearrange("p g k e -> p (g k) e"), X_AXIS, ALU.add).then_inc(step, 1)
                        nc.vector.tensor_scalar(flat(first_slot[:, :, :]), e_of, float(CAP), -1.0, ALU.mult, ALU.add).then_inc(step, 1)
                        dve.wait_ge(step, s + 17)
                        nc.vector.scalar_tensor_tensor(out=slot_read[:, bass.ds(n * GB, GB), :], in0=pos[:, :, :], scalar=float(CAP),
                                                       in1=first_slot[:, :, :], op0=ALU.min, op1=ALU.add).then_inc(step, 1)
                        nc.vector.tensor_scalar(flat(over[:, :, :]), flat(pos[:, :, :]), float(CAP), 4.0 * SLOTS, ALU.is_gt, ALU.mult).then_inc(half, 1)
                        dve.wait_ge(half, (2 + GB) * n + 1)
                        dve.wait_ge(step, s + 18)
                        nc.vector.tensor_tensor(slot_in[:, :, :], slot_read[:, bass.ds(n * GB, GB), :], over[:, :, :], ALU.add).then_inc(half, 1)
                        dve.wait_ge(half, (2 + GB) * n + 2)
                        for j in range(GB):
                            nc.vector.tensor_scalar(d1[:, j % 2, :], iota256[:, :], slot_in[:, j, 0:1], None, ALU.is_equal).then_inc(half, 1)
                            dve.wait_ge(half, (2 + GB) * n + 3 + j)
                            dve.wait_ge(xe_ready, GB * n + j + GB)
                            nc.vector.scalar_tensor_tensor(out=disp[:, j % 2, :], in0=iota256[:, :], scalar=slot_in[:, j, 1:2], in1=d1[:, j % 2, :],
                                                           op0=ALU.is_equal, op1=ALU.add).then_inc(disp_ready, 1)


def build_experts(core, taken):
    nc, inp = core.nc, core.inp
    GATE, UP, DOWN = 0, 2, 4
    N = B * CAP
    with Stage(core, "experts") as st:
        wg = st.sb("wg", [C, 2, HID])
        wu = st.sb("wu", [C, 2, HID])
        wp = st.sb("wp", [HID, 2, C])
        sg = st.sb("sg", [HID, 2, N])
        gs = st.sb("gs", [HID, 2, N])
        hid = st.sb("hid", [HID, 2, N])
        loaded = [st.sem("loaded0"), st.sem("loaded1")]
        up_ready, sig_done, gated, hid_ready, down_ready, down_done = (st.sem(n) for n in (
            "up_ready", "sig_done", "gated", "hid_ready", "down_ready", "down_done"))
        passed = st.sem("passed")
        with nc.Block() as block:
            @block.sync
            def _(sp):
                st.clear_retired(sp)

                def load(e, par):
                    sp.dma_start(wg[:, par, :], inp['L0_ffn_w_gate'].rearrange("e c h -> c e h")[:, e, :]).then_inc(loaded[par], 16)
                    sp.dma_start(wu[:, par, :], inp['L0_ffn_w_fc'].rearrange("e c h -> c e h")[:, e, :]).then_inc(loaded[par], 16)
                    sp.dma_start(wp[:, par, :], inp['L0_ffn_w_proj'].rearrange("e h c -> h e c")[:, e, :]).then_inc(loaded[par], 16)
                for par in range(2):
                    load(par, par)
                with sp.Fori(1, E16 // 2) as i:
                    for par in range(2):
                        sp.wait_ge(down_ready, 2 * i + par - 1)
                        load(2 * i + par, par)

            @block.tensor
            def _(pe):
                def up(i, par):
                    e = 2 * i + par
                    pe.wait_ge(loaded[par], 48 * i + 48)
                    pe.wait_ge(hid_ready, e)
                    rhs = taken[:, bass.ds(e, 1), :, :].rearrange("p a b s -> p (a b s)")
                    nc.tensor.matmul(core.psum[0:HID, GATE + par, :], wg[:, par, :], rhs, start=True, stop=True).then_inc(up_ready, 1)
                    nc.tensor.matmul(core.psum[0:HID, UP + par, :], wu[:, par, :], rhs, start=True, stop=True).then_inc(up_ready, 1)

                def down(e, par):
                    pe.wait_ge(hid_ready, e + 2)
                    pe.wait_ge(down_done, e)
                    nc.tensor.matmul(core.psum[:, DOWN + par, :], wp[:, par, :], hid[:, par, :], start=True, stop=True).then_inc(down_ready, 1)

                def pair(i, first):
                    for par in range(2):
                        up(i, par)
                        if not (first and par == 0):
                            down(2 * i + par - 1, 1 - par)
                pair(0, True)
                with pe.Fori(1, E16 // 2) as i:
                    pair(i, False)
                down(E16 - 1, 1)

            @block.scalar
            def _(act):
                act.sem_inc(down_done, 1)

                def sigmoid(e, par):
                    act.wait_ge(up_ready, 2 * e + 1)
                    act.wait_ge(gated, e)
                    nc.scalar.activation(sg[:, par, :], core.psum[0:HID, GATE + par, :], ACT.Sigmoid).then_inc(sig_done, 1)

                def copy_down(e, par):
                    act.wait_ge(down_ready, e + 1)
                    nc.scalar.activation(taken[:, bass.ds(e, 1), :, :].rearrange("p a b s -> p (a b s)"), core.psum[:, DOWN + par, :],
                                         ACT.Identity).then_inc(down_done, 1)

                def pair(i, first):
                    for par in range(2):
                        sigmoid(2 * i + par, par)
                        if not (first and par == 0):
                            copy_down(2 * i + par - 1, 1 - par)
                pair(0, True)
                with act.Fori(1, E16 // 2) as i:
                    pair(i, False)
                copy_down(E16 - 1, 1)

            @block.vector
            def _(dve):
                dve.sem_inc(gated, 1)
                dve.sem_inc(hid_ready, 1)
                dve.wait_ge(gated, 1)
                with dve.Fori(0, E16 // 2) as i:
                    for par in range(2):
                        e = 2 * i + par
                        dve.wait_ge(sig_done, e + 1)
                        nc.vector.tensor_tensor(gs[:, par, :], core.psum[0:HID, GATE + par, :], sg[:, par, :], ALU.mult).then_inc(gated, 1)
                        dve.wait_ge(gated, e + 2)
                        dve.wait_ge(up_ready, 2 * e + 2)
                        nc.vector.tensor_tensor(hid[:, par, :], core.psum[0:HID, UP + par, :], gs[:, par, :], ALU.mult).then_inc(hid_ready, 1)


def build_combine(core, taken, slot_read, prob):
    nc = core.nc
    with Stage(core, "combine") as st:
        iota256 = st.sb("iota256", [T, SLOTS])
        c1 = st.sb("c1", [T, 2, SLOTS])
        c2 = st.sb("c2", [T, 2, SLOTS])
        cw = st.sb("cw", [T, 2, SLOTS])
        eo = st.sb("eo", [C, 2, SLOTS])
        cwT = st.sb("cwT", [128, 2, 2, T])
        eoT = st.sb("eoT", [128, 2, 2, C])
        consts, eo_ready, step, cw_ready, cwT_ready, eoT_ready, cwT_done, eoT_done, y_ready, y_done = (st.sem(n) for n in (
            "consts", "eo_ready", "step", "cw_ready", "cwT_ready", "eoT_ready", "cwT_done", "eoT_done", "y_ready", "y_done"))
        CW_BANK, EO_BANK, Y_BANK = 0, 2, 4
        passed = st.sem("passed")
        with nc.Block() as block:
            @block.gpsimd
            def _(pool):
                st.clear_retired(pool)
                nc.gpsimd.iota(iota256[:, :], pattern=[[1, SLOTS]], base=0, channel_multiplier=0, allow_small_or_imprecise_dtypes=True).then_inc(consts, 1)
                with pool.Fori(0, B // 2) as i:
                    for par in range(2):
                        b = 2 * i + par
                        pool.wait_ge(eoT_ready, b + 1)
                        nc.gpsimd.tensor_copy(eo[:, par, :].rearrange("p (e a s) -> p e a s", e=E16, a=1),
                                              taken[:, :, bass.ds(b, 1), :]).then_inc(eo_ready, 1)

            @block.tensor
            def _(pe):
                pe.sem_inc(eoT_ready, 2)
                pe.sem_inc(y_ready, 2)
                pe.sem_inc(cwT_ready, 1)

                def turn(b, par):
                    pe.wait_ge(cw_ready, b + 1)
                    pe.wait_ge(cwT_done, b)
                    for s in range(2):
                        mm = nc.tensor.transpose(core.psum[:, CW_BANK + par, s * T:(s + 1) * T], cw[:, par, s * 128:(s + 1) * 128], core.ident[:, :])
                    mm.then_inc(cwT_ready, 1)
                    pe.wait_ge(eo_ready, b + 1)
                    pe.wait_ge(eoT_done, b)
                    for s in range(2):
                        mm = nc.tensor.transpose(core.psum[:, EO_BANK + par, s * C:(s + 1) * C], eo[:, par, s * 128:(s + 1) * 128], core.ident[:, :])
                    mm.then_inc(eoT_ready, 1)

                def gather(b, par):
                    pe.wait_ge(cwT_done, b + 2)
                    pe.wait_ge(eoT_done, b + 2)
                    pe.wait_ge(y_done, b)
                    for s in range(2):
                        mm = nc.tensor.matmul(core.psum[:, Y_BANK + par, 0:C], cwT[:, par, s, :], eoT[:, par, s, :], start=(s == 0), stop=(s == 1))
                    mm.then_inc(y_ready, 1)

                def pair(i, first):
                    for par in range(2):
                        turn(2 * i + par, par)
                        if not (first and par == 0):
                            gather(2 * i + par - 1, 1 - par)
                pair(0, True)
                with pe.Fori(1, B // 2) as i:
                    pair(i, False)
                gather(B - 1, 1)

            @block.scalar
            def _(act):
                act.sem_inc(cwT_done, 1)
                act.sem_inc(eoT_done, 1)
                with act.Fori(0, B // 2) as i:
                    for par in range(2):
                        b = 2 * i + par
                        act.wait_ge(cwT_ready, b + 2)
                        act.wait_ge(y_ready, b + 1)
                        nc.scalar.activation(cwT[:, par, :, :], core.psum[:, CW_BANK + par, 0:SLOTS].rearrange("p (s t) -> p s t", s=2),
                                             ACT.Identity).then_inc(cwT_done, 1)
                        act.wait_ge(eoT_ready, b + 3)
                        nc.scalar.activation(eoT[:, par, :, :], core.psum[:, EO_BANK + par, 0:SLOTS].rearrange("p (s c) -> p s c", s=2),
                                             ACT.Identity).then_inc(eoT_done, 1)

            @block.vector
            def _(dve):
                dve.wait_ge(consts, 1)
                dve.sem_inc(y_done, 1)

                def weights(b, par):
                    for k, dst in enumerate((c1, c2)):
                        nc.vector.tensor_scalar(dst[:, par, :], iota256[:, :], slot_read[:, b, k:k + 1], prob[:, b, k:k + 1],
                                                ALU.is_equal, ALU.mult).then_inc(step, 1)
                    dve.wait_ge(step, 2 * b + 2)
                    dve.wait_ge(cwT_ready, b)
                    nc.vector.tensor_tensor(cw[:, par, :], c1[:, par, :], c2[:, par, :], ALU.add).then_inc(cw_ready, 1)

                def keep(b, par):
                    dve.wait_ge(y_ready, b + 3)
                    stand_alone(dve, passed)
                    nc.vector.tensor_copy(core.branch[:, b, :], core.psum[:, Y_BANK + par, 0:C]).then_inc(y_done, 1)

                def pair(i, first):
                    for par in range(2):
                        weights(2 * i + par, par)
                        if not (first and par == 0):
                            keep(2 * i + par - 1, 1 - par)
                pair(0, True)
                with dve.Fori(1, B // 2) as i:
                    pair(i, False)
                keep(B - 1, 1)


def build_attention64(core, name):
    nc, inp = core.nc, core.inp
    scale = float(D64) ** -0.5
    nk = NCTX
    INNER = H * D64
    QK = 2 * T + 2 * nk
    S_BANK, T_BANK, O_BANK, OT_BANK, Y_BANK, QK_BANK, V_BANK = 0, 2, 3, 4, 5, 6, 7
    with Stage(core, name) as st:
        wq = st.sb("wq", [C, INNER])
        wk = st.sb("wk", [CC, INNER])
        wv = st.sb("wv", [CC, INNER])
        wo = st.sb("wo", [128, H // 2, C])
        xc = st.sb("xc", [C, 2, T])
        cc = st.sb("cc", [CC, 2, nk])
        qT = st.sb("qT", [128, NU, 2, T])
        keys_q = st.sb("keys_q", [128, NU, 2, 2, nk])
        va = st.sb("va", [nk, NU, QUAD, D64 + 1])
        sc = st.sb("sc", [T, 2, QUAD, nk])
        pT = st.sb("pT", [nk, 2, QUAD, T])
        on = st.sb("on", [T, 2, QUAD, D64])
        oT = st.sb("oT", [128, 2, 2, T])
        negmax = st.sb("negmax", [T, 2, QUAD])
        rden = st.sb("rden", [T, 2, QUAD])
        loaded, consts, src_ready, projected = (st.sem(n) for n in ("loaded", "consts", "src_ready", "projected"))
        qk_done, v_done, scored, max_step, shifted, p_ready, turned, pT_ready = (st.sem(n) for n in (
            "qk_done", "v_done", "scored", "max_step", "shifted", "p_ready", "turned", "pT_ready"))
        o_ready, den_step, o_done, o_turned, oT_done, y_ready, y_done, y_part = (st.sem(n) for n in (
            "o_ready", "den_step", "o_done", "o_turned", "oT_done", "y_ready", "y_done", "y_part"))
        UNITS = NU * B

        passed = st.sem("passed")
        with nc.Block() as block:
            @block.sync
            def _(sp):
                for dst, src in ((wq[:, :], inp['L1_xattn_Wq'][:, :]), (wk[:, :], inp['L1_xattn_Wk'][:, :]), (wv[:, :], inp['L1_xattn_Wv'][:, :]),
                                 (wo[:, :, :], inp['L1_xattn_Wo'].rearrange("(t p) c -> p t c", p=128))):
                    sp.dma_start(dst, src).then_inc(loaded, 16)
                sp.wait_ge(loaded, 64)

            @block.gpsimd
            def _(pool):
                st.clear_retired(pool)
                nc.gpsimd.memset(keys_q[:, :, :, :, :], 0.0).then_inc(consts, 1)
                nc.gpsimd.memset(va[:, :, :, D64:D64 + 1], 1.0).then_inc(consts, 1)
                with pool.Fori(0, B // 2) as i:
                    for par in range(2):
                        b = 2 * i + par
                        pool.wait_ge(projected, 2 * NU * b + 1)
                        nc.gpsimd.tensor_copy(xc[:, par, :], core.xT[:, b, :]).then_inc(src_ready, 1)
                        nc.gpsimd.tensor_copy(cc[:, par, :], core.ctxT[:, b, :]).then_inc(src_ready, 1)

            @block.tensor
            def _(pe):
                pe.sem_inc(projected, 2 * NU + 1)
                pe.wait_ge(loaded, 64)
                pe.wait_ge(consts, 2)

                def project(b, par, g):
                    u = NU * b + g
                    if g == 0:
                        pe.wait_ge(src_ready, 2 * b + 2)
                    pe.wait_ge(qk_done, 3 * u)
                    for k in range(2):
                        cols = slice((2 * g + k) * 128, (2 * g + k + 1) * 128)
                        nc.tensor.matmul(core.psum[:, QK_BANK, k * T:(k + 1) * T], wq[:, cols], xc[:, par, :], start=True, stop=True)
                        mm = nc.tensor.matmul(core.psum[:, QK_BANK, 2 * T + k * nk:2 * T + (k + 1) * nk], wk[:, cols], cc[:, par, :],
                                              start=True, stop=True)
                    mm.then_inc(projected, 1)
                    pe.wait_ge(v_done, u)
                    nc.tensor.matmul(core.psum[0:nk, V_BANK, 0:QUAD * D64], cc[:, par, :], wv[:, g * QUAD * D64:(g + 1) * QUAD * D64],
                                     start=True, stop=True).then_inc(projected, 1)

                def score(b, par, g):
                    u = NU * b + g
                    pe.wait_ge(qk_done, 3 * u + 3)
                    pe.wait_ge(shifted, u)
                    for k in range(2):
                        mm = nc.tensor.matmul(core.psum[:, S_BANK + g % 2, 2 * k * nk:2 * (k + 1) * nk], qT[:, g, k, :], keys_q[:, g, k, :, :],
                                              start=True, stop=True)
                    mm.then_inc(scored, 1)

                def turn(b, par, g):
                    u = NU * b + g
                    pe.wait_ge(p_ready, u + 1)
                    pe.wait_ge(pT_ready, u)
                    for j in range(QUAD):
                        mm = nc.tensor.transpose(core.psum[0:nk, T_BANK, j * T:(j + 1) * T], sc[:, g % 2, j, :], core.ident[:, :])
                    mm.then_inc(turned, 1)

                def weigh(b, par, g):
                    u = NU * b + g
                    pe.wait_ge(pT_ready, u + 1)
                    pe.wait_ge(v_done, u + 1)
                    pe.wait_ge(o_done, u)
                    for j in range(QUAD):
                        mm = nc.tensor.matmul(core.psum[:, O_BANK, j * (D64 + 1):(j + 1) * (D64 + 1)], pT[:, g % 2, j, :], va[:, g, j, :],
                                              start=True, stop=True)
                    mm.then_inc(o_ready, 1)

                def turn_o(b, par, g):
                    u = NU * b + g
                    pe.wait_ge(o_done, u + 1)
                    pe.wait_ge(oT_done, u)
                    for k in range(2):
                        mm = nc.tensor.transpose(core.psum[:, OT_BANK, k * T:(k + 1) * T],
                                                 on[:, g % 2, 2 * k:2 * k + 2, :].rearrange("p a d -> p (a d)"), core.ident[:, :])
                    mm.then_inc(o_turned, 1)

                def out_project(b, par, g):
                    u = NU * b + g
                    pe.wait_ge(oT_done, u + 1)
                    if g == 0:
                        pe.wait_ge(y_done, b)
                    for k in range(2):
                        mm = nc.tensor.matmul(core.psum[:, Y_BANK, 0:C], oT[:, g % 2, k, :], wo[:, 2 * g + k, :],
                                              start=(g == 0 and k == 0), stop=(g == NU - 1 and k == 1))
                    if g == NU - 1:
                        mm.then_inc(y_ready, 1)

                steps = [(score, 0), (weigh, 2), (turn, 1), (turn_o, 3), (out_project, 4), (project, -2)]

                def at(i, par, g, back):
                    t = NU * par + g - back
                    return 2 * i + t // NU, (t // NU) % 2, t % NU

                def pair(i, first, last):
                    for par in range(2):
                        for g in range(NU):
                            for step, back in steps:
                                t = NU * par + g - back
                                if (first and t < 0) or (last and t >= 2 * NU):
                                    continue
                                step(*at(i, par, g, back))

                project(0, 0, 0)
                project(0, 0, 1)
                pair(0, True, False)
                with pe.Fori(1, B // 2 - 1) as i:
                    pair(i, False, False)
                pair(B // 2 - 1, False, True)
                for over in range(4):
                    for step, back in steps:
                        t = 2 * NU + over - back
                        if back > over:
                            step(*at(B // 2 - 1, 0, 2 * NU + over, back))

            @block.scalar
            def _(act):
                def copy_qk(u, g):
                    act.wait_ge(projected, 2 * u + 2 + 2 * NU)
                    nc.scalar.activation(qT[:, g, :, :], core.psum[:, QK_BANK, 0:2 * T].rearrange("p (k t) -> p k t", k=2),
                                         ACT.Identity).then_inc(qk_done, 1)
                    for a in range(2):
                        rows = slice(D64 * a, D64 * a + D64)
                        nc.scalar.activation(keys_q[rows, g, :, a, :], core.psum[rows, QK_BANK, 2 * T:QK].rearrange("p (k n) -> p k n", k=2),
                                             ACT.Identity).then_inc(qk_done, 1)

                def exponential(u, g):
                    act.wait_ge(shifted, u + 2)
                    nc.scalar.activation(sc[:, g % 2, :, :], sc[:, g % 2, :, :], ACT.Exp, scale=scale).then_inc(p_ready, 1)

                def copy_pT(u, g):
                    act.wait_ge(turned, u + 1)
                    nc.scalar.activation(pT[:, g % 2, :, :], core.psum[0:nk, T_BANK, :].rearrange("p (j t) -> p j t", j=QUAD),
                                         ACT.Identity).then_inc(pT_ready, 1)

                def copy_oT(u, g):
                    act.wait_ge(o_turned, u + 1)
                    nc.scalar.activation(oT[:, g % 2, :, :], core.psum[:, OT_BANK, 0:2 * T].rearrange("p (k t) -> p k t", k=2),
                                         ACT.Identity).then_inc(oT_done, 1)

                steps = [(exponential, 0), (copy_pT, 1), (copy_oT, 3), (copy_qk, -2)]

                def pair(i, first, last):
                    for t0 in range(2 * NU):
                        for step, back in steps:
                            t = t0 - back
                            if (first and t < 0) or (last and t >= 2 * NU):
                                continue
                            step(2 * NU * i + t, t % NU)

                act.wait_ge(consts, 2)
                copy_qk(0, 0)
                copy_qk(1, 1)
                pair(0, True, False)
                with act.Fori(1, B // 2 - 1) as i:
                    pair(i, False, False)
                pair(B // 2 - 1, False, True)
                for over in range(3):
                    for step, back in steps:
                        if back > over:
                            step(UNITS + over - back, (over - back) % NU)

            @block.vector
            def _(dve):
                dve.sem_inc(shifted, 1)

                def copy_v(u, g):
                    dve.wait_ge(projected, 2 * u + 3 + 2 * NU)
                    nc.vector.tensor_copy(va[:, g, :, 0:D64], core.psum[0:nk, V_BANK, 0:QUAD * D64].rearrange("p (j d) -> p j d", j=QUAD)).then_inc(v_done, 1)

                def shift(u, g, fresh=False):
                    dve.wait_ge(scored, u + 1)
                    s = core.psum[:, S_BANK + g % 2, 0:QUAD * nk].rearrange("p (j n) -> p j n", j=QUAD)
                    nc.vector.tensor_reduce(negmax[:, g % 2, :], s, X_AXIS, ALU.max, negate=True).then_inc(max_step, 1)
                    dve.wait_ge(max_step, u + 1)
                    if not fresh:
                        dve.wait_ge(turned, u - 1)
                    nm = negmax[:, g % 2, :].rearrange("p (q a) -> p q a", a=1).broadcast_to([T, QUAD, nk])
                    nc.vector.tensor_tensor(sc[:, g % 2, :, :], s, nm, ALU.add).then_inc(shifted, 1)

                def norm(u, g, fresh=False):
                    dve.wait_ge(o_ready, u + 1)
                    o = core.psum[:, O_BANK, 0:QUAD * (D64 + 1)].rearrange("p (j d) -> p j d", j=QUAD)
                    nc.vector.reciprocal(rden[:, g % 2, :], o[:, :, D64]).then_inc(den_step, 1)
                    dve.wait_ge(den_step, u + 1)
                    if not fresh:
                        dve.wait_ge(o_turned, u - 1)
                    rd = rden[:, g % 2, :].rearrange("p (j a) -> p j a", a=1).broadcast_to([T, QUAD, D64])
                    nc.vector.tensor_tensor(on[:, g % 2, :, :], o[:, :, 0:D64], rd, ALU.mult).then_inc(o_done, 1)

                def keep_y(b):
                    dve.wait_ge(y_ready, b + 1)
                    stand_alone(dve, passed)
                    nc.vector.tensor_copy(core.branch[:, b, :], core.psum[:, Y_BANK, 0:C]).then_inc(y_done, 1)

                steps = [(shift, 0), (norm, 2), (copy_v, -2)]

                def pair(i, first, last):
                    for t0 in range(2 * NU):
                        for step, back in steps:
                            t = t0 - back
                            if (first and t < 0) or (last and t >= 2 * NU):
                                continue
                            if step is copy_v:
                                step(2 * NU * i + t, t % NU)
                            else:
                                step(2 * NU * i + t, t % NU, first and t < 2)
                        if t0 % NU == NU - 1 and not (first and t0 < NU):
                            keep_y(2 * i + t0 // NU - 1)

                copy_v(0, 0)
                copy_v(1, 1)
                pair(0, True, False)
                with dve.Fori(1, B // 2 - 1) as i:
                    pair(i, False, False)
                pair(B // 2 - 1, False, True)
                for over in range(2):
                    norm(UNITS + over - 2, (over - 2) % NU)
                keep_y(B - 1)


def build_gate(core, gate, mixed_bias, experts):
    nc, inp = core.nc, core.inp
    E4, HG = 4, 128
    with Stage(core, "gate") as st:
        w1 = st.sb("w1", [C, HG])
        b1 = st.sb("b1", [HG, 1])
        w2 = st.sb("w2", [HG, E4])
        b2 = st.sb("b2", [1, E4])
        be = st.sb("be", [E4, 3, C])
        pooled = st.sb("pooled", [C, B])
        mean = st.sb("mean", [C, B])
        hid = st.sb("hid", [HG, B])
        lg = st.sb("lg", [B, 8])
        top = st.sb("top", [B, 8])
        idx = st.sb("idx", [B, 8], U32)
        idf = st.sb("idf", [B, 2])
        diff = st.sb("diff", [B, 2])
        ex = st.sb("ex", [B, 2])
        sm = st.sb("sm", [B, 2])
        total = st.sb("total", [B, 2])
        iota4 = st.sb("iota4", [B, E4])
        w_1 = st.sb("w_1", [B, E4])
        w_2 = st.sb("w_2", [B, E4])
        w = st.sb("w", [B, E4])
        wT = st.sb("wT", [E4, B])
        diag = st.sb("diag", [B, B, E4])
        loaded, consts, step, mm, acted = (st.sem(n) for n in ("loaded", "consts", "step", "mm", "acted"))
        passed = st.sem("passed")
        with nc.Block() as block:
            @block.sync
            def _(sp):
                n = 0
                for dst, src in ((w1[:, :], inp['L1_ffn_Wg1'][:, :]), (b1[:, :], col(inp['L1_ffn_bg1'])), (w2[:, :], inp['L1_ffn_Wg2'][:, :]),
                                 (b2[:, :], row(inp['L1_ffn_bg2'])), (be[:, 0, :], inp['L1_ffn_bq'][:, :]), (be[:, 1, :], inp['L1_ffn_bk'][:, :]),
                                 (be[:, 2, :], inp['L1_ffn_bv'][:, :])):
                    sp.dma_start(dst, src).then_inc(loaded, 16)
                    n += 1
                for k, name in enumerate(('L1_ffn_Wq', 'L1_ffn_Wk', 'L1_ffn_Wv')):
                    sp.dma_start(experts[:, :, k * C:(k + 1) * C], inp[name].rearrange("e c d -> c e d")).then_inc(loaded, 16)
                    n += 1
                sp.wait_ge(loaded, 16 * n)

            @block.gpsimd
            def _(pool):
                st.clear_retired(pool)
                nc.gpsimd.iota(iota4[:, :], pattern=[[1, E4]], base=0, channel_multiplier=0, allow_small_or_imprecise_dtypes=True).then_inc(consts, 1)

            @block.tensor
            def _(pe):
                pe.wait_ge(loaded, 160)
                pe.wait_ge(step, 2)
                nc.tensor.matmul(core.psum[0:HG, 0, 0:B], w1[:, :], mean[:, :], start=True, stop=True).then_inc(mm, 1)
                pe.wait_ge(step, 3)
                nc.tensor.matmul(core.psum[0:B, 1, 0:E4], hid[:, :], w2[:, :], start=True, stop=False)
                nc.tensor.matmul(core.psum[0:B, 1, 0:E4], core.ones[0:1, 0:B], b2[:, :], start=False, stop=True).then_inc(mm, 1)
                pe.wait_ge(step, 14)
                nc.tensor.transpose(core.psum[0:E4, 2, 0:B], w[:, :], core.ident[0:B, 0:B]).then_inc(mm, 1)
                pe.wait_ge(step, 15)
                nc.tensor.matmul(core.psum[:, 3, 0:B * E4], core.ones[0:B, :], diag[:, :, :].rearrange("p b e -> p (b e)"), start=True, stop=True).then_inc(mm, 1)
                pe.wait_ge(step, 16)
                for k in range(3):
                    nc.tensor.matmul(core.psum[:, 4 + k, 0:B], be[:, k, :], wT[:, :], start=True, stop=True).then_inc(mm, 1)

            @block.scalar
            def _(act):
                act.wait_ge(step, 7)
                nc.scalar.activation(ex[:, :], diff[:, :], ACT.Exp).then_inc(acted, 1)

            @block.vector
            def _(dve):
                v = nc.vector
                dve.wait_ge(loaded, 160)
                dve.wait_ge(consts, 1)
                v.tensor_reduce(pooled[:, :], core.xT[:, :, :], X_AXIS, ALU.add).then_inc(step, 1)
                dve.wait_ge(step, 1)
                v.tensor_scalar(mean[:, :], pooled[:, :], 1.0 / T, None, ALU.mult).then_inc(step, 1)
                dve.wait_ge(mm, 1)
                v.tensor_scalar(hid[:, :], core.psum[0:HG, 0, 0:B], b1[:, :], 0.0, ALU.add, ALU.max).then_inc(step, 1)
                v.memset(lg[:, :], NEG).then_inc(step, 1)
                dve.wait_ge(mm, 2)
                dve.wait_ge(step, 4)
                v.tensor_copy(lg[:, 0:E4], core.psum[0:B, 1, 0:E4]).then_inc(step, 1)
                dve.wait_ge(step, 5)
                v.max(top[:, :], lg[:, :]).then_inc(step, 1)
                dve.wait_ge(step, 6)
                v.tensor_scalar(diff[:, :], top[:, 0:2], top[:, 0:1], None, ALU.subtract).then_inc(step, 1)
                v.max_index(idx[:, :], top[:, :], lg[:, :]).then_inc(step, 1)
                dve.wait_ge(step, 8)
                v.tensor_copy(idf[:, :], idx[:, 0:2]).then_inc(step, 1)
                dve.wait_ge(acted, 1)
                v.tensor_reduce(total[:, 0:1], ex[:, :], X_AXIS, ALU.add).then_inc(step, 1)
                dve.wait_ge(step, 10)
                v.reciprocal(total[:, 1:2], total[:, 0:1]).then_inc(step, 1)
                dve.wait_ge(step, 11)
                v.tensor_scalar(sm[:, :], ex[:, :], total[:, 1:2], None, ALU.mult).then_inc(step, 1)
                dve.wait_ge(step, 12)
                v.tensor_scalar(w_1[:, :], iota4[:, :], idf[:, 0:1], sm[:, 0:1], ALU.is_equal, ALU.mult).then_inc(step, 1)
                v.tensor_scalar(w_2[:, :], iota4[:, :], idf[:, 1:2], sm[:, 1:2], ALU.is_equal, ALU.mult).then_inc(acted, 1)
                dve.wait_ge(step, 13)
                dve.wait_ge(acted, 2)
                v.tensor_tensor(w[:, :], w_1[:, :], w_2[:, :], ALU.add).then_inc(step, 1)
                dve.wait_ge(step, 14)
                v.tensor_tensor(diag[:, :, :], core.ident[0:B, 0:B].rearrange("p (b a) -> p b a", a=1).broadcast_to([B, B, E4]),
                                w[:, :].rearrange("p (a e) -> p a e", a=1).broadcast_to([B, B, E4]), ALU.mult).then_inc(step, 1)
                dve.wait_ge(mm, 3)
                v.tensor_copy(wT[:, :], core.psum[0:E4, 2, 0:B]).then_inc(step, 1)
                dve.wait_ge(mm, 4)
                v.tensor_copy(gate[:, :], core.psum[:, 3, 0:B * E4]).then_inc(acted, 1)
                dve.wait_ge(mm, 7)
                v.tensor_copy(mixed_bias[:, :, :], core.psum[:, 4:7, 0:B]).then_inc(acted, 1)


def build(nc, inp, out, stages=None):
    with ExitStack() as ctx:
        core = Core(nc, ctx, inp, out)
        recip_all = core.sb("recip_all", [T, B, H])
        taken = core.sb("taken", [C, E16, B, CAP])
        slot_read = core.sb("slot_read", [T, B, 2])
        prob = core.sb("prob", [T, B, 2])
        gate = core.sb("gate", [128, B * 4])
        mixed_bias = core.sb("mixed_bias", [C, 3, B])
        experts = core.sb("experts", [C, 4, 3 * C])
        steps = [
            lambda: build_setup(core),
            lambda: build_gru(core),
            lambda: build_close(core, "close0", turned=True),
            lambda: build_attention8(core, "xattn0", NCTX, inp['L0_xattn_Wq'][:, :], inp['L0_xattn_Wk'][:, :], inp['L0_xattn_Wv'][:, :],
                                     cross=True, b_q=inp['L0_xattn_bq'], b_k=inp['L0_xattn_bk'], clip=True, recip_all=recip_all),
            lambda: build_close(core, "close1", wo=inp['L0_xattn_Wo'][:, :], v_bias=inp['L0_xattn_bv'], out_bias=inp['L0_xattn_bo'], nan_guard=(recip_all, inp['L0_xattn_Wv'][:, :])),
            lambda: build_route(core, taken, slot_read, prob),
            lambda: build_experts(core, taken),
            lambda: build_combine(core, taken, slot_read, prob),
            lambda: build_close(core, "close2"),
            lambda: build_attention8(core, "attn1", T, None, None, None, transposed=(4, 5, 6), causal=True, guard=True),
            lambda: build_close(core, "close3", wo=core.wT[:, 7, :]),
            lambda: build_attention64(core, "xattn1"),
            lambda: build_close(core, "close4", out_bias=inp['L1_xattn_bo']),
            lambda: build_gate(core, gate, mixed_bias, experts),
            lambda: build_attention8(core, "ffn1", T, None, None, None, mixed=(gate, mixed_bias, experts)),
            lambda: build_close(core, "close5", wo=inp['L1_ffn_Wo'][:, :], v_bias_by_batch=mixed_bias[:, 2, :], out_bias=inp['L1_ffn_bo'],
                                last=True),
        ]
        n = len(steps) if stages is None else stages
        for step in steps[:n]:
            step()


def kernel(**inputs):
    import numpy as np
    import concourse.bacc as bacc
    from concourse.bass_utils import run_bass_kernel_spmd

    nc = bacc.Bacc("TRN2", target_bir_lowering=False, num_devices=1)
    arrays, inp = {}, {}
    for name in INS:
        a = np.ascontiguousarray(inputs[name])
        arrays[f"in_{name}_dram"] = a
        inp[name] = nc.dram_tensor(f"in_{name}_dram", a.shape, mybir.dt.from_np(a.dtype), kind="ExternalInput").ap()
    out = nc.dram_tensor("out_0_dram", (B, T, C), F32, kind="ExternalOutput").ap()
    build(nc, inp, out)
    return run_bass_kernel_spmd(nc, [arrays], core_ids=[0]).results[0]["out_0_dram"]
```

```python
from contextlib import ExitStack

import concourse.bass as bass
from concourse import mybir

F32 = mybir.dt.float32
BF16 = mybir.dt.bfloat16
U32 = mybir.dt.uint32
ALU = mybir.AluOpType
ACT = mybir.ActivationFunctionType
X_AXIS = mybir.AxisListType.X

B = 32
T = 128
C = 128
NCTX = 77
CC = 96
H = 16
D8 = C // H
D64 = 64
QUAD = 4
NU = H // QUAD
GB = 4
NG = B // GB
E16 = 16
CAP = 16
SLOTS = E16 * CAP
HID = 64
EPS = 1e-5
CLAMP = 10000.0
NEG = -3.0e38

INS = ['x', 'ctx_768', 'L0_attn_Wz', 'L0_attn_bz', 'L0_attn_Wh', 'L0_attn_bh', 'L0_xattn_Wq', 'L0_xattn_bq',
       'L0_xattn_Wk', 'L0_xattn_bk', 'L0_xattn_Wv', 'L0_xattn_bv', 'L0_xattn_Wo', 'L0_xattn_bo',
       'L0_ffn_w_router', 'L0_ffn_w_fc', 'L0_ffn_w_gate', 'L0_ffn_w_proj', 'L1_attn_Wq', 'L1_attn_Wk',
       'L1_attn_Wv', 'L1_attn_Wo', 'L1_xattn_Wq', 'L1_xattn_Wk', 'L1_xattn_Wv', 'L1_xattn_Wo', 'L1_xattn_bo',
       'L1_ffn_Wq', 'L1_ffn_bq', 'L1_ffn_Wk', 'L1_ffn_bk', 'L1_ffn_Wv', 'L1_ffn_bv', 'L1_ffn_Wg1', 'L1_ffn_bg1',
       'L1_ffn_Wg2', 'L1_ffn_bg2', 'L1_ffn_Wo', 'L1_ffn_bo']


class Core:

    def __init__(self, nc, ctx, inp, out):
        self.nc, self.ctx, self.inp, self.out = nc, ctx, inp, out
        self.retired = []
        self.psum = ctx.enter_context(nc.psum_tensor("psum", [128, 8, 512], F32))
        self.x = self.sb("x", [T, B, C])
        self.xT = self.sb("xT", [C, B, T])
        self.branch = self.sb("branch", [128, B, 128])
        self.ctxT = self.sb("ctxT", [CC, B, NCTX])
        self.ident = self.sb("ident", [128, 128])
        self.ones = self.sb("ones", [128, 128])
        self.zeros = self.sb("zeros", [128, 512])
        self.pow_half = self.sb("pow_half", [128, GB])
        self.head_mask = self.sb("head_mask", [128, H])
        self.wT = self.sb("wT", [128, 8, 128])

    def sb(self, name, shape, dt=F32):
        return self.ctx.enter_context(self.nc.sbuf_tensor(name, shape, dt))

    def bank(self, n):
        return self.psum[:, n, :]


class Stage:

    def __init__(self, core, name):
        self.core, self.name, self.ctx, self.sems = core, name, ExitStack(), []

    def __enter__(self):
        return self

    def __exit__(self, *_):
        self.ctx.close()
        for handle in self.core.retired:
            self.core.nc.release_semaphore(handle)
        self.core.retired = self.sems

    def sb(self, name, shape, dt=F32):
        return self.ctx.enter_context(self.core.nc.sbuf_tensor(f"{self.name}_{name}", shape, dt))

    def sem(self, name):
        self.sems.append(self.core.nc.alloc_semaphore(name=f"{self.name}_{name}"))
        return self.sems[-1]

    def clear_retired(self, engine):
        numbers = sorted(handle.num for handle in self.core.retired)
        while numbers:
            run = 1
            while run < len(numbers) and numbers[run] == numbers[0] + run:
                run += 1
            engine.sem_clear(range(numbers[0], numbers[0] + run))
            numbers = numbers[run:]


def stand_alone(engine, passed):
    engine.sem_inc(passed, 1)


def row(ap):
    return ap.rearrange("(a n) -> a n", a=1)


def col(ap):
    return ap.rearrange("(n a) -> n a", a=1)


def build_setup(core):
    nc, inp = core.nc, core.inp
    with Stage(core, "setup") as st:
        wn = st.sb("w_natural", [128, 8, 128])
        xin = st.sb("xin", [T, 2, GB, C])
        cin = st.sb("cin", [NCTX, 2, GB, CC])
        loaded_w, loaded_x, loaded_res = st.sem("loaded_w"), [st.sem("loaded_x0"), st.sem("loaded_x1")], st.sem("loaded_res")
        zeroed, ident_ready, consts = st.sem("zeroed"), st.sem("ident_ready"), st.sem("consts")
        tr_ready, xT_done, cT_done, w_ready, w_done = (st.sem(n) for n in ("tr_ready", "xT_done", "cT_done", "w_ready", "w_done"))
        x_g = inp['x'].rearrange("(n g) t c -> n t g c", g=GB)
        c_g = inp['ctx_768'].rearrange("(n g) t c -> n t g c", g=GB)

        passed = st.sem("passed")
        with nc.Block() as block:
            @block.sync
            def _(sp):
                for k, (name, l) in enumerate([('L0_attn_Wz', 0), ('L0_attn_Wz', 1), ('L0_attn_Wh', 0), ('L0_attn_Wh', 1)]):
                    sp.dma_start(wn[:, k, :], inp[name][l]).then_inc(loaded_w, 16)
                for k, name in enumerate(['L1_attn_Wq', 'L1_attn_Wk', 'L1_attn_Wv', 'L1_attn_Wo']):
                    sp.dma_start(wn[:, 4 + k, :], inp[name][:, :]).then_inc(loaded_w, 16)
                sp.dma_start(core.x[:, :, :], inp['x'].rearrange("b t c -> t b c")).then_inc(loaded_res, 16)
                for par in range(2):
                    sp.dma_start(xin[:, par, :, :], x_g[par]).then_inc(loaded_x[par], 16)
                    sp.dma_start(cin[:, par, :, :], c_g[par]).then_inc(loaded_x[par], 16)
                with sp.Fori(1, NG // 2) as i:
                    for par in range(2):
                        sp.wait_ge(tr_ready, 4 * i + 2 * par - 2)
                        sp.dma_start(xin[:, par, :, :], x_g[2 * i + par]).then_inc(loaded_x[par], 16)
                        sp.dma_start(cin[:, par, :, :], c_g[2 * i + par]).then_inc(loaded_x[par], 16)
                sp.wait_ge(loaded_res, 16)

            @block.gpsimd
            def _(pool):
                st.clear_retired(pool)
                nc.gpsimd.memset(core.ones[:, :], 1.0).then_inc(consts, 1)
                nc.gpsimd.memset(core.zeros[:, :], 0.0).then_inc(consts, 1)
                nc.gpsimd.memset(core.pow_half[:, :], -0.5).then_inc(consts, 1)
                pool.wait_ge(consts, 3)
                nc.gpsimd.affine_select(out=core.ident[:, :], in_=core.zeros[:, 0:128], compare_op=ALU.not_equal, fill=1.0,
                                        base=0, pattern=[[-1, 128]], channel_multiplier=1).then_inc(ident_ready, 1)
                nc.gpsimd.affine_select(out=core.head_mask[:, :], in_=core.ones[:, 0:H], compare_op=ALU.is_ge, fill=0.0,
                                        base=0, pattern=[[-D8, H]], channel_multiplier=1).then_inc(zeroed, 1)
                pool.wait_ge(zeroed, 1)
                nc.gpsimd.affine_select(out=core.head_mask[:, :], in_=core.head_mask[:, :], compare_op=ALU.is_ge, fill=0.0,
                                        base=D8 - 1, pattern=[[D8, H]], channel_multiplier=-1).then_inc(zeroed, 1)

            @block.tensor
            def _(pe):
                pe.wait_ge(ident_ready, 1)
                pe.wait_ge(loaded_w, 16 * 8)
                for k in range(8):
                    nc.tensor.transpose(core.psum[:, 4 + k // 4, (k % 4) * 128:(k % 4 + 1) * 128], wn[:, k, :], core.ident[:, :]).then_inc(w_ready, 1)
                with pe.Fori(0, NG // 2) as i:
                    for par in range(2):
                        pe.wait_ge(loaded_x[par], 32 * i + 32)
                        pe.wait_ge(xT_done, 2 * i + par + 1)
                        for j in range(GB):
                            last = nc.tensor.transpose(core.psum[:, 0, j * T:(j + 1) * T], xin[:, par, j, :], core.ident[:, :])
                        last.then_inc(tr_ready, 1)
                        pe.wait_ge(cT_done, 2 * i + par + 1)
                        for j in range(GB):
                            last = nc.tensor.transpose(core.psum[0:CC, 1, j * NCTX:(j + 1) * NCTX], cin[:, par, j, :],
                                                       core.ident[0:NCTX, 0:NCTX])
                        last.then_inc(tr_ready, 1)

            @block.scalar
            def _(act):
                act.sem_inc(xT_done, 1)
                with act.Fori(0, NG) as n:
                    act.wait_ge(tr_ready, 2 * n + 1)
                    nc.scalar.activation(core.xT[:, bass.ts(n, GB), :], core.psum[:, 0, :].rearrange("p (g t) -> p g t", g=GB),
                                         ACT.Identity).then_inc(xT_done, 1)

            @block.vector
            def _(dve):
                dve.sem_inc(cT_done, 1)
                dve.wait_ge(w_ready, 8)
                nc.vector.tensor_copy(core.wT[:, :, :], core.psum[:, 4:6, :].rearrange("p a (k n) -> p (a k) n", k=4)).then_inc(w_done, 1)
                with dve.Fori(0, NG) as n:
                    dve.wait_ge(tr_ready, 2 * n + 2)
                    nc.vector.tensor_copy(core.ctxT[:, bass.ts(n, GB), :],
                                          core.psum[0:CC, 1, 0:GB * NCTX].rearrange("p (g t) -> p g t", g=GB)).then_inc(cT_done, 1)


def build_gru(core):
    nc, inp = core.nc, core.inp
    with Stage(core, "gru") as st:
        h1 = st.sb("h1", [C, B, T])
        bias = st.sb("bias", [128, 4, 2])
        keep = st.sb("keep", [128, 2, 512])
        z = st.sb("z", [128, 2, 512])
        sg = st.sb("sg", [128, 2, 512])
        g = st.sb("g", [128, 2, 512])
        v = st.sb("v", [128, 2, 512])
        loaded, bias_ready = st.sem("loaded"), st.sem("bias_ready")
        passed = st.sem("passed")
        with nc.Block() as block:
            @block.sync
            def _(sp):
                st.clear_retired(sp)
                for l in range(2):
                    sp.dma_start(bias[:, 0, l:l + 1], col(inp['L0_attn_bz'][l])).then_inc(loaded, 16)
                    sp.dma_start(bias[:, 1, l:l + 1], col(inp['L0_attn_bh'][l])).then_inc(loaded, 16)

            for l, (src, dst) in enumerate([(core.xT, h1), (h1, core.branch)]):
                pre_ready, gates_ready, cand, value, scanned = (
                    st.sem(f"{n}{l}") for n in ("pre_ready", "gates_ready", "cand", "value", "scanned"))
                lay = [pre_ready, gates_ready, cand, value, scanned]
                gru_layer(core, block, l, src, dst, bias, keep, z, sg, g, v, loaded, bias_ready, *lay,
                          prev_scanned=prev if l else None)
                prev = scanned


def gru_layer(core, block, l, src, dst, bias, keep, z, sg, g, v, loaded, bias_ready, pre_ready, gates_ready, cand, value,
              scanned, prev_scanned):
    nc = core.nc
    groups = [(lambda i, par=par: 2 * i + par) for par in range(2)]

    @block.tensor
    def _(pe):
        if prev_scanned is not None:
            pe.wait_ge(prev_scanned, GB * (NG + 1) + 1)
        with pe.Fori(0, NG // 2) as i:
            for par in range(2):
                n = groups[par](i)
                pe.wait_ge(cand, n + 1)
                rhs = src[:, bass.ds(n * GB, GB), :]
                nc.tensor.matmul(core.bank(2 * par), core.wT[:, l, :], rhs, start=True, stop=True).then_inc(pre_ready, 1)
                nc.tensor.matmul(core.bank(2 * par + 1), core.wT[:, 2 + l, :], rhs, start=True, stop=True).then_inc(pre_ready, 1)

    @block.scalar
    def _(act):
        act.wait_ge(bias_ready, 2)
        with act.Fori(0, NG // 2) as i:
            for par in range(2):
                n = groups[par](i)
                act.wait_ge(pre_ready, 2 * n + 1)
                act.wait_ge(value, n + 1)
                nc.scalar.activation(z[:, par, :], core.bank(2 * par), ACT.Sigmoid, bias=bias[:, 0, l:l + 1]).then_inc(gates_ready, 1)
                act.wait_ge(scanned, GB * n + 1)
                nc.scalar.activation(keep[:, par, :], core.bank(2 * par), ACT.Sigmoid, bias=bias[:, 2, l:l + 1],
                                     scale=-1.0).then_inc(gates_ready, 1)
                act.wait_ge(pre_ready, 2 * n + 2)
                nc.scalar.activation(sg[:, par, :], core.bank(2 * par + 1), ACT.Sigmoid, bias=bias[:, 1, l:l + 1]).then_inc(gates_ready, 1)

    @block.vector
    def _(dve):
        if l == 0:
            dve.wait_ge(loaded, 64)
            nc.vector.tensor_scalar(bias[:, 2, :], bias[:, 0, :], -1.0, None, ALU.mult).then_inc(bias_ready, 1)
            nc.vector.tensor_scalar(bias[:, 3, :], bias[:, 1, :], 0.5, None, ALU.add).then_inc(bias_ready, 1)
            dve.wait_ge(bias_ready, 2)
        dve.sem_inc(cand, 2)
        dve.sem_inc(value, 2)
        dve.sem_inc(scanned, GB + 1)
        with dve.Fori(0, NG // 2) as i:
            for par in range(2):
                n = groups[par](i)
                dve.wait_ge(gates_ready, 3 * n + 3)
                nc.vector.scalar_tensor_tensor(out=g[:, par, :], in0=core.bank(2 * par + 1), scalar=bias[:, 3, l:l + 1],
                                               in1=sg[:, par, :], op0=ALU.add, op1=ALU.max).then_inc(cand, 1)
                dve.wait_ge(cand, n + 3)
                nc.vector.tensor_tensor(v[:, par, :], g[:, par, :], z[:, par, :], ALU.mult).then_inc(value, 1)
                dve.wait_ge(value, n + 3)
                for j in range(GB):
                    nc.vector.tensor_tensor_scan(dst[:, n * GB + j, :], keep[:, par, j * T:(j + 1) * T],
                                                 v[:, par, j * T:(j + 1) * T], 0.5, ALU.mult, ALU.add).then_inc(scanned, 1)


def build_close(core, name, wo=None, v_bias=None, v_bias_by_batch=None, out_bias=None, turned=False, nan_guard=None, last=False):
    nc, inp = core.nc, core.inp
    with_pe = turned or wo is not None
    with Stage(core, name) as st:
        cur = st.sb("cur", [128, 2, GB, 128])
        oT = st.sb("oT", [128, 2, GB, 128])
        z = st.sb("z", [128, 2, GB, C])
        xn = st.sb("xn", [128, 2, GB, C])
        stats = st.sb("stats", [128, GB, 6])
        mv = st.sb("mv", [128, 2, GB, 2])
        rstd = st.sb("rstd", [128, 2, GB])
        ve = st.sb("ve", [128, 2, GB])
        w_o = st.sb("w_o", [128, 128])
        b_v = st.sb("b_v", [128, 1])
        b_o = st.sb("b_o", [128, 128])
        loaded = st.sem("loaded")
        cur_ready, turned_ready, oT_done, y_ready, summed = (st.sem(n) for n in ("cur_ready", "turned_ready", "oT_done", "y_ready", "summed"))
        stat_step, ve_done, rstd_done, normed, xT_ready, xT_done = (
            st.sem(n) for n in ("stat_step", "ve_done", "rstd_done", "normed", "xT_ready", "xT_done"))
        stored = [st.sem("stored0"), st.sem("stored1")]
        x_copied, bo_added = st.sem("x_copied"), st.sem("bo_added")
        guard_step, guard_mm, mean_copied, oT_final = (st.sem(n) for n in ("guard_step", "guard_mm", "mean_copied", "oT_final"))
        if nan_guard:
            recip_all, w_v = nan_guard
            wv = st.sb("wv", [CC, C])
            csum = st.sb("csum", [CC, B])
            vmean = st.sb("vmean", [C, B])
            mean4 = st.sb("mean4", [C, 2, GB])
            rsum = st.sb("rsum", [T, 2])
            mask = st.sb("mask", [T, 1], U32)
            isnan = st.sb("isnan", [T, 1])
        n_load = (wo is not None) + (v_bias is not None) + (out_bias is not None) + (nan_guard is not None)
        Y = 4
        y_bank = (lambda par: 0 + par) if turned else (lambda par: 2 + par)

        passed = st.sem("passed")
        with nc.Block() as block:
            @block.sync
            def _(sp):
                if wo is not None:
                    sp.dma_start(w_o[:, :], wo).then_inc(loaded, 16)
                if v_bias is not None:
                    sp.dma_start(b_v[:, :], col(v_bias)).then_inc(loaded, 16)
                if nan_guard:
                    sp.dma_start(wv[:, :], w_v).then_inc(loaded, 16)
                if out_bias is not None:
                    sp.dma_start(b_o[:, :], row(out_bias).broadcast_to([128, 128])).then_inc(loaded, 16)
                if last:
                    with sp.Fori(0, NG // 2) as i:
                        for par in range(2):
                            n = 2 * i + par
                            sp.wait_ge(normed, GB * (n + 2))
                            sp.dma_start(core.out.rearrange("(n g) t c -> n t g c", g=GB)[n], xn[:, par, :, :]).then_inc(stored[par], 16)
                    for par in range(2):
                        sp.wait_ge(stored[par], 16 * (NG // 2))

            @block.gpsimd
            def _(pool):
                st.clear_retired(pool)
                if out_bias is not None:
                    pool.wait_ge(loaded, 16 * n_load)

                def add_out_bias(n):
                    if out_bias is not None:
                        xs = core.x[:, bass.ds(n * GB, GB), :]
                        nc.gpsimd.tensor_tensor(xs, xs, b_o[:, :].rearrange("p (a c) -> p a c", a=1).broadcast_to([128, GB, C]),
                                                ALU.add).then_inc(bo_added, 1)

                def rsqrt(n, par):
                    pool.wait_ge(ve_done, n + 1)
                    nc.gpsimd.tensor_tensor(rstd[:, par, :], ve[:, par, :], core.pow_half[:, :], ALU.pow).then_inc(rstd_done, 1)

                def pair(i, last_pair):
                    for par in range(2):
                        n = 2 * i + par
                        if not (last_pair and par == 1):
                            add_out_bias(n + 1)
                        rsqrt(n, par)

                add_out_bias(0)
                with pool.Fori(0, NG // 2 - 1) as i:
                    pair(i, False)
                pair(NG // 2 - 1, True)

            @block.tensor
            def _(pe):
                if wo is not None:
                    pe.wait_ge(loaded, 16 * n_load)
                pe.sem_inc(turned_ready, 2)

                def turn_x(n, par):
                    pe.wait_ge(normed, GB * (n + 2))
                    pe.wait_ge(xT_done, n)
                    for j in range(GB):
                        mm = nc.tensor.transpose(core.psum[:, 4 + par, j * T:(j + 1) * T], xn[:, par, j, :], core.ident[:, :])
                    mm.then_inc(xT_ready, 1)

                def front(n, par):
                    if not with_pe:
                        return
                    pe.wait_ge(cur_ready, n + 1)
                    if turned:
                        pe.wait_ge(summed, n)
                    else:
                        pe.wait_ge(oT_done, n)
                    for j in range(GB):
                        mm = nc.tensor.transpose(core.psum[:, par, j * T:(j + 1) * T], cur[:, par, j, :], core.ident[:, :])
                    mm.then_inc(turned_ready, 1)
                    if wo is not None:
                        if nan_guard:
                            pe.wait_ge(oT_final, n + 1)
                        else:
                            pe.wait_ge(oT_done, n + 2)
                        pe.wait_ge(summed, n)
                        for j in range(GB):
                            mm = nc.tensor.matmul(core.psum[:, 2 + par, j * C:(j + 1) * C], oT[:, par, j, :], w_o[:, :], start=True, stop=True)
                        mm.then_inc(y_ready, 1)

                def pair(i, first):
                    for par in range(2):
                        n = 2 * i + par
                        front(n, par)
                        if not last and not (first and par == 0):
                            turn_x(n - 1, 1 - par)

                if nan_guard:
                    pe.wait_ge(guard_step, 1)
                    nc.tensor.matmul(core.psum[:, 6, 0:1], core.ones[:, :], rsum[:, 0:1], start=True, stop=True).then_inc(guard_mm, 1)
                    pe.wait_ge(guard_step, 2)
                    nc.tensor.matmul(core.psum[:, 7, 0:B], wv[:, :], csum[:, :], start=True, stop=True).then_inc(guard_mm, 1)
                pair(0, True)
                with pe.Fori(1, NG // 2) as i:
                    pair(i, False)
                if not last:
                    turn_x(NG - 1, (NG - 1) % 2)

            @block.scalar
            def _(act):
                act.sem_inc(oT_done, 1)
                act.sem_inc(xT_done, 1)

                def copy_cur(n, par):
                    act.wait_ge(turned_ready, n + 1)
                    nc.scalar.activation(cur[:, par, :, :], core.branch[:, bass.ds(n * GB, GB), :], ACT.Identity).then_inc(cur_ready, 1)

                def copy_oT(n, par):
                    act.wait_ge(turned_ready, n + 3)
                    src = core.psum[:, par, :].rearrange("p (g t) -> p g t", g=GB)
                    if v_bias is not None:
                        ins = nc.scalar.activation(oT[:, par, :, :], src, ACT.Identity, bias=b_v[:, :])
                        ins.then_inc(oT_done, 1)
                    elif v_bias_by_batch is not None:
                        for j in range(GB):
                            ins = nc.scalar.activation(oT[:, par, j, :], src[:, j, :], ACT.Identity,
                                                       bias=v_bias_by_batch[:, bass.ds(n * GB + j, 1)])
                        ins.then_inc(oT_done, 1)
                    else:
                        nc.scalar.activation(oT[:, par, :, :], src, ACT.Identity).then_inc(oT_done, 1)

                def copy_xT(n, par):
                    act.wait_ge(xT_ready, n + 1)
                    nc.scalar.activation(core.xT[:, bass.ds(n * GB, GB), :],
                                         core.psum[:, 4 + par, :].rearrange("p (g t) -> p g t", g=GB), ACT.Identity).then_inc(xT_done, 1)

                if v_bias is not None:
                    act.wait_ge(loaded, 16 * n_load)

                def pair(i, first, last_pair):
                    for par in range(2):
                        n = 2 * i + par
                        if with_pe and not (last_pair and par == 1):
                            copy_cur(n + 1, 1 - par)
                        if wo is not None:
                            copy_oT(n, par)
                        if not last and not (first and par == 0):
                            copy_xT(n - 1, 1 - par)

                if with_pe:
                    copy_cur(0, 0)
                pair(0, True, False)
                with act.Fori(1, NG // 2 - 1) as i:
                    pair(i, False, False)
                pair(NG // 2 - 1, False, True)
                if not last:
                    copy_xT(NG - 1, (NG - 1) % 2)

            @block.vector
            def _(dve):
                dve.sem_inc(summed, 1)
                dve.sem_inc(normed, GB)
                if nan_guard:
                    nc.vector.tensor_reduce(rsum[:, 0:1], recip_all[:, :, :].rearrange("p b h -> p (b h)"), X_AXIS, ALU.add).then_inc(guard_step, 1)
                    nc.vector.tensor_reduce(csum[:, :], core.ctxT[:, :, :], X_AXIS, ALU.add).then_inc(guard_step, 1)
                    dve.wait_ge(guard_mm, 1)
                    nc.vector.tensor_copy(rsum[:, 1:2], core.psum[:, 6, 0:1]).then_inc(guard_step, 1)
                    dve.wait_ge(guard_step, 3)
                    nc.vector.tensor_tensor(isnan[:, :], rsum[:, 1:2], rsum[:, 1:2], ALU.not_equal).then_inc(guard_step, 1)
                    dve.wait_ge(guard_step, 4)
                    nc.vector.tensor_copy(mask[:, :], isnan[:, :]).then_inc(guard_step, 1)
                    dve.wait_ge(guard_mm, 2)
                    dve.wait_ge(loaded, 16 * n_load)
                    nc.vector.tensor_scalar(vmean[:, :], core.psum[:, 7, 0:B], 1.0 / NCTX, b_v[:, :], ALU.mult, ALU.add).then_inc(guard_step, 1)
                    dve.wait_ge(guard_step, 6)

                def blend(n, par):
                    nc.vector.tensor_copy(mean4[:, par, :], vmean[:, bass.ds(n * GB, GB)]).then_inc(mean_copied, 1)
                    dve.wait_ge(mean_copied, n + 1)
                    dve.wait_ge(oT_done, n + 2)
                    stand_alone(dve, passed)
                    nc.vector.copy_predicated(oT[:, par, :, :], mask[:, :].rearrange("p (a b) -> p a b", a=1).broadcast_to([C, GB, T]),
                                              mean4[:, par, :].rearrange("p (g a) -> p g a", a=1).broadcast_to([C, GB, T])).then_inc(oT_final, 1)

                def add_up(n, par):
                    xs = core.x[:, bass.ds(n * GB, GB), :]
                    if out_bias is not None:
                        dve.wait_ge(bo_added, n + 1)
                    if turned:
                        dve.wait_ge(turned_ready, n + 3)
                        y = core.psum[:, par, :].rearrange("p (g c) -> p g c", g=GB)
                    elif wo is not None:
                        if nan_guard:
                            blend(n, par)
                        dve.wait_ge(y_ready, n + 1)
                        y = core.psum[:, 2 + par, :].rearrange("p (g c) -> p g c", g=GB)
                    else:
                        y = core.branch[:, bass.ds(n * GB, GB), :]
                    nc.vector.tensor_tensor(z[:, par, :, :], y, xs, ALU.add).then_inc(summed, 1)
                    dve.wait_ge(summed, n + 2)
                    for j in range(GB):
                        nc.vector.bn_stats(stats[:, j, :], z[:, par, j, :]).then_inc(stat_step, 1)
                    dve.wait_ge(stat_step, 8 * n + 4)
                    stand_alone(dve, passed)
                    for j in range(GB):
                        nc.vector.bn_aggr(mv[:, par, j, :], stats[:, j, :]).then_inc(stat_step, 1)
                    dve.wait_ge(stat_step, 8 * n + 8)
                    nc.vector.tensor_scalar(ve[:, par, :], mv[:, par, :, 1], EPS, None, ALU.add).then_inc(ve_done, 1)

                def norm(n, par, earlier):
                    dve.wait_ge(rstd_done, n + 1)
                    if last and not (isinstance(earlier, int) and earlier == 0):
                        dve.wait_ge(stored[par], 16 * earlier)
                    if not last and not (isinstance(n, int) and n < 2):
                        dve.wait_ge(xT_ready, n - 1)
                    for j in range(GB):
                        nc.vector.tensor_scalar(xn[:, par, j, :], z[:, par, j, :], mv[:, par, j, 0:1], rstd[:, par, j:j + 1],
                                                ALU.subtract, ALU.mult).then_inc(normed, 1)
                    dve.wait_ge(normed, GB * (n + 2))
                    if not last:
                        stand_alone(dve, passed)
                        nc.vector.tensor_copy(core.x[:, bass.ds(n * GB, GB), :], xn[:, par, :, :]).then_inc(x_copied, 1)

                def pair(i, first):
                    for par in range(2):
                        n = 2 * i + par
                        add_up(n, par)
                        if not (first and par == 0):
                            norm(n - 1, 1 - par, i - (1 - par))

                pair(0, True)
                with dve.Fori(1, NG // 2) as i:
                    pair(i, False)
                norm(NG - 1, 1, NG // 2 - 1)


def build_attention8(core, name, nk, w_q, w_k, w_v, cross=False, b_q=None, b_k=None, transposed=None, causal=False,
                     clip=False, guard=False, mixed=None, recip_all=None):
    nc, inp = core.nc, core.inp
    scale = float(D8) ** -0.5
    ck = CC if cross else C
    S_BANK, T_BANK, OT_BANK, O_BANK, QK_BANK, V_BANK = 0, 2, 4, 5, 6, 7
    Q_AT, K_AT = slice(0, T), slice(T, T + nk)
    PAD = 32
    COPY_LAG = 2
    TURN_LAG, WEIGH_LAG = 3, 4
    with Stage(core, name) as st:
        xc = st.sb("xc", [C, 2, T])
        cc = st.sb("cc", [CC, 2, NCTX])
        qT = st.sb("qT", [C, 2, T])
        kT = st.sb("kT", [C, 2, nk])
        keys_q = st.sb("keys_q", [C, 2, H, nk])
        va = st.sb("va", [nk, 2, H, PAD])
        sc = st.sb("sc", [T, NU, QUAD, nk])
        clipped = st.sb("clipped", [T, 2, QUAD, nk])
        pT = st.sb("pT", [nk, 2, QUAD, T])
        negmax = st.sb("negmax", [T, NU, QUAD])
        oT = st.sb("oT", [QUAD * PAD, 2, NU, T])
        den = st.sb("den", [T, 2, H])
        rden = st.sb("rden", [T, 2, H])
        wq, wk, wv = (st.sb(n, [128, C]) for n in ("wq", "wk", "wv"))
        bq, bk = st.sb("bq", [C, 1]), st.sb("bk", [C, 1])
        wmix = st.sb("wmix", [C, 2, 3, C]) if mixed else None
        weighted = st.sb("weighted", [C, 4, 3 * C]) if mixed else None
        gate_b = st.sb("gate_b", [C, 2, 4]) if mixed else None
        future = st.sb("future", [T, T], BF16) if causal else None
        identb = st.sb("identb", [T, T], BF16) if causal else None
        loaded, consts, src_ready, qk_projected, v_projected = (
            st.sem(n) for n in ("loaded", "consts", "src_ready", "qk_projected", "v_projected"))
        q_done, k_done, v_done, gate_step, mix_step, k_copied = (st.sem(n) for n in ("q_done", "k_done", "v_done", "gate_step", "mix_step", "k_copied"))
        scored, clip_step, max_step, shifted, p_ready, turned, pT_ready, weighed, oT_done, o_ready, norm_step, o_done = (st.sem(n) for n in (
            "scored", "clip_step", "max_step", "shifted", "p_ready", "turned", "pT_ready", "weighed", "oT_done", "o_ready",
            "norm_step", "o_done"))
        biased = b_q is not None
        n_load = 0
        weights = []
        if mixed is None and transposed is None:
            weights = [(wq[:, :], w_q), (wk[0:ck, :], w_k), (wv[0:ck, :], w_v)]
        if biased:
            weights += [(bq[:, :], col(b_q)), (bk[:, :], col(b_k))]
        n_load = len(weights)
        NORM = 1 + guard + (recip_all is not None)

        passed = st.sem("passed")
        with nc.Block() as block:
            @block.sync
            def _(sp):
                for dst, src in weights:
                    sp.dma_start(dst, src).then_inc(loaded, 16)
                if n_load:
                    sp.wait_ge(loaded, 16 * n_load)

            @block.gpsimd
            def _(pool):
                st.clear_retired(pool)
                nc.gpsimd.memset(va[:, :, :, :], 0.0).then_inc(consts, 1)
                pool.wait_ge(consts, 1)
                nc.gpsimd.memset(va[:, :, :, D8:D8 + 1], 1.0).then_inc(consts, 1)
                if causal:
                    nc.gpsimd.tensor_copy(identb[:, :], core.ident[:, :]).then_inc(consts, 1)
                    nc.gpsimd.affine_select(out=future[:, :], in_=core.zeros[:, 0:T], compare_op=ALU.is_ge, fill=NEG, base=0,
                                            pattern=[[-1, T]], channel_multiplier=1).then_inc(consts, 1)

                def mix(b, par):
                    gate, _, experts = mixed
                    nc.gpsimd.tensor_copy(gate_b[:, par, :], gate[:, bass.ds(4 * b, 4)]).then_inc(gate_step, 1)
                    pool.wait_ge(gate_step, b + 1)
                    nc.gpsimd.tensor_tensor(weighted[:, :, :], experts[:, :, :],
                                            gate_b[:, par, :].rearrange("p (e a) -> p e a", a=1).broadcast_to([C, 4, 3 * C]),
                                            ALU.mult).then_inc(mix_step, 1)
                    pool.wait_ge(mix_step, 3 * b + 1)
                    nc.gpsimd.tensor_tensor(weighted[:, 0:2, :], weighted[:, 0:2, :], weighted[:, 2:4, :], ALU.add).then_inc(mix_step, 1)
                    pool.wait_ge(mix_step, 3 * b + 2)
                    nc.gpsimd.tensor_tensor(wmix[:, par, :, :].rearrange("p k n -> p (k n)"), weighted[:, 0, :], weighted[:, 1, :],
                                            ALU.add).then_inc(mix_step, 1)

                with pool.Fori(0, B // 2) as i:
                    for par in range(2):
                        b = 2 * i + par
                        pool.wait_ge(v_projected, b + 1)
                        nc.gpsimd.tensor_copy(xc[:, par, :], core.xT[:, b, :]).then_inc(src_ready, 1)
                        if cross:
                            nc.gpsimd.tensor_copy(cc[:, par, :], core.ctxT[:, b, :]).then_inc(src_ready, 1)
                        if mixed is not None:
                            mix(b, par)

            @block.tensor
            def _(pe):
                pe.sem_inc(v_projected, 2)
                if n_load:
                    pe.wait_ge(loaded, 16 * n_load)
                pe.wait_ge(consts, 4 if causal else 2)

                def projection(k, par):
                    if mixed is not None:
                        return wmix[:, par, k, :]
                    if transposed is not None:
                        return core.wT[:, transposed[k], :]
                    return (wq[:, :], wk[0:ck, :], wv[0:ck, :])[k]

                def project_qk(b, par):
                    pe.wait_ge(src_ready, (2 if cross else 1) * (b + 1))
                    if mixed is not None:
                        pe.wait_ge(mix_step, 3 * b + 3)
                    kv = cc[:, par, :] if cross else xc[:, par, :]
                    pe.wait_ge(q_done, b)
                    pe.wait_ge(k_copied, b)
                    nc.tensor.matmul(core.psum[:, QK_BANK, Q_AT], projection(0, par), xc[:, par, :], start=True, stop=True)
                    nc.tensor.matmul(core.psum[:, QK_BANK, K_AT], projection(1, par), kv, start=True, stop=True).then_inc(qk_projected, 1)

                def project_v(b, par):
                    pe.wait_ge(v_done, b)
                    nc.tensor.matmul(core.psum[0:nk, V_BANK, 0:C], cc[:, par, :] if cross else xc[:, par, :], projection(2, par),
                                     start=True, stop=True).then_inc(v_projected, 1)

                def score(b, par, g):
                    u = NU * b + g
                    if g == 0:
                        pe.wait_ge(q_done, b + 1)
                    pe.wait_ge(k_done, u + 1)
                    pe.wait_ge(clip_step if clip else shifted, u)
                    out = core.psum[:, S_BANK + g % 2, 0:QUAD * nk]
                    mm = nc.tensor.matmul(out, qT[:, par, :], keys_q[:, par, QUAD * g:QUAD * g + QUAD, :], start=True, stop=not causal)
                    if causal:
                        for j in range(QUAD):
                            mm = nc.tensor.matmul(out[:, j * nk:(j + 1) * nk], identb[:, :], future[:, :], start=False, stop=(j == QUAD - 1))
                    mm.then_inc(scored, 1)

                def turn(b, g):
                    u = NU * b + g
                    pe.wait_ge(p_ready, u + 1)
                    pe.wait_ge(pT_ready, u)
                    for j in range(QUAD):
                        mm = nc.tensor.transpose(core.psum[0:nk, T_BANK + g % 2, j * T:(j + 1) * T], sc[:, g, j, :], core.ident[:, :])
                    mm.then_inc(turned, 1)

                def weigh(b, par, g):
                    u = NU * b + g
                    if g == 0:
                        pe.wait_ge(v_done, b + 1)
                        pe.wait_ge(oT_done, b)
                    pe.wait_ge(pT_ready, u + 2)
                    for j in range(QUAD):
                        rows = slice(PAD * j, PAD * j + PAD)
                        mm = nc.tensor.matmul(core.psum[rows, OT_BANK, g * T:(g + 1) * T], va[:, par, QUAD * g + j, :], pT[:, g % 2, j, :],
                                              start=True, stop=True, tile_position=(0, PAD * j))
                    if g == NU - 1:
                        mm.then_inc(weighed, 1)

                def turn_back(b, par):
                    pe.wait_ge(oT_done, b + 1)
                    pe.wait_ge(o_done, b + 1)
                    for g in range(NU):
                        mm = nc.tensor.transpose(core.psum[:, O_BANK, g * T:(g + 1) * T], oT[:, par, g, :], core.ident[:, :])
                    mm.then_inc(o_ready, 1)

                def before(b, par, g, back):
                    k = g - back
                    return (b, par, k) if k >= 0 else (b - 1, 1 - par, k + NU)

                def pair(i, first, last):
                    for par in range(2):
                        b = 2 * i + par
                        for g in range(NU):
                            score(b, par, g)
                            if g == 0 and not (last and par == 1):
                                project_qk(b + 1, 1 - par)
                            if not (first and par == 0 and g < TURN_LAG):
                                bb, _, gg = before(b, par, g, TURN_LAG)
                                turn(bb, gg)
                            if not (first and par == 0 and g < WEIGH_LAG):
                                weigh(*before(b, par, g, WEIGH_LAG))
                            if g == 0 and not first:
                                turn_back(b - 2, par)
                            if g == 2 and not (last and par == 1):
                                project_v(b + 1, 1 - par)

                project_qk(0, 0)
                project_v(0, 0)
                pair(0, True, False)
                with pe.Fori(1, B // 2 - 1) as i:
                    pair(i, False, False)
                pair(B // 2 - 1, False, True)
                for over in range(WEIGH_LAG):
                    if over < TURN_LAG:
                        turn(B - 1, NU - TURN_LAG + over)
                    weigh(B - 1, 1, NU - WEIGH_LAG + over)
                    if over == 0:
                        turn_back(B - 2, 0)
                turn_back(B - 1, 1)

            @block.scalar
            def _(act):
                act.sem_inc(pT_ready, 1)
                if n_load:
                    act.wait_ge(loaded, 16 * n_load)
                act.wait_ge(consts, 4 if causal else 2)

                def copy_qk(b, par):
                    act.wait_ge(qk_projected, b + 1)
                    q_bias = bq[:, :] if biased else (mixed[1][:, 0, bass.ds(b, 1)] if mixed else 0.0)
                    nc.scalar.activation(qT[:, par, :], core.psum[:, QK_BANK, Q_AT], ACT.Identity, bias=q_bias).then_inc(q_done, 1)
                    k_bias = bk[:, :] if biased else (mixed[1][:, 1, bass.ds(b, 1)] if mixed else 0.0)
                    nc.scalar.activation(kT[:, par, :], core.psum[:, QK_BANK, K_AT], ACT.Identity, bias=k_bias).then_inc(k_copied, 1)

                def copy_v(b, par, fresh=False):
                    act.wait_ge(v_projected, b + 3)
                    if not fresh:
                        act.wait_ge(weighed, b - 1)
                    nc.scalar.activation(va[:, par, :, 0:D8], core.psum[0:nk, V_BANK, 0:C].rearrange("p (h d) -> p h d", h=H),
                                         ACT.Identity).then_inc(v_done, 1)

                def copy_oT(b, par):
                    act.wait_ge(weighed, b + 1)
                    nc.scalar.activation(oT[:, par, :, :], core.psum[:, OT_BANK, :].rearrange("p (u t) -> p u t", u=NU),
                                         ACT.Identity).then_inc(oT_done, 1)

                def exponential(u, g):
                    act.wait_ge(shifted, u + 2)
                    nc.scalar.activation(sc[:, g, :, :], sc[:, g, :, :], ACT.Exp, scale=scale).then_inc(p_ready, 1)

                def copy_pT(u, g):
                    act.wait_ge(turned, u + 1)
                    nc.scalar.activation(pT[:, g % 2, :, :], core.psum[0:nk, T_BANK + g % 2, :].rearrange("p (j t) -> p j t", j=QUAD),
                                         ACT.Identity).then_inc(pT_ready, 1)

                def pair(i, first, last):
                    for par in range(2):
                        b = 2 * i + par
                        for g in range(NU):
                            if g == 0 and not (last and par == 1):
                                copy_qk(b + 1, 1 - par)
                            exponential(NU * b + g, g)
                            if g == 2 and not (first and par == 0):
                                copy_oT(b - 1, 1 - par)
                            if not (first and par == 0 and g < COPY_LAG):
                                copy_pT(NU * b + g - COPY_LAG, (g - COPY_LAG) % 2)
                            if g == 3 and not (last and par == 1):
                                copy_v(b + 1, 1 - par, first and par == 0)

                copy_qk(0, 0)
                copy_v(0, 0, True)
                pair(0, True, False)
                with act.Fori(1, B // 2 - 1) as i:
                    pair(i, False, False)
                pair(B // 2 - 1, False, True)
                for back in range(COPY_LAG, 0, -1):
                    copy_pT(NU * B - back, back % 2)
                copy_oT(B - 1, 1)

            @block.vector
            def _(dve):
                dve.sem_inc(shifted, 1)
                dve.sem_inc(clip_step, 1)
                dve.sem_inc(o_done, 1)
                if n_load:
                    dve.wait_ge(loaded, 16 * n_load)

                def spread_keys(b, par, g):
                    if g == 0:
                        dve.wait_ge(k_copied, b + 1)
                    heads = slice(QUAD * g, QUAD * g + QUAD)
                    k_in = kT[:, par, :].rearrange("p (a n) -> p a n", a=1).broadcast_to([C, QUAD, nk])
                    mask = core.head_mask[:, heads].rearrange("p (h a) -> p h a", a=1).broadcast_to([C, QUAD, nk])
                    nc.vector.tensor_tensor(keys_q[:, par, heads, :], k_in, mask, ALU.mult).then_inc(k_done, 1)

                def scores(g):
                    return core.psum[:, S_BANK + g % 2, 0:QUAD * nk].rearrange("p (j n) -> p j n", j=QUAD)

                def clamp(u, g, fresh=False):
                    dve.wait_ge(scored, u + 1)
                    if not fresh:
                        dve.wait_ge(shifted, u)
                    nc.vector.tensor_scalar(clipped[:, g % 2, :, :], scores(g), CLAMP / scale, -CLAMP / scale, ALU.min, ALU.max).then_inc(clip_step, 1)

                def maximum(u, g):
                    if clip:
                        dve.wait_ge(clip_step, u + 2)
                    else:
                        dve.wait_ge(scored, u + 1)
                    nc.vector.tensor_reduce(negmax[:, g, :], clipped[:, g % 2, :, :] if clip else scores(g), X_AXIS, ALU.max,
                                            negate=True).then_inc(max_step, 1)

                def shift(u, g, fresh):
                    dve.wait_ge(max_step, u + 1)
                    if not fresh:
                        dve.wait_ge(turned, u - NU + 1)
                    nm = negmax[:, g, :].rearrange("p (q a) -> p q a", a=1).broadcast_to([T, QUAD, nk])
                    nc.vector.tensor_tensor(sc[:, g, :, :], clipped[:, g % 2, :, :] if clip else scores(g), nm, ALU.add).then_inc(shifted, 1)

                def norm(b, par):
                    k = NORM * b
                    dve.wait_ge(o_ready, b + 1)
                    o = core.psum[:, O_BANK, :].rearrange("p (h d) -> p h d", h=H)
                    rd = rden[:, par, :]
                    if guard:
                        nc.vector.tensor_scalar(den[:, par, :], o[:, :, D8], 1e-12, None, ALU.max).then_inc(norm_step, 1)
                        dve.wait_ge(norm_step, k + 1)
                        k = k + 1
                        nc.vector.reciprocal(rd, den[:, par, :]).then_inc(norm_step, 1)
                    else:
                        nc.vector.reciprocal(rd, o[:, :, D8]).then_inc(norm_step, 1)
                    dve.wait_ge(norm_step, k + 1)
                    out = core.branch[:, b, :].rearrange("p (h d) -> p h d", h=H)
                    nc.vector.tensor_tensor(out, o[:, :, 0:D8], rd.rearrange("p (h a) -> p h a", a=1).broadcast_to([T, H, D8]),
                                            ALU.mult).then_inc(o_done, 1)
                    if recip_all is not None:
                        nc.vector.tensor_copy(recip_all[:, b, :], rd).then_inc(norm_step, 1)

                def pair(i, first, last):
                    for par in range(2):
                        b = 2 * i + par
                        for g in range(NU):
                            u, ahead = NU * b + g, not (last and par == 1 and g == NU - 1)
                            maximum(u, g)
                            if clip and ahead:
                                clamp(u + 1, (g + 1) % NU, first and par == 0 and g == 0)
                            if not clip and not (last and par == 1):
                                spread_keys(b + 1, 1 - par, g)
                            shift(u, g, first and par == 0)
                            if clip and not (last and par == 1):
                                spread_keys(b + 1, 1 - par, g)
                            if g == 0 and not first:
                                norm(b - 2, par)

                for piece in range(NU):
                    spread_keys(0, 0, piece)
                if clip:
                    clamp(0, 0, True)
                pair(0, True, False)
                with dve.Fori(1, B // 2 - 1) as i:
                    pair(i, False, False)
                pair(B // 2 - 1, False, True)
                norm(B - 2, 0)
                norm(B - 1, 1)


def build_route(core, taken, slot_read, prob):
    nc, inp = core.nc, core.inp
    LOGITS, COUNTS, XE = 0, 2, 4
    with Stage(core, "route") as st:
        w_r = st.sb("w_r", [C, E16])
        xt = st.sb("xt", [C, 2, GB, T])
        xs = st.sb("xs", [T, 2, GB, C])
        iota16 = st.sb("iota16", [T, E16])
        iota256 = st.sb("iota256", [T, SLOTS])
        upto = st.sb("upto", [T, T], BF16)
        onesb = st.sb("onesb", [T, T], BF16)
        mx = st.sb("mx", [T, GB])
        lg = st.sb("lg", [T, 2, GB, E16])
        rs = st.sb("rs", [T, GB])
        rr = st.sb("rr", [T, GB])
        pr = st.sb("pr", [T, 2, GB, E16])
        top = st.sb("top", [T, GB, 8])
        idx = st.sb("idx", [T, GB, 8], U32)
        idf = st.sb("idf", [T, GB, 2])
        chosen = st.sb("chosen", [T, 2, GB, 2, E16], BF16)
        ranks = st.sb("ranks", [T, GB, 2, E16])
        pos = st.sb("pos", [T, GB, 2])
        capped = st.sb("capped", [T, GB, 2])
        first_slot = st.sb("first_slot", [T, GB, 2])
        over = st.sb("over", [T, GB, 2])
        slot_in = st.sb("slot_in", [T, GB, 2])
        d1 = st.sb("d1", [T, 2, SLOTS])
        disp = st.sb("disp", [T, 2, SLOTS])
        loaded, consts, src_ready, logit_ready, counted, xe_ready, xe_done = (st.sem(n) for n in (
            "loaded", "consts", "src_ready", "logit_ready", "counted", "xe_ready", "xe_done"))
        shifted, exp_done, step, chosen_done, half, disp_ready = (st.sem(n) for n in (
            "shifted", "exp_done", "step", "chosen_done", "half", "disp_ready"))
        passed = st.sem("passed")
        with nc.Block() as block:
            @block.sync
            def _(sp):
                sp.dma_start(w_r[:, :], inp['L0_ffn_w_router'][:, :]).then_inc(loaded, 16)
                sp.wait_ge(loaded, 16)

            @block.gpsimd
            def _(pool):
                st.clear_retired(pool)
                nc.gpsimd.iota(iota16[:, :], pattern=[[1, E16]], base=0, channel_multiplier=0, allow_small_or_imprecise_dtypes=True).then_inc(consts, 1)
                nc.gpsimd.iota(iota256[:, :], pattern=[[1, SLOTS]], base=0, channel_multiplier=0, allow_small_or_imprecise_dtypes=True).then_inc(consts, 1)
                nc.gpsimd.tensor_copy(onesb[:, :], core.ones[:, :]).then_inc(consts, 1)
                nc.gpsimd.affine_select(out=upto[:, :], in_=core.ones[:, 0:T], compare_op=ALU.is_ge, fill=0.0, base=0,
                                        pattern=[[1, T]], channel_multiplier=-1).then_inc(consts, 1)
                with pool.Fori(0, NG // 2) as i:
                    for par in range(2):
                        n = 2 * i + par
                        pool.wait_ge(xe_ready, GB * n + 1)
                        nc.gpsimd.tensor_copy(xt[:, par, :, :], core.xT[:, bass.ds(n * GB, GB), :]).then_inc(src_ready, 1)
                        nc.gpsimd.tensor_copy(xs[:, par, :, :], core.x[:, bass.ds(n * GB, GB), :]).then_inc(src_ready, 1)

            @block.tensor
            def _(pe):
                pe.wait_ge(loaded, 16)
                pe.wait_ge(consts, 4)
                pe.sem_inc(xe_ready, GB + 1)

                def logits(n, par):
                    pe.wait_ge(src_ready, 2 * n + 1)
                    pe.wait_ge(shifted, n)
                    for j in range(GB):
                        mm = nc.tensor.matmul(core.psum[:, LOGITS + par, j * E16:(j + 1) * E16], xt[:, par, j, :], w_r[:, :], start=True, stop=True)
                    mm.then_inc(logit_ready, 1)

                def dispatch(n, par):
                    pe.wait_ge(chosen_done, n + 1)
                    counts = core.psum[:, COUNTS + par, 0:GB * 2 * E16].rearrange("p (g k e) -> p g k e", g=GB, k=2)
                    nc.tensor.matmul(counts, upto[:, :], chosen[:, par, :, :, :], start=True, stop=False)
                    nc.tensor.matmul(counts[:, :, 1, :], onesb[:, :], chosen[:, par, :, 0, :], start=False, stop=True).then_inc(counted, 1)
                    pe.wait_ge(src_ready, 2 * n + 2)
                    for j in range(GB):
                        pe.wait_ge(disp_ready, GB * n + j + 1)
                        pe.wait_ge(xe_done, GB * n + j + 1)
                        nc.tensor.matmul(core.psum[:, XE + j % 2, 0:SLOTS], xs[:, par, j, :], disp[:, j % 2, :], start=True,
                                         stop=True).then_inc(xe_ready, 1)

                def pair(i, last):
                    for par in range(2):
                        n = 2 * i + par
                        if not (last and par == 1):
                            logits(n + 1, 1 - par)
                        dispatch(n, par)

                logits(0, 0)
                with pe.Fori(0, NG // 2 - 1) as i:
                    pair(i, False)
                pair(NG // 2 - 1, True)

            @block.scalar
            def _(act):
                act.sem_inc(xe_done, 2)
                with act.Fori(0, NG // 2) as i:
                    for par in range(2):
                        n = 2 * i + par
                        act.wait_ge(shifted, n + 2)
                        nc.scalar.activation(pr[:, par, :, :], lg[:, par, :, :], ACT.Exp).then_inc(exp_done, 1)
                        for j in range(GB):
                            act.wait_ge(xe_ready, GB * n + j + 2 + GB)
                            nc.scalar.activation(taken[:, :, bass.ds(n * GB + j, 1), :],
                                                 core.psum[:, XE + j % 2, 0:SLOTS].rearrange("p (e a s) -> p e a s", e=E16, a=1),
                                                 ACT.Identity).then_inc(xe_done, 1)

            @block.vector
            def _(dve):
                dve.wait_ge(consts, 4)
                dve.sem_inc(shifted, 1)
                K = 18
                with dve.Fori(0, NG // 2) as i:
                    for par in range(2):
                        n = 2 * i + par
                        s = K * n
                        wide = lambda t, w: t.rearrange("p (g a) -> p g a", a=1).broadcast_to([T, GB, w])
                        dve.wait_ge(logit_ready, n + 1)
                        lp = core.psum[:, LOGITS + par, 0:GB * E16].rearrange("p (g e) -> p g e", g=GB)
                        nc.vector.tensor_reduce(mx[:, :], lp, X_AXIS, ALU.max, negate=True).then_inc(step, 1)
                        dve.wait_ge(step, s + 1)
                        nc.vector.tensor_tensor(lg[:, par, :, :], lp, wide(mx[:, :], E16), ALU.add).then_inc(shifted, 1)
                        dve.wait_ge(exp_done, n + 1)
                        p = pr[:, par, :, :]
                        nc.vector.tensor_reduce(rs[:, :], p, X_AXIS, ALU.add).then_inc(step, 1)
                        dve.wait_ge(step, s + 2)
                        nc.vector.reciprocal(rr[:, :], rs[:, :]).then_inc(step, 1)
                        dve.wait_ge(step, s + 3)
                        nc.vector.tensor_tensor(p, p, wide(rr[:, :], E16), ALU.mult).then_inc(step, 1)
                        dve.wait_ge(step, s + 4)
                        stand_alone(dve, passed)
                        for j in range(GB):
                            nc.vector.max(top[:, j, :], pr[:, par, j, :]).then_inc(step, 1)
                        dve.wait_ge(step, s + 8)
                        stand_alone(dve, passed)
                        for j in range(GB):
                            nc.vector.max_index(idx[:, j, :], top[:, j, :], pr[:, par, j, :]).then_inc(step, 1)
                        nc.vector.tensor_copy(prob[:, bass.ds(n * GB, GB), :], top[:, :, 0:2]).then_inc(step, 1)
                        dve.wait_ge(step, s + 13)
                        nc.vector.tensor_copy(idf[:, :, :], idx[:, :, 0:2]).then_inc(step, 1)
                        dve.wait_ge(step, s + 14)
                        e_of = idf[:, :, :].rearrange("p g k -> p (g k)")
                        flat = lambda t: t.rearrange("p g k -> p (g k)")
                        nc.vector.tensor_tensor(chosen[:, par, :, :, :].rearrange("p g k e -> p (g k) e"),
                                                iota16[:, :].rearrange("p (a e) -> p a e", a=1).broadcast_to([T, 2 * GB, E16]),
                                                e_of.rearrange("p (q a) -> p q a", a=1).broadcast_to([T, 2 * GB, E16]),
                                                ALU.is_equal).then_inc(chosen_done, 1)
                        dve.wait_ge(chosen_done, n + 1)
                        dve.wait_ge(counted, n + 1)
                        nc.vector.tensor_tensor(ranks[:, :, :, :].rearrange("p g k e -> p (g k) e"),
                                                core.psum[:, COUNTS + par, 0:GB * 2 * E16].rearrange("p (q e) -> p q e", e=E16),
                                                chosen[:, par, :, :, :].rearrange("p g k e -> p (g k) e"), ALU.mult).then_inc(step, 1)
                        dve.wait_ge(step, s + 15)
                        nc.vector.tensor_reduce(flat(pos[:, :, :]), ranks[:, :, :, :].rearrange("p g k e -> p (g k) e"), X_AXIS, ALU.add).then_inc(step, 1)
                        nc.vector.tensor_scalar(flat(first_slot[:, :, :]), e_of, float(CAP), -1.0, ALU.mult, ALU.add).then_inc(step, 1)
                        dve.wait_ge(step, s + 17)
                        nc.vector.scalar_tensor_tensor(out=slot_read[:, bass.ds(n * GB, GB), :], in0=pos[:, :, :], scalar=float(CAP),
                                                       in1=first_slot[:, :, :], op0=ALU.min, op1=ALU.add).then_inc(step, 1)
                        nc.vector.tensor_scalar(flat(over[:, :, :]), flat(pos[:, :, :]), float(CAP), 4.0 * SLOTS, ALU.is_gt, ALU.mult).then_inc(half, 1)
                        dve.wait_ge(half, (2 + GB) * n + 1)
                        dve.wait_ge(step, s + 18)
                        nc.vector.tensor_tensor(slot_in[:, :, :], slot_read[:, bass.ds(n * GB, GB), :], over[:, :, :], ALU.add).then_inc(half, 1)
                        dve.wait_ge(half, (2 + GB) * n + 2)
                        for j in range(GB):
                            nc.vector.tensor_scalar(d1[:, j % 2, :], iota256[:, :], slot_in[:, j, 0:1], None, ALU.is_equal).then_inc(half, 1)
                            dve.wait_ge(half, (2 + GB) * n + 3 + j)
                            dve.wait_ge(xe_ready, GB * n + j + GB)
                            nc.vector.scalar_tensor_tensor(out=disp[:, j % 2, :], in0=iota256[:, :], scalar=slot_in[:, j, 1:2], in1=d1[:, j % 2, :],
                                                           op0=ALU.is_equal, op1=ALU.add).then_inc(disp_ready, 1)


def build_experts(core, taken):
    nc, inp = core.nc, core.inp
    GATE, UP, DOWN = 0, 2, 4
    N = B * CAP
    DEEP = 4
    with Stage(core, "experts") as st:
        wg = st.sb("wg", [C, DEEP, HID])
        wu = st.sb("wu", [C, DEEP, HID])
        wp = st.sb("wp", [HID, DEEP, C])
        sg = st.sb("sg", [HID, 2, N])
        gs = st.sb("gs", [HID, 2, N])
        hid = st.sb("hid", [HID, 2, N])
        loaded = [st.sem(f"loaded{k}") for k in range(DEEP)]
        up_ready, sig_done, gated, hid_ready, down_ready, down_done = (st.sem(n) for n in (
            "up_ready", "sig_done", "gated", "hid_ready", "down_ready", "down_done"))
        passed = st.sem("passed")
        with nc.Block() as block:
            @block.sync
            def _(sp):
                st.clear_retired(sp)

                def load(e, k):
                    sp.dma_start(wg[:, k, :], inp['L0_ffn_w_gate'].rearrange("e c h -> c e h")[:, e, :]).then_inc(loaded[k], 16)
                    sp.dma_start(wu[:, k, :], inp['L0_ffn_w_fc'].rearrange("e c h -> c e h")[:, e, :]).then_inc(loaded[k], 16)
                    sp.dma_start(wp[:, k, :], inp['L0_ffn_w_proj'].rearrange("e h c -> h e c")[:, e, :]).then_inc(loaded[k], 16)
                for k in range(DEEP):
                    load(k, k)
                with sp.Fori(1, E16 // DEEP) as i:
                    for k in range(DEEP):
                        sp.wait_ge(down_ready, DEEP * i + k - DEEP + 1)
                        load(DEEP * i + k, k)

            @block.tensor
            def _(pe):
                def up(i, k):
                    e, par = DEEP * i + k, k % 2
                    pe.wait_ge(loaded[k], 48 * i + 48)
                    pe.wait_ge(hid_ready, e)
                    rhs = taken[:, bass.ds(e, 1), :, :].rearrange("p a b s -> p (a b s)")
                    nc.tensor.matmul(core.psum[0:HID, GATE + par, :], wg[:, k, :], rhs, start=True, stop=True).then_inc(up_ready, 1)
                    nc.tensor.matmul(core.psum[0:HID, UP + par, :], wu[:, k, :], rhs, start=True, stop=True).then_inc(up_ready, 1)

                def down(e, k):
                    par = k % 2
                    pe.wait_ge(hid_ready, e + 2)
                    pe.wait_ge(down_done, e)
                    nc.tensor.matmul(core.psum[:, DOWN + par, :], wp[:, k, :], hid[:, par, :], start=True, stop=True).then_inc(down_ready, 1)

                def experts(i, first):
                    for k in range(DEEP):
                        up(i, k)
                        if not (first and k == 0):
                            down(DEEP * i + k - 1, (k - 1) % DEEP)
                experts(0, True)
                with pe.Fori(1, E16 // DEEP) as i:
                    experts(i, False)
                down(E16 - 1, DEEP - 1)

            @block.scalar
            def _(act):
                act.sem_inc(down_done, 1)

                def sigmoid(e, par):
                    act.wait_ge(up_ready, 2 * e + 1)
                    act.wait_ge(gated, e)
                    nc.scalar.activation(sg[:, par, :], core.psum[0:HID, GATE + par, :], ACT.Sigmoid).then_inc(sig_done, 1)

                def copy_down(e, par):
                    act.wait_ge(down_ready, e + 1)
                    nc.scalar.activation(taken[:, bass.ds(e, 1), :, :].rearrange("p a b s -> p (a b s)"), core.psum[:, DOWN + par, :],
                                         ACT.Identity).then_inc(down_done, 1)

                def pair(i, first):
                    for par in range(2):
                        sigmoid(2 * i + par, par)
                        if not (first and par == 0):
                            copy_down(2 * i + par - 1, 1 - par)
                pair(0, True)
                with act.Fori(1, E16 // 2) as i:
                    pair(i, False)
                copy_down(E16 - 1, 1)

            @block.vector
            def _(dve):
                dve.sem_inc(gated, 1)
                dve.sem_inc(hid_ready, 1)
                dve.wait_ge(gated, 1)
                with dve.Fori(0, E16 // 2) as i:
                    for par in range(2):
                        e = 2 * i + par
                        dve.wait_ge(sig_done, e + 1)
                        nc.vector.tensor_tensor(gs[:, par, :], core.psum[0:HID, GATE + par, :], sg[:, par, :], ALU.mult).then_inc(gated, 1)
                        dve.wait_ge(gated, e + 2)
                        dve.wait_ge(up_ready, 2 * e + 2)
                        nc.vector.tensor_tensor(hid[:, par, :], core.psum[0:HID, UP + par, :], gs[:, par, :], ALU.mult).then_inc(hid_ready, 1)


def build_combine(core, taken, slot_read, prob):
    nc = core.nc
    with Stage(core, "combine") as st:
        iota256 = st.sb("iota256", [T, SLOTS])
        c1 = st.sb("c1", [T, 2, SLOTS])
        c2 = st.sb("c2", [T, 2, SLOTS])
        cw = st.sb("cw", [T, 2, SLOTS])
        eo = st.sb("eo", [C, 2, SLOTS])
        cwT = st.sb("cwT", [128, 2, 2, T])
        eoT = st.sb("eoT", [128, 2, 2, C])
        consts, eo_ready, step, cw_ready, cwT_ready, eoT_ready, cwT_done, eoT_done, y_ready, y_done = (st.sem(n) for n in (
            "consts", "eo_ready", "step", "cw_ready", "cwT_ready", "eoT_ready", "cwT_done", "eoT_done", "y_ready", "y_done"))
        CW_BANK, EO_BANK, Y_BANK = 0, 2, 4
        passed = st.sem("passed")
        with nc.Block() as block:
            @block.gpsimd
            def _(pool):
                st.clear_retired(pool)
                nc.gpsimd.iota(iota256[:, :], pattern=[[1, SLOTS]], base=0, channel_multiplier=0, allow_small_or_imprecise_dtypes=True).then_inc(consts, 1)
                with pool.Fori(0, B // 2) as i:
                    for par in range(2):
                        b = 2 * i + par
                        pool.wait_ge(eoT_ready, b + 1)
                        nc.gpsimd.tensor_copy(eo[:, par, :].rearrange("p (e a s) -> p e a s", e=E16, a=1),
                                              taken[:, :, bass.ds(b, 1), :]).then_inc(eo_ready, 1)

            @block.tensor
            def _(pe):
                pe.sem_inc(eoT_ready, 2)
                pe.sem_inc(y_ready, 2)
                pe.sem_inc(cwT_ready, 1)

                def turn(b, par):
                    pe.wait_ge(cw_ready, b + 1)
                    pe.wait_ge(cwT_done, b)
                    for s in range(2):
                        mm = nc.tensor.transpose(core.psum[:, CW_BANK + par, s * T:(s + 1) * T], cw[:, par, s * 128:(s + 1) * 128], core.ident[:, :])
                    mm.then_inc(cwT_ready, 1)
                    pe.wait_ge(eo_ready, b + 1)
                    pe.wait_ge(eoT_done, b)
                    for s in range(2):
                        mm = nc.tensor.transpose(core.psum[:, EO_BANK + par, s * C:(s + 1) * C], eo[:, par, s * 128:(s + 1) * 128], core.ident[:, :])
                    mm.then_inc(eoT_ready, 1)

                def gather(b, par):
                    pe.wait_ge(cwT_done, b + 2)
                    pe.wait_ge(eoT_done, b + 2)
                    pe.wait_ge(y_done, b)
                    for s in range(2):
                        mm = nc.tensor.matmul(core.psum[:, Y_BANK + par, 0:C], cwT[:, par, s, :], eoT[:, par, s, :], start=(s == 0), stop=(s == 1))
                    mm.then_inc(y_ready, 1)

                def pair(i, first):
                    for par in range(2):
                        turn(2 * i + par, par)
                        if not first:
                            gather(2 * i + par - 2, par)
                pair(0, True)
                with pe.Fori(1, B // 2) as i:
                    pair(i, False)
                gather(B - 2, 0)
                gather(B - 1, 1)

            @block.scalar
            def _(act):
                act.sem_inc(cwT_done, 1)
                act.sem_inc(eoT_done, 1)
                with act.Fori(0, B // 2) as i:
                    for par in range(2):
                        b = 2 * i + par
                        act.wait_ge(cwT_ready, b + 2)
                        act.wait_ge(y_ready, b + 1)
                        nc.scalar.activation(cwT[:, par, :, :], core.psum[:, CW_BANK + par, 0:SLOTS].rearrange("p (s t) -> p s t", s=2),
                                             ACT.Identity).then_inc(cwT_done, 1)
                        act.wait_ge(eoT_ready, b + 3)
                        nc.scalar.activation(eoT[:, par, :, :], core.psum[:, EO_BANK + par, 0:SLOTS].rearrange("p (s c) -> p s c", s=2),
                                             ACT.Identity).then_inc(eoT_done, 1)

            @block.vector
            def _(dve):
                dve.wait_ge(consts, 1)
                dve.sem_inc(y_done, 1)

                def weights(b, par):
                    for k, dst in enumerate((c1, c2)):
                        nc.vector.tensor_scalar(dst[:, par, :], iota256[:, :], slot_read[:, b, k:k + 1], prob[:, b, k:k + 1],
                                                ALU.is_equal, ALU.mult).then_inc(step, 1)
                    dve.wait_ge(step, 2 * b + 2)
                    dve.wait_ge(cwT_ready, b)
                    nc.vector.tensor_tensor(cw[:, par, :], c1[:, par, :], c2[:, par, :], ALU.add).then_inc(cw_ready, 1)

                def keep(b, par):
                    dve.wait_ge(y_ready, b + 3)
                    stand_alone(dve, passed)
                    nc.vector.tensor_copy(core.branch[:, b, :], core.psum[:, Y_BANK + par, 0:C]).then_inc(y_done, 1)

                def pair(i, first):
                    for par in range(2):
                        weights(2 * i + par, par)
                        if not first:
                            keep(2 * i + par - 2, par)
                pair(0, True)
                with dve.Fori(1, B // 2) as i:
                    pair(i, False)
                keep(B - 2, 0)
                keep(B - 1, 1)


def build_attention64(core, name):
    nc, inp = core.nc, core.inp
    scale = float(D64) ** -0.5
    nk = NCTX
    INNER = H * D64
    QK = 2 * T + 2 * nk
    S_BANK, T_BANK, O_BANK, OT_BANK, Y_BANK, QK_BANK, V_BANK = 0, 2, 3, 4, 5, 6, 7
    with Stage(core, name) as st:
        wq = st.sb("wq", [C, INNER])
        wk = st.sb("wk", [CC, INNER])
        wv = st.sb("wv", [CC, INNER])
        wo = st.sb("wo", [128, H // 2, C])
        xc = st.sb("xc", [C, 2, T])
        cc = st.sb("cc", [CC, 2, nk])
        qT = st.sb("qT", [128, NU, 2, T])
        keys_q = st.sb("keys_q", [128, NU, 2, 2, nk])
        va = st.sb("va", [nk, NU, QUAD, D64 + 1])
        sc = st.sb("sc", [T, 2, QUAD, nk])
        pT = st.sb("pT", [nk, 2, QUAD, T])
        on = st.sb("on", [T, 2, QUAD, D64])
        oT = st.sb("oT", [128, 2, 2, T])
        negmax = st.sb("negmax", [T, 2, QUAD])
        rden = st.sb("rden", [T, 2, QUAD])
        loaded, consts, src_ready, projected = (st.sem(n) for n in ("loaded", "consts", "src_ready", "projected"))
        qk_done, v_done, scored, max_step, shifted, p_ready, turned, pT_ready = (st.sem(n) for n in (
            "qk_done", "v_done", "scored", "max_step", "shifted", "p_ready", "turned", "pT_ready"))
        o_ready, den_step, o_done, o_turned, oT_done, y_ready, y_done, y_part = (st.sem(n) for n in (
            "o_ready", "den_step", "o_done", "o_turned", "oT_done", "y_ready", "y_done", "y_part"))
        UNITS = NU * B

        passed = st.sem("passed")
        with nc.Block() as block:
            @block.sync
            def _(sp):
                for dst, src in ((wq[:, :], inp['L1_xattn_Wq'][:, :]), (wk[:, :], inp['L1_xattn_Wk'][:, :]), (wv[:, :], inp['L1_xattn_Wv'][:, :]),
                                 (wo[:, :, :], inp['L1_xattn_Wo'].rearrange("(t p) c -> p t c", p=128))):
                    sp.dma_start(dst, src).then_inc(loaded, 16)
                sp.wait_ge(loaded, 64)

            @block.gpsimd
            def _(pool):
                st.clear_retired(pool)
                nc.gpsimd.memset(keys_q[:, :, :, :, :], 0.0).then_inc(consts, 1)
                nc.gpsimd.memset(va[:, :, :, D64:D64 + 1], 1.0).then_inc(consts, 1)
                with pool.Fori(0, B // 2) as i:
                    for par in range(2):
                        b = 2 * i + par
                        pool.wait_ge(projected, 2 * NU * b + 1)
                        nc.gpsimd.tensor_copy(xc[:, par, :], core.xT[:, b, :]).then_inc(src_ready, 1)
                        nc.gpsimd.tensor_copy(cc[:, par, :], core.ctxT[:, b, :]).then_inc(src_ready, 1)

            @block.tensor
            def _(pe):
                pe.sem_inc(projected, 2 * NU + 1)
                pe.wait_ge(loaded, 64)
                pe.wait_ge(consts, 2)

                def project(b, par, g):
                    u = NU * b + g
                    if g == 0:
                        pe.wait_ge(src_ready, 2 * b + 2)
                    pe.wait_ge(qk_done, 3 * u)
                    for k in range(2):
                        cols = slice((2 * g + k) * 128, (2 * g + k + 1) * 128)
                        nc.tensor.matmul(core.psum[:, QK_BANK, k * T:(k + 1) * T], wq[:, cols], xc[:, par, :], start=True, stop=True)
                        mm = nc.tensor.matmul(core.psum[:, QK_BANK, 2 * T + k * nk:2 * T + (k + 1) * nk], wk[:, cols], cc[:, par, :],
                                              start=True, stop=True)
                    mm.then_inc(projected, 1)
                    pe.wait_ge(v_done, u)
                    nc.tensor.matmul(core.psum[0:nk, V_BANK, 0:QUAD * D64], cc[:, par, :], wv[:, g * QUAD * D64:(g + 1) * QUAD * D64],
                                     start=True, stop=True).then_inc(projected, 1)

                def score(b, par, g):
                    u = NU * b + g
                    pe.wait_ge(qk_done, 3 * u + 3)
                    pe.wait_ge(shifted, u)
                    for k in range(2):
                        mm = nc.tensor.matmul(core.psum[:, S_BANK + g % 2, 2 * k * nk:2 * (k + 1) * nk], qT[:, g, k, :], keys_q[:, g, k, :, :],
                                              start=True, stop=True)
                    mm.then_inc(scored, 1)

                def turn(b, par, g):
                    u = NU * b + g
                    pe.wait_ge(p_ready, u + 1)
                    pe.wait_ge(pT_ready, u)
                    for j in range(QUAD):
                        mm = nc.tensor.transpose(core.psum[0:nk, T_BANK, j * T:(j + 1) * T], sc[:, g % 2, j, :], core.ident[:, :])
                    mm.then_inc(turned, 1)

                def weigh(b, par, g):
                    u = NU * b + g
                    pe.wait_ge(pT_ready, u + 1)
                    pe.wait_ge(v_done, u + 1)
                    pe.wait_ge(o_done, u)
                    for j in range(QUAD):
                        mm = nc.tensor.matmul(core.psum[:, O_BANK, j * (D64 + 1):(j + 1) * (D64 + 1)], pT[:, g % 2, j, :], va[:, g, j, :],
                                              start=True, stop=True)
                    mm.then_inc(o_ready, 1)

                def turn_o(b, par, g):
                    u = NU * b + g
                    pe.wait_ge(o_done, u + 1)
                    pe.wait_ge(oT_done, u)
                    for k in range(2):
                        mm = nc.tensor.transpose(core.psum[:, OT_BANK, k * T:(k + 1) * T],
                                                 on[:, g % 2, 2 * k:2 * k + 2, :].rearrange("p a d -> p (a d)"), core.ident[:, :])
                    mm.then_inc(o_turned, 1)

                def out_project(b, par, g):
                    u = NU * b + g
                    pe.wait_ge(oT_done, u + 1)
                    if g == 0:
                        pe.wait_ge(y_done, b)
                    for k in range(2):
                        mm = nc.tensor.matmul(core.psum[:, Y_BANK, 0:C], oT[:, g % 2, k, :], wo[:, 2 * g + k, :],
                                              start=(g == 0 and k == 0), stop=(g == NU - 1 and k == 1))
                    if g == NU - 1:
                        mm.then_inc(y_ready, 1)

                steps = [(score, 0), (weigh, 2), (turn, 1), (turn_o, 3), (out_project, 4), (project, -2)]

                def at(i, par, g, back):
                    t = NU * par + g - back
                    return 2 * i + t // NU, (t // NU) % 2, t % NU

                def pair(i, first, last):
                    for par in range(2):
                        for g in range(NU):
                            for step, back in steps:
                                t = NU * par + g - back
                                if (first and t < 0) or (last and t >= 2 * NU):
                                    continue
                                step(*at(i, par, g, back))

                project(0, 0, 0)
                project(0, 0, 1)
                pair(0, True, False)
                with pe.Fori(1, B // 2 - 1) as i:
                    pair(i, False, False)
                pair(B // 2 - 1, False, True)
                for over in range(4):
                    for step, back in steps:
                        t = 2 * NU + over - back
                        if back > over:
                            step(*at(B // 2 - 1, 0, 2 * NU + over, back))

            @block.scalar
            def _(act):
                def copy_qk(u, g):
                    act.wait_ge(projected, 2 * u + 2 + 2 * NU)
                    nc.scalar.activation(qT[:, g, :, :], core.psum[:, QK_BANK, 0:2 * T].rearrange("p (k t) -> p k t", k=2),
                                         ACT.Identity).then_inc(qk_done, 1)
                    for a in range(2):
                        rows = slice(D64 * a, D64 * a + D64)
                        nc.scalar.activation(keys_q[rows, g, :, a, :], core.psum[rows, QK_BANK, 2 * T:QK].rearrange("p (k n) -> p k n", k=2),
                                             ACT.Identity).then_inc(qk_done, 1)

                def exponential(u, g):
                    act.wait_ge(shifted, u + 2)
                    nc.scalar.activation(sc[:, g % 2, :, :], sc[:, g % 2, :, :], ACT.Exp, scale=scale).then_inc(p_ready, 1)

                def copy_pT(u, g):
                    act.wait_ge(turned, u + 1)
                    nc.scalar.activation(pT[:, g % 2, :, :], core.psum[0:nk, T_BANK, :].rearrange("p (j t) -> p j t", j=QUAD),
                                         ACT.Identity).then_inc(pT_ready, 1)

                def copy_oT(u, g):
                    act.wait_ge(o_turned, u + 1)
                    nc.scalar.activation(oT[:, g % 2, :, :], core.psum[:, OT_BANK, 0:2 * T].rearrange("p (k t) -> p k t", k=2),
                                         ACT.Identity).then_inc(oT_done, 1)

                steps = [(exponential, 0), (copy_pT, 1), (copy_oT, 3), (copy_qk, -2)]

                def pair(i, first, last):
                    for t0 in range(2 * NU):
                        for step, back in steps:
                            t = t0 - back
                            if (first and t < 0) or (last and t >= 2 * NU):
                                continue
                            step(2 * NU * i + t, t % NU)

                act.wait_ge(consts, 2)
                copy_qk(0, 0)
                copy_qk(1, 1)
                pair(0, True, False)
                with act.Fori(1, B // 2 - 1) as i:
                    pair(i, False, False)
                pair(B // 2 - 1, False, True)
                for over in range(3):
                    for step, back in steps:
                        if back > over:
                            step(UNITS + over - back, (over - back) % NU)

            @block.vector
            def _(dve):
                dve.sem_inc(shifted, 1)

                def copy_v(u, g):
                    dve.wait_ge(projected, 2 * u + 3 + 2 * NU)
                    nc.vector.tensor_copy(va[:, g, :, 0:D64], core.psum[0:nk, V_BANK, 0:QUAD * D64].rearrange("p (j d) -> p j d", j=QUAD)).then_inc(v_done, 1)

                def shift(u, g, fresh=False):
                    dve.wait_ge(scored, u + 1)
                    s = core.psum[:, S_BANK + g % 2, 0:QUAD * nk].rearrange("p (j n) -> p j n", j=QUAD)
                    nc.vector.tensor_reduce(negmax[:, g % 2, :], s, X_AXIS, ALU.max, negate=True).then_inc(max_step, 1)
                    dve.wait_ge(max_step, u + 1)
                    if not fresh:
                        dve.wait_ge(turned, u - 1)
                    nm = negmax[:, g % 2, :].rearrange("p (q a) -> p q a", a=1).broadcast_to([T, QUAD, nk])
                    nc.vector.tensor_tensor(sc[:, g % 2, :, :], s, nm, ALU.add).then_inc(shifted, 1)

                def norm(u, g, fresh=False):
                    dve.wait_ge(o_ready, u + 1)
                    o = core.psum[:, O_BANK, 0:QUAD * (D64 + 1)].rearrange("p (j d) -> p j d", j=QUAD)
                    nc.vector.reciprocal(rden[:, g % 2, :], o[:, :, D64]).then_inc(den_step, 1)
                    dve.wait_ge(den_step, u + 1)
                    if not fresh:
                        dve.wait_ge(o_turned, u - 1)
                    rd = rden[:, g % 2, :].rearrange("p (j a) -> p j a", a=1).broadcast_to([T, QUAD, D64])
                    nc.vector.tensor_tensor(on[:, g % 2, :, :], o[:, :, 0:D64], rd, ALU.mult).then_inc(o_done, 1)

                def keep_y(b):
                    dve.wait_ge(y_ready, b + 1)
                    stand_alone(dve, passed)
                    nc.vector.tensor_copy(core.branch[:, b, :], core.psum[:, Y_BANK, 0:C]).then_inc(y_done, 1)

                steps = [(shift, 0), (norm, 2), (copy_v, -2)]

                def pair(i, first, last):
                    for t0 in range(2 * NU):
                        for step, back in steps:
                            t = t0 - back
                            if (first and t < 0) or (last and t >= 2 * NU):
                                continue
                            if step is copy_v:
                                step(2 * NU * i + t, t % NU)
                            else:
                                step(2 * NU * i + t, t % NU, first and t < 2)
                        if t0 % NU == NU - 1 and not (first and t0 < NU):
                            keep_y(2 * i + t0 // NU - 1)

                copy_v(0, 0)
                copy_v(1, 1)
                pair(0, True, False)
                with dve.Fori(1, B // 2 - 1) as i:
                    pair(i, False, False)
                pair(B // 2 - 1, False, True)
                for over in range(2):
                    norm(UNITS + over - 2, (over - 2) % NU)
                keep_y(B - 1)


def build_gate(core, gate, mixed_bias, experts):
    nc, inp = core.nc, core.inp
    E4, HG = 4, 128
    with Stage(core, "gate") as st:
        w1 = st.sb("w1", [C, HG])
        b1 = st.sb("b1", [HG, 1])
        w2 = st.sb("w2", [HG, E4])
        b2 = st.sb("b2", [1, E4])
        be = st.sb("be", [E4, 3, C])
        pooled = st.sb("pooled", [C, B])
        mean = st.sb("mean", [C, B])
        hid = st.sb("hid", [HG, B])
        lg = st.sb("lg", [B, 8])
        top = st.sb("top", [B, 8])
        idx = st.sb("idx", [B, 8], U32)
        idf = st.sb("idf", [B, 2])
        diff = st.sb("diff", [B, 2])
        ex = st.sb("ex", [B, 2])
        sm = st.sb("sm", [B, 2])
        total = st.sb("total", [B, 2])
        iota4 = st.sb("iota4", [B, E4])
        w_1 = st.sb("w_1", [B, E4])
        w_2 = st.sb("w_2", [B, E4])
        w = st.sb("w", [B, E4])
        wT = st.sb("wT", [E4, B])
        diag = st.sb("diag", [B, B, E4])
        loaded, consts, step, mm, acted = (st.sem(n) for n in ("loaded", "consts", "step", "mm", "acted"))
        passed = st.sem("passed")
        with nc.Block() as block:
            @block.sync
            def _(sp):
                n = 0
                for dst, src in ((w1[:, :], inp['L1_ffn_Wg1'][:, :]), (b1[:, :], col(inp['L1_ffn_bg1'])), (w2[:, :], inp['L1_ffn_Wg2'][:, :]),
                                 (b2[:, :], row(inp['L1_ffn_bg2'])), (be[:, 0, :], inp['L1_ffn_bq'][:, :]), (be[:, 1, :], inp['L1_ffn_bk'][:, :]),
                                 (be[:, 2, :], inp['L1_ffn_bv'][:, :])):
                    sp.dma_start(dst, src).then_inc(loaded, 16)
                    n += 1
                for k, name in enumerate(('L1_ffn_Wq', 'L1_ffn_Wk', 'L1_ffn_Wv')):
                    sp.dma_start(experts[:, :, k * C:(k + 1) * C], inp[name].rearrange("e c d -> c e d")).then_inc(loaded, 16)
                    n += 1
                sp.wait_ge(loaded, 16 * n)

            @block.gpsimd
            def _(pool):
                st.clear_retired(pool)
                nc.gpsimd.iota(iota4[:, :], pattern=[[1, E4]], base=0, channel_multiplier=0, allow_small_or_imprecise_dtypes=True).then_inc(consts, 1)

            @block.tensor
            def _(pe):
                pe.wait_ge(loaded, 160)
                pe.wait_ge(step, 2)
                nc.tensor.matmul(core.psum[0:HG, 0, 0:B], w1[:, :], mean[:, :], start=True, stop=True).then_inc(mm, 1)
                pe.wait_ge(step, 3)
                nc.tensor.matmul(core.psum[0:B, 1, 0:E4], hid[:, :], w2[:, :], start=True, stop=False)
                nc.tensor.matmul(core.psum[0:B, 1, 0:E4], core.ones[0:1, 0:B], b2[:, :], start=False, stop=True).then_inc(mm, 1)
                pe.wait_ge(step, 14)
                nc.tensor.transpose(core.psum[0:E4, 2, 0:B], w[:, :], core.ident[0:B, 0:B]).then_inc(mm, 1)
                pe.wait_ge(step, 15)
                nc.tensor.matmul(core.psum[:, 3, 0:B * E4], core.ones[0:B, :], diag[:, :, :].rearrange("p b e -> p (b e)"), start=True, stop=True).then_inc(mm, 1)
                pe.wait_ge(step, 16)
                for k in range(3):
                    nc.tensor.matmul(core.psum[:, 4 + k, 0:B], be[:, k, :], wT[:, :], start=True, stop=True).then_inc(mm, 1)

            @block.scalar
            def _(act):
                act.wait_ge(step, 7)
                nc.scalar.activation(ex[:, :], diff[:, :], ACT.Exp).then_inc(acted, 1)

            @block.vector
            def _(dve):
                v = nc.vector
                dve.wait_ge(loaded, 160)
                dve.wait_ge(consts, 1)
                v.tensor_reduce(pooled[:, :], core.xT[:, :, :], X_AXIS, ALU.add).then_inc(step, 1)
                dve.wait_ge(step, 1)
                v.tensor_scalar(mean[:, :], pooled[:, :], 1.0 / T, None, ALU.mult).then_inc(step, 1)
                dve.wait_ge(mm, 1)
                v.tensor_scalar(hid[:, :], core.psum[0:HG, 0, 0:B], b1[:, :], 0.0, ALU.add, ALU.max).then_inc(step, 1)
                v.memset(lg[:, :], NEG).then_inc(step, 1)
                dve.wait_ge(mm, 2)
                dve.wait_ge(step, 4)
                v.tensor_copy(lg[:, 0:E4], core.psum[0:B, 1, 0:E4]).then_inc(step, 1)
                dve.wait_ge(step, 5)
                v.max(top[:, :], lg[:, :]).then_inc(step, 1)
                dve.wait_ge(step, 6)
                v.tensor_scalar(diff[:, :], top[:, 0:2], top[:, 0:1], None, ALU.subtract).then_inc(step, 1)
                v.max_index(idx[:, :], top[:, :], lg[:, :]).then_inc(step, 1)
                dve.wait_ge(step, 8)
                v.tensor_copy(idf[:, :], idx[:, 0:2]).then_inc(step, 1)
                dve.wait_ge(acted, 1)
                v.tensor_reduce(total[:, 0:1], ex[:, :], X_AXIS, ALU.add).then_inc(step, 1)
                dve.wait_ge(step, 10)
                v.reciprocal(total[:, 1:2], total[:, 0:1]).then_inc(step, 1)
                dve.wait_ge(step, 11)
                v.tensor_scalar(sm[:, :], ex[:, :], total[:, 1:2], None, ALU.mult).then_inc(step, 1)
                dve.wait_ge(step, 12)
                v.tensor_scalar(w_1[:, :], iota4[:, :], idf[:, 0:1], sm[:, 0:1], ALU.is_equal, ALU.mult).then_inc(step, 1)
                v.tensor_scalar(w_2[:, :], iota4[:, :], idf[:, 1:2], sm[:, 1:2], ALU.is_equal, ALU.mult).then_inc(acted, 1)
                dve.wait_ge(step, 13)
                dve.wait_ge(acted, 2)
                v.tensor_tensor(w[:, :], w_1[:, :], w_2[:, :], ALU.add).then_inc(step, 1)
                dve.wait_ge(step, 14)
                v.tensor_tensor(diag[:, :, :], core.ident[0:B, 0:B].rearrange("p (b a) -> p b a", a=1).broadcast_to([B, B, E4]),
                                w[:, :].rearrange("p (a e) -> p a e", a=1).broadcast_to([B, B, E4]), ALU.mult).then_inc(step, 1)
                dve.wait_ge(mm, 3)
                v.tensor_copy(wT[:, :], core.psum[0:E4, 2, 0:B]).then_inc(step, 1)
                dve.wait_ge(mm, 4)
                v.tensor_copy(gate[:, :], core.psum[:, 3, 0:B * E4]).then_inc(acted, 1)
                dve.wait_ge(mm, 7)
                v.tensor_copy(mixed_bias[:, :, :], core.psum[:, 4:7, 0:B]).then_inc(acted, 1)


def build(nc, inp, out, stages=None):
    with ExitStack() as ctx:
        core = Core(nc, ctx, inp, out)
        recip_all = core.sb("recip_all", [T, B, H])
        taken = core.sb("taken", [C, E16, B, CAP])
        slot_read = core.sb("slot_read", [T, B, 2])
        prob = core.sb("prob", [T, B, 2])
        gate = core.sb("gate", [128, B * 4])
        mixed_bias = core.sb("mixed_bias", [C, 3, B])
        experts = core.sb("experts", [C, 4, 3 * C])
        steps = [
            lambda: build_setup(core),
            lambda: build_gru(core),
            lambda: build_close(core, "close0", turned=True),
            lambda: build_attention8(core, "xattn0", NCTX, inp['L0_xattn_Wq'][:, :], inp['L0_xattn_Wk'][:, :], inp['L0_xattn_Wv'][:, :],
                                     cross=True, b_q=inp['L0_xattn_bq'], b_k=inp['L0_xattn_bk'], clip=True, recip_all=recip_all),
            lambda: build_close(core, "close1", wo=inp['L0_xattn_Wo'][:, :], v_bias=inp['L0_xattn_bv'], out_bias=inp['L0_xattn_bo'], nan_guard=(recip_all, inp['L0_xattn_Wv'][:, :])),
            lambda: build_route(core, taken, slot_read, prob),
            lambda: build_experts(core, taken),
            lambda: build_combine(core, taken, slot_read, prob),
            lambda: build_close(core, "close2"),
            lambda: build_attention8(core, "attn1", T, None, None, None, transposed=(4, 5, 6), causal=True, guard=True),
            lambda: build_close(core, "close3", wo=core.wT[:, 7, :]),
            lambda: build_attention64(core, "xattn1"),
            lambda: build_close(core, "close4", out_bias=inp['L1_xattn_bo']),
            lambda: build_gate(core, gate, mixed_bias, experts),
            lambda: build_attention8(core, "ffn1", T, None, None, None, mixed=(gate, mixed_bias, experts)),
            lambda: build_close(core, "close5", wo=inp['L1_ffn_Wo'][:, :], v_bias_by_batch=mixed_bias[:, 2, :], out_bias=inp['L1_ffn_bo'],
                                last=True),
        ]
        n = len(steps) if stages is None else stages
        for step in steps[:n]:
            step()


def kernel(**inputs):
    import numpy as np
    import concourse.bacc as bacc
    from concourse.bass_utils import run_bass_kernel_spmd

    nc = bacc.Bacc("TRN2", target_bir_lowering=False, num_devices=1)
    arrays, inp = {}, {}
    for name in INS:
        a = np.ascontiguousarray(inputs[name])
        arrays[f"in_{name}_dram"] = a
        inp[name] = nc.dram_tensor(f"in_{name}_dram", a.shape, mybir.dt.from_np(a.dtype), kind="ExternalInput").ap()
    out = nc.dram_tensor("out_0_dram", (B, T, C), F32, kind="ExternalOutput").ap()
    build(nc, inp, out)
    return run_bass_kernel_spmd(nc, [arrays], core_ids=[0]).results[0]["out_0_dram"]
```

```python
from contextlib import ExitStack

import concourse.bass as bass
from concourse import mybir

F32 = mybir.dt.float32
BF16 = mybir.dt.bfloat16
U32 = mybir.dt.uint32
ALU = mybir.AluOpType
ACT = mybir.ActivationFunctionType
X_AXIS = mybir.AxisListType.X

B = 32
T = 128
C = 128
NCTX = 77
CC = 96
H = 16
D8 = C // H
D64 = 64
QUAD = 4
NU = H // QUAD
GB = 4
NG = B // GB
E16 = 16
CAP = 16
SLOTS = E16 * CAP
HID = 64
EPS = 1e-5
CLAMP = 10000.0
NEG = -3.0e38

INS = ['x', 'ctx_768', 'L0_attn_Wz', 'L0_attn_bz', 'L0_attn_Wh', 'L0_attn_bh', 'L0_xattn_Wq', 'L0_xattn_bq',
       'L0_xattn_Wk', 'L0_xattn_bk', 'L0_xattn_Wv', 'L0_xattn_bv', 'L0_xattn_Wo', 'L0_xattn_bo',
       'L0_ffn_w_router', 'L0_ffn_w_fc', 'L0_ffn_w_gate', 'L0_ffn_w_proj', 'L1_attn_Wq', 'L1_attn_Wk',
       'L1_attn_Wv', 'L1_attn_Wo', 'L1_xattn_Wq', 'L1_xattn_Wk', 'L1_xattn_Wv', 'L1_xattn_Wo', 'L1_xattn_bo',
       'L1_ffn_Wq', 'L1_ffn_bq', 'L1_ffn_Wk', 'L1_ffn_bk', 'L1_ffn_Wv', 'L1_ffn_bv', 'L1_ffn_Wg1', 'L1_ffn_bg1',
       'L1_ffn_Wg2', 'L1_ffn_bg2', 'L1_ffn_Wo', 'L1_ffn_bo']


class Core:

    def __init__(self, nc, ctx, inp, out):
        self.nc, self.ctx, self.inp, self.out = nc, ctx, inp, out
        self.retired = []
        self.psum = ctx.enter_context(nc.psum_tensor("psum", [128, 8, 512], F32))
        self.x = self.sb("x", [T, B, C])
        self.xT = self.sb("xT", [C, B, T])
        self.branch = self.sb("branch", [128, B, 128])
        self.ctxT = self.sb("ctxT", [CC, B, NCTX])
        self.ident = self.sb("ident", [128, 128])
        self.ones = self.sb("ones", [128, 128])
        self.zeros = self.sb("zeros", [128, 512])
        self.pow_half = self.sb("pow_half", [128, GB])
        self.head_mask = self.sb("head_mask", [128, H])
        self.wT = self.sb("wT", [128, 8, 128])

    def sb(self, name, shape, dt=F32):
        return self.ctx.enter_context(self.nc.sbuf_tensor(name, shape, dt))

    def bank(self, n):
        return self.psum[:, n, :]


class Stage:

    def __init__(self, core, name):
        self.core, self.name, self.ctx, self.sems = core, name, ExitStack(), []

    def __enter__(self):
        return self

    def __exit__(self, *_):
        self.ctx.close()
        for handle in self.core.retired:
            self.core.nc.release_semaphore(handle)
        self.core.retired = self.sems

    def sb(self, name, shape, dt=F32):
        return self.ctx.enter_context(self.core.nc.sbuf_tensor(f"{self.name}_{name}", shape, dt))

    def sem(self, name):
        self.sems.append(self.core.nc.alloc_semaphore(name=f"{self.name}_{name}"))
        return self.sems[-1]

    def clear_retired(self, engine):
        numbers = sorted(handle.num for handle in self.core.retired)
        while numbers:
            run = 1
            while run < len(numbers) and numbers[run] == numbers[0] + run:
                run += 1
            engine.sem_clear(range(numbers[0], numbers[0] + run))
            numbers = numbers[run:]


def stand_alone(engine, passed):
    engine.sem_inc(passed, 1)


def prefetch(sp, transfers, arrived):
    for dst, src in transfers:
        sp.dma_start(dst, src).then_inc(arrived, 16)
    if transfers:
        sp.wait_ge(arrived, 16 * len(transfers))


def row(ap):
    return ap.rearrange("(a n) -> a n", a=1)


def col(ap):
    return ap.rearrange("(n a) -> n a", a=1)


def build_setup(core):
    nc, inp = core.nc, core.inp
    with Stage(core, "setup") as st:
        wn = st.sb("w_natural", [128, 8, 128])
        NBUF = 4
        xin = st.sb("xin", [T, NBUF, GB, C])
        cin = st.sb("cin", [NCTX, NBUF, GB, CC])
        loaded_w, loaded_x, x_kept = st.sem("loaded_w"), [st.sem(f"loaded_x{k}") for k in range(NBUF)], st.sem("x_kept")
        zeroed, ident_ready, consts = st.sem("zeroed"), st.sem("ident_ready"), st.sem("consts")
        tr_ready, xT_done, cT_done, w_ready, w_done = (st.sem(n) for n in ("tr_ready", "xT_done", "cT_done", "w_ready", "w_done"))
        x_g = inp['x'].rearrange("(n g) t c -> n t g c", g=GB)
        c_g = inp['ctx_768'].rearrange("(n g) t c -> n t g c", g=GB)

        passed = st.sem("passed")
        with nc.Block() as block:
            @block.sync
            def _(sp):
                for k, (name, l) in enumerate([('L0_attn_Wz', 0), ('L0_attn_Wz', 1), ('L0_attn_Wh', 0), ('L0_attn_Wh', 1)]):
                    sp.dma_start(wn[:, k, :], inp[name][l]).then_inc(loaded_w, 16)
                for k, name in enumerate(['L1_attn_Wq', 'L1_attn_Wk', 'L1_attn_Wv', 'L1_attn_Wo']):
                    sp.dma_start(wn[:, 4 + k, :], inp[name][:, :]).then_inc(loaded_w, 16)
                for k in range(NBUF):
                    sp.dma_start(xin[:, k, :, :], x_g[k]).then_inc(loaded_x[k], 16)
                    sp.dma_start(cin[:, k, :, :], c_g[k]).then_inc(loaded_x[k], 16)
                with sp.Fori(1, NG // NBUF) as i:
                    for k in range(NBUF):
                        sp.wait_ge(tr_ready, 2 * (NBUF * (i - 1) + k) + 2)
                        sp.wait_ge(x_kept, NBUF * (i - 1) + k + 1)
                        sp.dma_start(xin[:, k, :, :], x_g[NBUF * i + k]).then_inc(loaded_x[k], 16)
                        sp.dma_start(cin[:, k, :, :], c_g[NBUF * i + k]).then_inc(loaded_x[k], 16)

            @block.gpsimd
            def _(pool):
                st.clear_retired(pool)
                nc.gpsimd.memset(core.ones[:, :], 1.0).then_inc(consts, 1)
                nc.gpsimd.memset(core.zeros[:, :], 0.0).then_inc(consts, 1)
                nc.gpsimd.memset(core.pow_half[:, :], -0.5).then_inc(consts, 1)
                pool.wait_ge(consts, 3)
                nc.gpsimd.affine_select(out=core.ident[:, :], in_=core.zeros[:, 0:128], compare_op=ALU.not_equal, fill=1.0,
                                        base=0, pattern=[[-1, 128]], channel_multiplier=1).then_inc(ident_ready, 1)
                nc.gpsimd.affine_select(out=core.head_mask[:, :], in_=core.ones[:, 0:H], compare_op=ALU.is_ge, fill=0.0,
                                        base=0, pattern=[[-D8, H]], channel_multiplier=1).then_inc(zeroed, 1)
                pool.wait_ge(zeroed, 1)
                nc.gpsimd.affine_select(out=core.head_mask[:, :], in_=core.head_mask[:, :], compare_op=ALU.is_ge, fill=0.0,
                                        base=D8 - 1, pattern=[[D8, H]], channel_multiplier=-1).then_inc(zeroed, 1)

            @block.tensor
            def _(pe):
                pe.wait_ge(ident_ready, 1)
                pe.wait_ge(loaded_w, 16 * 8)
                for k in range(8):
                    nc.tensor.transpose(core.psum[:, 4 + k // 4, (k % 4) * 128:(k % 4 + 1) * 128], wn[:, k, :], core.ident[:, :]).then_inc(w_ready, 1)
                with pe.Fori(0, NG // NBUF) as i:
                    for k in range(NBUF):
                        n = NBUF * i + k
                        pe.wait_ge(loaded_x[k], 32 * i + 32)
                        pe.wait_ge(xT_done, n + 1)
                        for j in range(GB):
                            last = nc.tensor.transpose(core.psum[:, k % 2, j * T:(j + 1) * T], xin[:, k, j, :], core.ident[:, :])
                        last.then_inc(tr_ready, 1)
                        pe.wait_ge(cT_done, n + 1)
                        for j in range(GB):
                            last = nc.tensor.transpose(core.psum[0:CC, 2 + k % 2, j * NCTX:(j + 1) * NCTX], cin[:, k, j, :],
                                                       core.ident[0:NCTX, 0:NCTX])
                        last.then_inc(tr_ready, 1)

            @block.scalar
            def _(act):
                act.sem_inc(xT_done, 2)

                def copy_xT(n, k):
                    act.wait_ge(tr_ready, 2 * n + 1)
                    nc.scalar.activation(core.xT[:, bass.ts(n, GB), :], core.psum[:, k % 2, :].rearrange("p (g t) -> p g t", g=GB),
                                         ACT.Identity).then_inc(xT_done, 1)

                for k in range(NBUF):
                    copy_xT(k, k)
                with act.Fori(1, NG // NBUF) as i:
                    for k in range(NBUF):
                        copy_xT(NBUF * i + k, k)

            @block.vector
            def _(dve):
                dve.sem_inc(cT_done, 2)
                dve.wait_ge(w_ready, 8)
                nc.vector.tensor_copy(core.wT[:, :, :], core.psum[:, 4:6, :].rearrange("p a (k n) -> p (a k) n", k=4)).then_inc(w_done, 1)
                with dve.Fori(0, NG // NBUF) as i:
                    for k in range(NBUF):
                        n = NBUF * i + k
                        dve.wait_ge(loaded_x[k], 32 * i + 32)
                        stand_alone(dve, passed)
                        nc.vector.tensor_copy(core.x[:, bass.ts(n, GB), :], xin[:, k, :, :]).then_inc(x_kept, 1)
                        dve.wait_ge(tr_ready, 2 * n + 2)
                        stand_alone(dve, passed)
                        nc.vector.tensor_copy(core.ctxT[:, bass.ts(n, GB), :],
                                              core.psum[0:CC, 2 + k % 2, 0:GB * NCTX].rearrange("p (g t) -> p g t", g=GB)).then_inc(cT_done, 1)


def build_gru(core):
    nc, inp = core.nc, core.inp
    with Stage(core, "gru") as st:
        h1 = st.sb("h1", [C, B, T])
        bias = st.sb("bias", [128, 4, 2])
        keep = st.sb("keep", [128, 2, 512])
        z = st.sb("z", [128, 2, 512])
        sg = st.sb("sg", [128, 2, 512])
        g = st.sb("g", [128, 2, 512])
        v = st.sb("v", [128, 2, 512])
        first = st.sb("first", [128, 1])
        loaded, bias_ready, first_done = st.sem("loaded"), st.sem("bias_ready"), st.sem("first_done")
        passed = st.sem("passed")
        with nc.Block() as block:
            @block.sync
            def _(sp):
                st.clear_retired(sp)
                for l in range(2):
                    sp.dma_start(bias[:, 0, l:l + 1], col(inp['L0_attn_bz'][l])).then_inc(loaded, 16)
                    sp.dma_start(bias[:, 1, l:l + 1], col(inp['L0_attn_bh'][l])).then_inc(loaded, 16)

            for l, (src, dst) in enumerate([(core.xT, h1), (h1, core.branch)]):
                pre_ready, gates_ready, cand, value, scanned = (
                    st.sem(f"{n}{l}") for n in ("pre_ready", "gates_ready", "cand", "value", "scanned"))
                lay = [pre_ready, gates_ready, cand, value, scanned]
                gru_layer(core, block, l, src, dst, first[:, :], first_done, bias, keep, z, sg, g, v, loaded, bias_ready, *lay,
                          prev_scanned=prev if l else None)
                prev = scanned


def gru_layer(core, block, l, src, dst, first, first_done, bias, keep, z, sg, g, v, loaded, bias_ready, pre_ready, gates_ready,
              cand, value, scanned, prev_scanned):
    nc = core.nc
    groups = [(lambda i, par=par: 2 * i + par) for par in range(2)]

    @block.tensor
    def _(pe):
        if prev_scanned is not None:
            pe.wait_ge(prev_scanned, GB * (NG + 1) + 1)
        with pe.Fori(0, NG // 2) as i:
            for par in range(2):
                n = groups[par](i)
                pe.wait_ge(cand, n + 1)
                rhs = src[:, bass.ds(n * GB, GB), :]
                nc.tensor.matmul(core.bank(2 * par), core.wT[:, l, :], rhs, start=True, stop=True).then_inc(pre_ready, 1)
                nc.tensor.matmul(core.bank(2 * par + 1), core.wT[:, 2 + l, :], rhs, start=True, stop=True).then_inc(pre_ready, 1)

    @block.scalar
    def _(act):
        if l == 0:
            nc.scalar.activation(first, core.zeros[:, 0:1], ACT.Sigmoid).then_inc(first_done, 1)
        act.wait_ge(bias_ready, 2)
        with act.Fori(0, NG // 2) as i:
            for par in range(2):
                n = groups[par](i)
                act.wait_ge(pre_ready, 2 * n + 1)
                act.wait_ge(value, n + 1)
                nc.scalar.activation(z[:, par, :], core.bank(2 * par), ACT.Sigmoid, bias=bias[:, 0, l:l + 1]).then_inc(gates_ready, 1)
                act.wait_ge(scanned, GB * n + 1)
                nc.scalar.activation(keep[:, par, :], core.bank(2 * par), ACT.Sigmoid, bias=bias[:, 2, l:l + 1],
                                     scale=-1.0).then_inc(gates_ready, 1)
                act.wait_ge(pre_ready, 2 * n + 2)
                nc.scalar.activation(sg[:, par, :], core.bank(2 * par + 1), ACT.Sigmoid, bias=bias[:, 1, l:l + 1]).then_inc(gates_ready, 1)

    @block.vector
    def _(dve):
        if l == 0:
            dve.wait_ge(loaded, 64)
            nc.vector.tensor_scalar(bias[:, 2, :], bias[:, 0, :], -1.0, None, ALU.mult).then_inc(bias_ready, 1)
            nc.vector.tensor_scalar(bias[:, 3, :], bias[:, 1, :], 0.5, None, ALU.add).then_inc(bias_ready, 1)
            dve.wait_ge(bias_ready, 2)
        dve.sem_inc(cand, 2)
        dve.sem_inc(value, 2)
        dve.sem_inc(scanned, GB + 1)
        with dve.Fori(0, NG // 2) as i:
            for par in range(2):
                n = groups[par](i)
                dve.wait_ge(gates_ready, 3 * n + 3)
                nc.vector.scalar_tensor_tensor(out=g[:, par, :], in0=core.bank(2 * par + 1), scalar=bias[:, 3, l:l + 1],
                                               in1=sg[:, par, :], op0=ALU.add, op1=ALU.max).then_inc(cand, 1)
                dve.wait_ge(cand, n + 3)
                nc.vector.tensor_tensor(v[:, par, :], g[:, par, :], z[:, par, :], ALU.mult).then_inc(value, 1)
                dve.wait_ge(value, n + 3)
                for j in range(GB):
                    nc.vector.tensor_tensor_scan(dst[:, n * GB + j, :], keep[:, par, j * T:(j + 1) * T],
                                                 v[:, par, j * T:(j + 1) * T], 0.5, ALU.mult, ALU.add).then_inc(scanned, 1)


def build_close(core, name, wo=None, v_bias=None, v_bias_by_batch=None, out_bias=None, turned=False, nan_guard=None, last=False):
    nc, inp = core.nc, core.inp
    with_pe = turned or wo is not None
    with Stage(core, name) as st:
        cur = st.sb("cur", [128, 2, GB, 128])
        oT = st.sb("oT", [128, 2, GB, 128])
        z = st.sb("z", [128, 2, GB, C])
        xn = st.sb("xn", [128, 2, GB, C])
        stats = st.sb("stats", [128, GB, 6])
        mv = st.sb("mv", [128, 2, GB, 2])
        rstd = st.sb("rstd", [128, 2, GB])
        ve = st.sb("ve", [128, 2, GB])
        w_o = st.sb("w_o", [128, 128])
        b_v = st.sb("b_v", [128, 1])
        b_o = st.sb("b_o", [128, 128])
        loaded = st.sem("loaded")
        cur_ready, turned_ready, oT_done, y_ready, summed = (st.sem(n) for n in ("cur_ready", "turned_ready", "oT_done", "y_ready", "summed"))
        stat_step, ve_done, rstd_done, normed, xT_ready, xT_done = (
            st.sem(n) for n in ("stat_step", "ve_done", "rstd_done", "normed", "xT_ready", "xT_done"))
        stored = [st.sem("stored0"), st.sem("stored1")]
        x_copied, bo_added = st.sem("x_copied"), st.sem("bo_added")
        guard_step, guard_mm, mean_copied, oT_final = (st.sem(n) for n in ("guard_step", "guard_mm", "mean_copied", "oT_final"))
        if nan_guard:
            recip_all, w_v = nan_guard
            wv = st.sb("wv", [CC, C])
            csum = st.sb("csum", [CC, B])
            vmean = st.sb("vmean", [C, B])
            mean4 = st.sb("mean4", [C, 2, GB])
            rsum = st.sb("rsum", [T, 2])
            mask = st.sb("mask", [T, 1], U32)
            isnan = st.sb("isnan", [T, 1])
        n_load = (wo is not None) + (v_bias is not None) + (out_bias is not None) + (nan_guard is not None)
        Y = 4
        y_bank = (lambda par: 0 + par) if turned else (lambda par: 2 + par)

        passed = st.sem("passed")
        with nc.Block() as block:
            @block.sync
            def _(sp):
                if wo is not None:
                    sp.dma_start(w_o[:, :], wo).then_inc(loaded, 16)
                if v_bias is not None:
                    sp.dma_start(b_v[:, :], col(v_bias)).then_inc(loaded, 16)
                if nan_guard:
                    sp.dma_start(wv[:, :], w_v).then_inc(loaded, 16)
                if out_bias is not None:
                    sp.dma_start(b_o[:, :], row(out_bias).broadcast_to([128, 128])).then_inc(loaded, 16)
                if last:
                    with sp.Fori(0, NG // 2) as i:
                        for par in range(2):
                            n = 2 * i + par
                            sp.wait_ge(normed, GB * (n + 2))
                            sp.dma_start(core.out.rearrange("(n g) t c -> n t g c", g=GB)[n], xn[:, par, :, :]).then_inc(stored[par], 16)
                    for par in range(2):
                        sp.wait_ge(stored[par], 16 * (NG // 2))

            @block.gpsimd
            def _(pool):
                st.clear_retired(pool)
                if out_bias is not None:
                    pool.wait_ge(loaded, 16 * n_load)

                def add_out_bias(n):
                    if out_bias is not None:
                        xs = core.x[:, bass.ds(n * GB, GB), :]
                        nc.gpsimd.tensor_tensor(xs, xs, b_o[:, :].rearrange("p (a c) -> p a c", a=1).broadcast_to([128, GB, C]),
                                                ALU.add).then_inc(bo_added, 1)

                def rsqrt(n, par):
                    pool.wait_ge(ve_done, n + 1)
                    nc.gpsimd.tensor_tensor(rstd[:, par, :], ve[:, par, :], core.pow_half[:, :], ALU.pow).then_inc(rstd_done, 1)

                def pair(i, last_pair):
                    for par in range(2):
                        n = 2 * i + par
                        if not (last_pair and par == 1):
                            add_out_bias(n + 1)
                        rsqrt(n, par)

                add_out_bias(0)
                with pool.Fori(0, NG // 2 - 1) as i:
                    pair(i, False)
                pair(NG // 2 - 1, True)

            @block.tensor
            def _(pe):
                if wo is not None:
                    pe.wait_ge(loaded, 16 * n_load)
                pe.sem_inc(turned_ready, 2)

                def turn_x(n, par):
                    pe.wait_ge(normed, GB * (n + 2))
                    pe.wait_ge(xT_done, n)
                    for j in range(GB):
                        mm = nc.tensor.transpose(core.psum[:, 4 + par, j * T:(j + 1) * T], xn[:, par, j, :], core.ident[:, :])
                    mm.then_inc(xT_ready, 1)

                def turn_branch(n, par):
                    pe.wait_ge(cur_ready, n + 1)
                    if turned:
                        pe.wait_ge(summed, n)
                    else:
                        pe.wait_ge(oT_done, n)
                    for j in range(GB):
                        mm = nc.tensor.transpose(core.psum[:, par, j * T:(j + 1) * T], cur[:, par, j, :], core.ident[:, :])
                    mm.then_inc(turned_ready, 1)

                def project(n, par):
                    if nan_guard:
                        pe.wait_ge(oT_final, n + 1)
                    else:
                        pe.wait_ge(oT_done, n + 2)
                    pe.wait_ge(summed, n)
                    for j in range(GB):
                        mm = nc.tensor.matmul(core.psum[:, 2 + par, j * C:(j + 1) * C], oT[:, par, j, :], w_o[:, :], start=True, stop=True)
                    mm.then_inc(y_ready, 1)

                def pair(i, first, last_pair):
                    for par in range(2):
                        n = 2 * i + par
                        if wo is not None:
                            project(n, par)
                        if with_pe and not (last_pair and par == 1):
                            turn_branch(n + 1, 1 - par)
                        if not last and not first:
                            turn_x(n - 2, par)

                if nan_guard:
                    pe.wait_ge(guard_step, 1)
                    nc.tensor.matmul(core.psum[:, 6, 0:1], core.ones[:, :], rsum[:, 0:1], start=True, stop=True).then_inc(guard_mm, 1)
                    pe.wait_ge(guard_step, 2)
                    nc.tensor.matmul(core.psum[:, 7, 0:B], wv[:, :], csum[:, :], start=True, stop=True).then_inc(guard_mm, 1)
                if with_pe:
                    turn_branch(0, 0)
                pair(0, True, False)
                with pe.Fori(1, NG // 2 - 1) as i:
                    pair(i, False, False)
                pair(NG // 2 - 1, False, True)
                if not last:
                    turn_x(NG - 2, 0)
                    turn_x(NG - 1, 1)

            @block.scalar
            def _(act):
                act.sem_inc(oT_done, 1)
                act.sem_inc(xT_done, 1)

                def copy_cur(n, par):
                    act.wait_ge(turned_ready, n + 1)
                    nc.scalar.activation(cur[:, par, :, :], core.branch[:, bass.ds(n * GB, GB), :], ACT.Identity).then_inc(cur_ready, 1)

                def copy_oT(n, par):
                    act.wait_ge(turned_ready, n + 3)
                    src = core.psum[:, par, :].rearrange("p (g t) -> p g t", g=GB)
                    if v_bias is not None:
                        ins = nc.scalar.activation(oT[:, par, :, :], src, ACT.Identity, bias=b_v[:, :])
                        ins.then_inc(oT_done, 1)
                    elif v_bias_by_batch is not None:
                        for j in range(GB):
                            ins = nc.scalar.activation(oT[:, par, j, :], src[:, j, :], ACT.Identity,
                                                       bias=v_bias_by_batch[:, bass.ds(n * GB + j, 1)])
                        ins.then_inc(oT_done, 1)
                    else:
                        nc.scalar.activation(oT[:, par, :, :], src, ACT.Identity).then_inc(oT_done, 1)

                def copy_xT(n, par):
                    act.wait_ge(xT_ready, n + 1)
                    nc.scalar.activation(core.xT[:, bass.ds(n * GB, GB), :],
                                         core.psum[:, 4 + par, :].rearrange("p (g t) -> p g t", g=GB), ACT.Identity).then_inc(xT_done, 1)

                if v_bias is not None:
                    act.wait_ge(loaded, 16 * n_load)

                def pair(i, first, last_pair):
                    for par in range(2):
                        n = 2 * i + par
                        if with_pe and not last_pair:
                            copy_cur(n + 2, par)
                        if wo is not None and not (last_pair and par == 1):
                            copy_oT(n + 1, 1 - par)
                        if not last and not first:
                            copy_xT(n - 2, par)

                if with_pe:
                    copy_cur(0, 0)
                    copy_cur(1, 1)
                if wo is not None:
                    copy_oT(0, 0)
                pair(0, True, False)
                with act.Fori(1, NG // 2 - 1) as i:
                    pair(i, False, False)
                pair(NG // 2 - 1, False, True)
                if not last:
                    copy_xT(NG - 2, 0)
                    copy_xT(NG - 1, 1)

            @block.vector
            def _(dve):
                dve.sem_inc(summed, 1)
                dve.sem_inc(normed, GB)
                if nan_guard:
                    nc.vector.tensor_reduce(rsum[:, 0:1], recip_all[:, :, :].rearrange("p b h -> p (b h)"), X_AXIS, ALU.add).then_inc(guard_step, 1)
                    nc.vector.tensor_reduce(csum[:, :], core.ctxT[:, :, :], X_AXIS, ALU.add).then_inc(guard_step, 1)
                    dve.wait_ge(guard_mm, 1)
                    nc.vector.tensor_copy(rsum[:, 1:2], core.psum[:, 6, 0:1]).then_inc(guard_step, 1)
                    dve.wait_ge(guard_step, 3)
                    nc.vector.tensor_tensor(isnan[:, :], rsum[:, 1:2], rsum[:, 1:2], ALU.not_equal).then_inc(guard_step, 1)
                    dve.wait_ge(guard_step, 4)
                    nc.vector.tensor_copy(mask[:, :], isnan[:, :]).then_inc(guard_step, 1)
                    dve.wait_ge(guard_mm, 2)
                    dve.wait_ge(loaded, 16 * n_load)
                    nc.vector.tensor_scalar(vmean[:, :], core.psum[:, 7, 0:B], 1.0 / NCTX, b_v[:, :], ALU.mult, ALU.add).then_inc(guard_step, 1)
                    dve.wait_ge(guard_step, 6)

                def blend(n, par):
                    nc.vector.tensor_copy(mean4[:, par, :], vmean[:, bass.ds(n * GB, GB)]).then_inc(mean_copied, 1)
                    dve.wait_ge(mean_copied, n + 1)
                    dve.wait_ge(oT_done, n + 2)
                    stand_alone(dve, passed)
                    nc.vector.copy_predicated(oT[:, par, :, :], mask[:, :].rearrange("p (a b) -> p a b", a=1).broadcast_to([C, GB, T]),
                                              mean4[:, par, :].rearrange("p (g a) -> p g a", a=1).broadcast_to([C, GB, T])).then_inc(oT_final, 1)

                def add_up(n, par):
                    xs = core.x[:, bass.ds(n * GB, GB), :]
                    if out_bias is not None:
                        dve.wait_ge(bo_added, n + 1)
                    if turned:
                        dve.wait_ge(turned_ready, n + 3)
                        y = core.psum[:, par, :].rearrange("p (g c) -> p g c", g=GB)
                    elif wo is not None:
                        dve.wait_ge(y_ready, n + 1)
                        y = core.psum[:, 2 + par, :].rearrange("p (g c) -> p g c", g=GB)
                    else:
                        y = core.branch[:, bass.ds(n * GB, GB), :]
                    nc.vector.tensor_tensor(z[:, par, :, :], y, xs, ALU.add).then_inc(summed, 1)

                def statistics(n, par):
                    dve.wait_ge(summed, n + 2)
                    for j in range(GB):
                        nc.vector.bn_stats(stats[:, j, :], z[:, par, j, :]).then_inc(stat_step, 1)

                def norm(n, par, earlier):
                    dve.wait_ge(rstd_done, n + 1)
                    if last and not (isinstance(earlier, int) and earlier == 0):
                        dve.wait_ge(stored[par], 16 * earlier)
                    if not last and not (isinstance(n, int) and n < 2):
                        dve.wait_ge(xT_ready, n - 1)
                    for j in range(GB):
                        nc.vector.tensor_scalar(xn[:, par, j, :], z[:, par, j, :], mv[:, par, j, 0:1], rstd[:, par, j:j + 1],
                                                ALU.subtract, ALU.mult).then_inc(normed, 1)

                def aggregate(n, par):
                    dve.wait_ge(stat_step, 8 * n + 4)
                    stand_alone(dve, passed)
                    for j in range(GB):
                        nc.vector.bn_aggr(mv[:, par, j, :], stats[:, j, :]).then_inc(stat_step, 1)

                def keep_x(n, par):
                    dve.wait_ge(normed, GB * (n + 2))
                    if not last:
                        stand_alone(dve, passed)
                        nc.vector.tensor_copy(core.x[:, bass.ds(n * GB, GB), :], xn[:, par, :, :]).then_inc(x_copied, 1)

                def add_eps(n, par):
                    dve.wait_ge(stat_step, 8 * n + 8)
                    nc.vector.tensor_scalar(ve[:, par, :], mv[:, par, :, 1], EPS, None, ALU.add).then_inc(ve_done, 1)

                def pair(i, first, last_pair):
                    for par in range(2):
                        n = 2 * i + par
                        add_up(n, par)
                        if nan_guard and not (last_pair and par == 1):
                            blend(n + 1, 1 - par)
                        statistics(n, par)
                        if not (first and par == 0):
                            norm(n - 1, 1 - par, i - (1 - par))
                        aggregate(n, par)
                        if not (first and par == 0):
                            keep_x(n - 1, 1 - par)
                        add_eps(n, par)

                if nan_guard:
                    blend(0, 0)
                pair(0, True, False)
                with dve.Fori(1, NG // 2 - 1) as i:
                    pair(i, False, False)
                pair(NG // 2 - 1, False, True)
                norm(NG - 1, 1, NG // 2 - 1)
                keep_x(NG - 1, 1)


def build_attention8(core, name, nk, w_q, w_k, w_v, cross=False, b_q=None, b_k=None, transposed=None, causal=False,
                     clip=False, guard=False, mixed=None, recip_all=None, later=()):
    nc, inp = core.nc, core.inp
    scale = float(D8) ** -0.5
    ck = CC if cross else C
    S_BANK, T_BANK, OT_BANK, O_BANK, QK_BANK, V_BANK = 0, 2, 4, 5, 6, 7
    Q_AT, K_AT = slice(0, T), slice(T, T + nk)
    PAD = 32
    COPY_LAG = 1 if clip else 2
    TURN_LAG, WEIGH_LAG = 3, 4
    with Stage(core, name) as st:
        xc = st.sb("xc", [C, 2, T])
        cc = st.sb("cc", [CC, 2, NCTX])
        qT = st.sb("qT", [C, 2, T])
        kT = st.sb("kT", [C, 2, nk])
        keys_q = st.sb("keys_q", [C, 2, H, nk])
        va = st.sb("va", [nk, 2, H, PAD])
        sc = st.sb("sc", [T, NU, QUAD, nk])
        clipped = st.sb("clipped", [T, 2, QUAD, nk])
        pT = st.sb("pT", [nk, 2, QUAD, T])
        negmax = st.sb("negmax", [T, NU, QUAD])
        oT = st.sb("oT", [QUAD * PAD, 2, NU, T])
        den = st.sb("den", [T, 2, H])
        rden = st.sb("rden", [T, 2, H])
        wq, wk, wv = (st.sb(n, [128, C]) for n in ("wq", "wk", "wv"))
        bq, bk = st.sb("bq", [C, 1]), st.sb("bk", [C, 1])
        wmix = st.sb("wmix", [C, 2, 3, C]) if mixed else None
        weighted = st.sb("weighted", [C, 4, 3 * C]) if mixed else None
        gate_b = st.sb("gate_b", [C, 2, 4]) if mixed else None
        future = st.sb("future", [T, T], BF16) if causal else None
        identb = st.sb("identb", [T, T], BF16) if causal else None
        loaded, consts, src_ready, qk_projected, v_projected = (
            st.sem(n) for n in ("loaded", "consts", "src_ready", "qk_projected", "v_projected"))
        q_done, k_done, v_done, gate_step, mix_step, k_copied = (st.sem(n) for n in ("q_done", "k_done", "v_done", "gate_step", "mix_step", "k_copied"))
        scored, clip_step, max_step, shifted, p_ready, turned, pT_ready, weighed, oT_done, o_ready, den_step, recip_step, recip_kept, o_done = (st.sem(n) for n in (
            "scored", "clip_step", "max_step", "shifted", "p_ready", "turned", "pT_ready", "weighed", "oT_done", "o_ready",
            "den_step", "recip_step", "recip_kept", "o_done"))
        biased = b_q is not None
        n_load = 0
        weights = []
        if mixed is None and transposed is None:
            weights = [(wq[:, :], w_q), (wk[0:ck, :], w_k), (wv[0:ck, :], w_v)]
        if biased:
            weights += [(bq[:, :], col(b_q)), (bk[:, :], col(b_k))]
        n_load = len(weights)

        arrived = st.sem("arrived")
        passed = st.sem("passed")

        def spread_keys(engine, instructions, b, par, g):
            engine.wait_ge(k_copied, b + 1)
            heads = slice(QUAD * g, QUAD * g + QUAD)
            k_in = kT[:, par, :].rearrange("p (a n) -> p a n", a=1).broadcast_to([C, QUAD, nk])
            mask = core.head_mask[:, heads].rearrange("p (h a) -> p h a", a=1).broadcast_to([C, QUAD, nk])
            instructions.tensor_tensor(keys_q[:, par, heads, :], k_in, mask, ALU.mult).then_inc(k_done, 1)

        with nc.Block() as block:
            @block.sync
            def _(sp):
                for dst, src in weights:
                    sp.dma_start(dst, src).then_inc(loaded, 16)
                if n_load:
                    sp.wait_ge(loaded, 16 * n_load)
                prefetch(sp, later, arrived)

            @block.gpsimd
            def _(pool):
                st.clear_retired(pool)
                nc.gpsimd.memset(va[:, :, :, :], 0.0).then_inc(consts, 1)
                pool.wait_ge(consts, 1)
                nc.gpsimd.memset(va[:, :, :, D8:D8 + 1], 1.0).then_inc(consts, 1)
                if causal:
                    nc.gpsimd.tensor_copy(identb[:, :], core.ident[:, :]).then_inc(consts, 1)
                    nc.gpsimd.affine_select(out=future[:, :], in_=core.zeros[:, 0:T], compare_op=ALU.is_ge, fill=NEG, base=0,
                                            pattern=[[-1, T]], channel_multiplier=1).then_inc(consts, 1)

                def mix(b, par):
                    gate, _, experts = mixed
                    nc.gpsimd.tensor_copy(gate_b[:, par, :], gate[:, bass.ds(4 * b, 4)]).then_inc(gate_step, 1)
                    pool.wait_ge(gate_step, b + 1)
                    nc.gpsimd.tensor_tensor(weighted[:, :, :], experts[:, :, :],
                                            gate_b[:, par, :].rearrange("p (e a) -> p e a", a=1).broadcast_to([C, 4, 3 * C]),
                                            ALU.mult).then_inc(mix_step, 1)
                    pool.wait_ge(mix_step, 3 * b + 1)
                    nc.gpsimd.tensor_tensor(weighted[:, 0:2, :], weighted[:, 0:2, :], weighted[:, 2:4, :], ALU.add).then_inc(mix_step, 1)
                    pool.wait_ge(mix_step, 3 * b + 2)
                    nc.gpsimd.tensor_tensor(wmix[:, par, :, :].rearrange("p k n -> p (k n)"), weighted[:, 0, :], weighted[:, 1, :],
                                            ALU.add).then_inc(mix_step, 1)

                def sources(b, par):
                    pool.wait_ge(v_projected, b + 1)
                    nc.gpsimd.tensor_copy(xc[:, par, :], core.xT[:, b, :]).then_inc(src_ready, 1)
                    if cross:
                        nc.gpsimd.tensor_copy(cc[:, par, :], core.ctxT[:, b, :]).then_inc(src_ready, 1)
                    if mixed is not None:
                        mix(b, par)

                def pair(i, last):
                    for par in range(2):
                        b = 2 * i + par
                        if not (last and par == 1):
                            sources(b + 1, 1 - par)
                        if clip:
                            for g in range(NU):
                                spread_keys(pool, nc.gpsimd, b, par, g)

                sources(0, 0)
                with pool.Fori(0, B // 2 - 1) as i:
                    pair(i, False)
                pair(B // 2 - 1, True)

            @block.tensor
            def _(pe):
                pe.sem_inc(v_projected, 2)
                if n_load:
                    pe.wait_ge(loaded, 16 * n_load)
                pe.wait_ge(consts, 4 if causal else 2)

                def projection(k, par):
                    if mixed is not None:
                        return wmix[:, par, k, :]
                    if transposed is not None:
                        return core.wT[:, transposed[k], :]
                    return (wq[:, :], wk[0:ck, :], wv[0:ck, :])[k]

                def project_qk(b, par):
                    pe.wait_ge(src_ready, (2 if cross else 1) * (b + 1))
                    if mixed is not None:
                        pe.wait_ge(mix_step, 3 * b + 3)
                    kv = cc[:, par, :] if cross else xc[:, par, :]
                    pe.wait_ge(q_done, b)
                    pe.wait_ge(k_copied, b)
                    nc.tensor.matmul(core.psum[:, QK_BANK, Q_AT], projection(0, par), xc[:, par, :], start=True, stop=True)
                    nc.tensor.matmul(core.psum[:, QK_BANK, K_AT], projection(1, par), kv, start=True, stop=True).then_inc(qk_projected, 1)

                def project_v(b, par):
                    pe.wait_ge(v_done, b)
                    nc.tensor.matmul(core.psum[0:nk, V_BANK, 0:C], cc[:, par, :] if cross else xc[:, par, :], projection(2, par),
                                     start=True, stop=True).then_inc(v_projected, 1)

                def score(b, par, g):
                    u = NU * b + g
                    if g == 0:
                        pe.wait_ge(q_done, b + 1)
                    pe.wait_ge(k_done, u + 1)
                    pe.wait_ge(clip_step if clip else shifted, u)
                    out = core.psum[:, S_BANK + g % 2, 0:QUAD * nk]
                    mm = nc.tensor.matmul(out, qT[:, par, :], keys_q[:, par, QUAD * g:QUAD * g + QUAD, :], start=True, stop=not causal)
                    if causal:
                        for j in range(QUAD):
                            mm = nc.tensor.matmul(out[:, j * nk:(j + 1) * nk], identb[:, :], future[:, :], start=False, stop=(j == QUAD - 1))
                    mm.then_inc(scored, 1)

                def turn(b, g):
                    u = NU * b + g
                    pe.wait_ge(p_ready, u + 1)
                    pe.wait_ge(pT_ready, u)
                    for j in range(QUAD):
                        mm = nc.tensor.transpose(core.psum[0:nk, T_BANK + g % 2, j * T:(j + 1) * T], sc[:, g, j, :], core.ident[:, :])
                    mm.then_inc(turned, 1)

                def weigh(b, par, g):
                    u = NU * b + g
                    if g == 0:
                        pe.wait_ge(v_done, b + 1)
                        pe.wait_ge(oT_done, b)
                    pe.wait_ge(pT_ready, u + 2)
                    for j in range(QUAD):
                        rows = slice(PAD * j, PAD * j + PAD)
                        mm = nc.tensor.matmul(core.psum[rows, OT_BANK, g * T:(g + 1) * T], va[:, par, QUAD * g + j, :], pT[:, g % 2, j, :],
                                              start=True, stop=True, tile_position=(0, PAD * j))
                    if g == NU - 1:
                        mm.then_inc(weighed, 1)

                def turn_back(b, par):
                    pe.wait_ge(oT_done, b + 1)
                    pe.wait_ge(o_done, b + 1)
                    for g in range(NU):
                        mm = nc.tensor.transpose(core.psum[:, O_BANK, g * T:(g + 1) * T], oT[:, par, g, :], core.ident[:, :])
                    mm.then_inc(o_ready, 1)

                def before(b, par, g, back):
                    k = g - back
                    return (b, par, k) if k >= 0 else (b - 1, 1 - par, k + NU)

                def pair(i, first, last):
                    for par in range(2):
                        b = 2 * i + par
                        for g in range(NU):
                            score(b, par, g)
                            if g == 0 and not (last and par == 1):
                                project_qk(b + 1, 1 - par)
                            if not (first and par == 0 and g < TURN_LAG):
                                bb, _, gg = before(b, par, g, TURN_LAG)
                                turn(bb, gg)
                            if not (first and par == 0 and g < WEIGH_LAG):
                                weigh(*before(b, par, g, WEIGH_LAG))
                            if g == 0 and not first:
                                turn_back(b - 2, par)
                            if g == 2 and not (last and par == 1):
                                project_v(b + 1, 1 - par)

                project_qk(0, 0)
                project_v(0, 0)
                pair(0, True, False)
                with pe.Fori(1, B // 2 - 1) as i:
                    pair(i, False, False)
                pair(B // 2 - 1, False, True)
                for over in range(WEIGH_LAG):
                    if over < TURN_LAG:
                        turn(B - 1, NU - TURN_LAG + over)
                    weigh(B - 1, 1, NU - WEIGH_LAG + over)
                    if over == 0:
                        turn_back(B - 2, 0)
                turn_back(B - 1, 1)

            @block.scalar
            def _(act):
                act.sem_inc(pT_ready, 1)
                if n_load:
                    act.wait_ge(loaded, 16 * n_load)
                act.wait_ge(consts, 4 if causal else 2)

                def copy_qk(b, par):
                    act.wait_ge(qk_projected, b + 1)
                    q_bias = bq[:, :] if biased else (mixed[1][:, 0, bass.ds(b, 1)] if mixed else 0.0)
                    nc.scalar.activation(qT[:, par, :], core.psum[:, QK_BANK, Q_AT], ACT.Identity, bias=q_bias).then_inc(q_done, 1)
                    k_bias = bk[:, :] if biased else (mixed[1][:, 1, bass.ds(b, 1)] if mixed else 0.0)
                    nc.scalar.activation(kT[:, par, :], core.psum[:, QK_BANK, K_AT], ACT.Identity, bias=k_bias).then_inc(k_copied, 1)

                def copy_v(b, par, fresh=False):
                    act.wait_ge(v_projected, b + 3)
                    if not fresh:
                        act.wait_ge(weighed, b - 1)
                    nc.scalar.activation(va[:, par, :, 0:D8], core.psum[0:nk, V_BANK, 0:C].rearrange("p (h d) -> p h d", h=H),
                                         ACT.Identity).then_inc(v_done, 1)

                def copy_oT(b, par):
                    act.wait_ge(weighed, b + 1)
                    nc.scalar.activation(oT[:, par, :, :], core.psum[:, OT_BANK, :].rearrange("p (u t) -> p u t", u=NU),
                                         ACT.Identity).then_inc(oT_done, 1)

                def exponential(u, g):
                    act.wait_ge(shifted, u + 2)
                    nc.scalar.activation(sc[:, g, :, :], sc[:, g, :, :], ACT.Exp, scale=scale).then_inc(p_ready, 1)

                def copy_pT(u, g):
                    act.wait_ge(turned, u + 1)
                    nc.scalar.activation(pT[:, g % 2, :, :], core.psum[0:nk, T_BANK + g % 2, :].rearrange("p (j t) -> p j t", j=QUAD),
                                         ACT.Identity).then_inc(pT_ready, 1)

                def pair(i, first, last):
                    for par in range(2):
                        b = 2 * i + par
                        for g in range(NU):
                            if g == 0 and not (last and par == 1):
                                copy_qk(b + 1, 1 - par)
                            exponential(NU * b + g, g)
                            if g == 2 and not (first and par == 0):
                                copy_oT(b - 1, 1 - par)
                            if not (first and par == 0 and g < COPY_LAG):
                                copy_pT(NU * b + g - COPY_LAG, (g - COPY_LAG) % 2)
                            if g == 3 and not (last and par == 1):
                                copy_v(b + 1, 1 - par, first and par == 0)

                copy_qk(0, 0)
                copy_v(0, 0, True)
                pair(0, True, False)
                with act.Fori(1, B // 2 - 1) as i:
                    pair(i, False, False)
                pair(B // 2 - 1, False, True)
                for back in range(COPY_LAG, 0, -1):
                    copy_pT(NU * B - back, back % 2)
                copy_oT(B - 1, 1)

            @block.vector
            def _(dve):
                dve.sem_inc(shifted, 1)
                dve.sem_inc(clip_step, 1)
                dve.sem_inc(o_done, 1)
                if n_load:
                    dve.wait_ge(loaded, 16 * n_load)

                def scores(g):
                    return core.psum[:, S_BANK + g % 2, 0:QUAD * nk].rearrange("p (j n) -> p j n", j=QUAD)

                def clamp(u, g, fresh=False):
                    dve.wait_ge(scored, u + 1)
                    if not fresh:
                        dve.wait_ge(shifted, u)
                    nc.vector.tensor_scalar(clipped[:, g % 2, :, :], scores(g), CLAMP / scale, -CLAMP / scale, ALU.min, ALU.max).then_inc(clip_step, 1)

                def maximum(u, g):
                    if clip:
                        dve.wait_ge(clip_step, u + 2)
                    else:
                        dve.wait_ge(scored, u + 1)
                    nc.vector.tensor_reduce(negmax[:, g, :], clipped[:, g % 2, :, :] if clip else scores(g), X_AXIS, ALU.max,
                                            negate=True).then_inc(max_step, 1)

                def shift(u, g, fresh):
                    dve.wait_ge(max_step, u + 1)
                    if not fresh:
                        dve.wait_ge(turned, u - NU + 1)
                    nm = negmax[:, g, :].rearrange("p (q a) -> p q a", a=1).broadcast_to([T, QUAD, nk])
                    nc.vector.tensor_tensor(sc[:, g, :, :], clipped[:, g % 2, :, :] if clip else scores(g), nm, ALU.add).then_inc(shifted, 1)

                def spread_next(b, par, g, first, last):
                    if g == 0:
                        spread_keys(dve, nc.vector, b, par, NU - 1)
                    elif not (last and par == 1):
                        spread_keys(dve, nc.vector, b + 1, 1 - par, g - 1)

                def outputs():
                    return core.psum[:, O_BANK, :].rearrange("p (h d) -> p h d", h=H)

                def floor(b, par):
                    dve.wait_ge(o_ready, b + 1)
                    nc.vector.tensor_scalar(den[:, par, :], outputs()[:, :, D8], 1e-12, None, ALU.max).then_inc(den_step, 1)

                def invert(b, par):
                    if guard:
                        dve.wait_ge(den_step, b + 1)
                    else:
                        dve.wait_ge(o_ready, b + 1)
                    nc.vector.reciprocal(rden[:, par, :], den[:, par, :] if guard else outputs()[:, :, D8]).then_inc(recip_step, 1)

                def divide(b, par):
                    dve.wait_ge(recip_step, b + 1)
                    rd = rden[:, par, :]
                    out = core.branch[:, b, :].rearrange("p (h d) -> p h d", h=H)
                    nc.vector.tensor_tensor(out, outputs()[:, :, 0:D8], rd.rearrange("p (h a) -> p h a", a=1).broadcast_to([T, H, D8]),
                                            ALU.mult).then_inc(o_done, 1)
                    if recip_all is not None:
                        nc.vector.tensor_copy(recip_all[:, b, :], rd).then_inc(recip_kept, 1)

                def pair(i, first, last):
                    for par in range(2):
                        b = 2 * i + par
                        for g in range(NU):
                            u, ahead = NU * b + g, not (last and par == 1 and g == NU - 1)
                            dividing = g == 1 and not first
                            maximum(u, g)
                            if clip and ahead:
                                clamp(u + 1, (g + 1) % NU, first and par == 0 and g == 0)
                            if not clip:
                                spread_next(b, par, g, first, last)
                            if dividing and guard:
                                floor(b - 2, par)
                            shift(u, g, first and par == 0)
                            if dividing:
                                invert(b - 2, par)
                            if dividing:
                                divide(b - 2, par)

                if not clip:
                    for piece in range(NU - 1):
                        spread_keys(dve, nc.vector, 0, 0, piece)
                if clip:
                    clamp(0, 0, True)
                pair(0, True, False)
                with dve.Fori(1, B // 2 - 1) as i:
                    pair(i, False, False)
                pair(B // 2 - 1, False, True)
                for b in (B - 2, B - 1):
                    if guard:
                        floor(b, b % 2)
                    invert(b, b % 2)
                    divide(b, b % 2)


def build_route(core, taken, slot_read, prob):
    nc, inp = core.nc, core.inp
    LOGITS, COUNTS, XE = 0, 2, 4
    with Stage(core, "route") as st:
        w_r = st.sb("w_r", [C, E16])
        xt = st.sb("xt", [C, 2, GB, T])
        xs = st.sb("xs", [T, 2, GB, C])
        iota16 = st.sb("iota16", [T, E16])
        iota256 = st.sb("iota256", [T, SLOTS])
        upto = st.sb("upto", [T, T], BF16)
        onesb = st.sb("onesb", [T, T], BF16)
        mx = st.sb("mx", [T, GB])
        lg = st.sb("lg", [T, 2, GB, E16])
        rs = st.sb("rs", [T, GB])
        rr = st.sb("rr", [T, GB])
        pr = st.sb("pr", [T, 2, GB, E16])
        top = st.sb("top", [T, GB, 8])
        idx = st.sb("idx", [T, GB, 8], U32)
        idf = st.sb("idf", [T, GB, 2])
        chosen = st.sb("chosen", [T, 2, GB, 2, E16], BF16)
        ranks = st.sb("ranks", [T, GB, 2, E16])
        pos = st.sb("pos", [T, GB, 2])
        capped = st.sb("capped", [T, GB, 2])
        first_slot = st.sb("first_slot", [T, GB, 2])
        over = st.sb("over", [T, GB, 2])
        slot_in = st.sb("slot_in", [T, GB, 2])
        d1 = st.sb("d1", [T, GB, SLOTS])
        disp = st.sb("disp", [T, 2, SLOTS])
        loaded, consts, src_ready, logit_ready, counted, xe_ready, xe_done = (st.sem(n) for n in (
            "loaded", "consts", "src_ready", "logit_ready", "counted", "xe_ready", "xe_done"))
        shifted, exp_done, step, chosen_done, half, disp_ready = (st.sem(n) for n in (
            "shifted", "exp_done", "step", "chosen_done", "half", "disp_ready"))
        passed = st.sem("passed")
        with nc.Block() as block:
            @block.sync
            def _(sp):
                sp.dma_start(w_r[:, :], inp['L0_ffn_w_router'][:, :]).then_inc(loaded, 16)
                sp.wait_ge(loaded, 16)

            @block.gpsimd
            def _(pool):
                st.clear_retired(pool)
                nc.gpsimd.iota(iota16[:, :], pattern=[[1, E16]], base=0, channel_multiplier=0, allow_small_or_imprecise_dtypes=True).then_inc(consts, 1)
                nc.gpsimd.iota(iota256[:, :], pattern=[[1, SLOTS]], base=0, channel_multiplier=0, allow_small_or_imprecise_dtypes=True).then_inc(consts, 1)
                nc.gpsimd.tensor_copy(onesb[:, :], core.ones[:, :]).then_inc(consts, 1)
                nc.gpsimd.affine_select(out=upto[:, :], in_=core.ones[:, 0:T], compare_op=ALU.is_ge, fill=0.0, base=0,
                                        pattern=[[1, T]], channel_multiplier=-1).then_inc(consts, 1)
                with pool.Fori(0, NG // 2) as i:
                    for par in range(2):
                        n = 2 * i + par
                        pool.wait_ge(logit_ready, n + 1)
                        nc.gpsimd.tensor_copy(xt[:, par, :, :], core.xT[:, bass.ds(n * GB, GB), :]).then_inc(src_ready, 1)
                        pool.wait_ge(xe_ready, GB * n + 1)
                        nc.gpsimd.tensor_copy(xs[:, par, :, :], core.x[:, bass.ds(n * GB, GB), :]).then_inc(src_ready, 1)

            @block.tensor
            def _(pe):
                pe.wait_ge(loaded, 16)
                pe.wait_ge(consts, 4)
                pe.sem_inc(xe_ready, GB + 1)
                pe.sem_inc(logit_ready, 2)

                def logits(n, par):
                    pe.wait_ge(src_ready, 2 * n + 1)
                    pe.wait_ge(shifted, n)
                    for j in range(GB):
                        mm = nc.tensor.matmul(core.psum[:, LOGITS + par, j * E16:(j + 1) * E16], xt[:, par, j, :], w_r[:, :], start=True, stop=True)
                    mm.then_inc(logit_ready, 1)

                def dispatch(n, par):
                    pe.wait_ge(chosen_done, n + 1)
                    counts = core.psum[:, COUNTS + par, 0:GB * 2 * E16].rearrange("p (g k e) -> p g k e", g=GB, k=2)
                    nc.tensor.matmul(counts, upto[:, :], chosen[:, par, :, :, :], start=True, stop=False)
                    nc.tensor.matmul(counts[:, :, 1, :], onesb[:, :], chosen[:, par, :, 0, :], start=False, stop=True).then_inc(counted, 1)
                    pe.wait_ge(src_ready, 2 * n + 2)
                    for j in range(GB):
                        pe.wait_ge(disp_ready, GB * n + j + 1)
                        pe.wait_ge(xe_done, GB * n + j + 1)
                        nc.tensor.matmul(core.psum[:, XE + j % 2, 0:SLOTS], xs[:, par, j, :], disp[:, j % 2, :], start=True,
                                         stop=True).then_inc(xe_ready, 1)

                def pair(i, last):
                    for par in range(2):
                        n = 2 * i + par
                        if not (last and par == 1):
                            logits(n + 1, 1 - par)
                        dispatch(n, par)

                logits(0, 0)
                with pe.Fori(0, NG // 2 - 1) as i:
                    pair(i, False)
                pair(NG // 2 - 1, True)

            @block.scalar
            def _(act):
                act.sem_inc(xe_done, 2)

                def exponential(n, par):
                    act.wait_ge(shifted, n + 2)
                    nc.scalar.activation(pr[:, par, :, :], lg[:, par, :, :], ACT.Exp).then_inc(exp_done, 1)

                def pair(i, last):
                    for par in range(2):
                        n = 2 * i + par
                        for j in range(GB):
                            if j == GB - 1 and not (last and par == 1):
                                exponential(n + 1, 1 - par)
                            act.wait_ge(xe_ready, GB * n + j + 2 + GB)
                            nc.scalar.activation(taken[:, :, bass.ds(n * GB + j, 1), :],
                                                 core.psum[:, XE + j % 2, 0:SLOTS].rearrange("p (e a s) -> p e a s", e=E16, a=1),
                                                 ACT.Identity).then_inc(xe_done, 1)

                exponential(0, 0)
                with act.Fori(0, NG // 2 - 1) as i:
                    pair(i, False)
                pair(NG // 2 - 1, True)

            @block.vector
            def _(dve):
                dve.wait_ge(consts, 4)
                dve.sem_inc(shifted, 1)
                K = 18
                with dve.Fori(0, NG // 2) as i:
                    for par in range(2):
                        n = 2 * i + par
                        s = K * n
                        wide = lambda t, w: t.rearrange("p (g a) -> p g a", a=1).broadcast_to([T, GB, w])
                        dve.wait_ge(logit_ready, n + 3)
                        lp = core.psum[:, LOGITS + par, 0:GB * E16].rearrange("p (g e) -> p g e", g=GB)
                        nc.vector.tensor_reduce(mx[:, :], lp, X_AXIS, ALU.max, negate=True).then_inc(step, 1)
                        dve.wait_ge(step, s + 1)
                        nc.vector.tensor_tensor(lg[:, par, :, :], lp, wide(mx[:, :], E16), ALU.add).then_inc(shifted, 1)
                        dve.wait_ge(exp_done, n + 1)
                        p = pr[:, par, :, :]
                        nc.vector.tensor_reduce(rs[:, :], p, X_AXIS, ALU.add).then_inc(step, 1)
                        dve.wait_ge(step, s + 2)
                        nc.vector.reciprocal(rr[:, :], rs[:, :]).then_inc(step, 1)
                        dve.wait_ge(step, s + 3)
                        nc.vector.tensor_tensor(p, p, wide(rr[:, :], E16), ALU.mult).then_inc(step, 1)
                        dve.wait_ge(step, s + 4)
                        stand_alone(dve, passed)
                        for j in range(GB):
                            nc.vector.max(top[:, j, :], pr[:, par, j, :]).then_inc(step, 1)
                        dve.wait_ge(step, s + 8)
                        stand_alone(dve, passed)
                        for j in range(GB):
                            nc.vector.max_index(idx[:, j, :], top[:, j, :], pr[:, par, j, :]).then_inc(step, 1)
                        nc.vector.tensor_copy(prob[:, bass.ds(n * GB, GB), :], top[:, :, 0:2]).then_inc(step, 1)
                        dve.wait_ge(step, s + 13)
                        nc.vector.tensor_copy(idf[:, :, :], idx[:, :, 0:2]).then_inc(step, 1)
                        dve.wait_ge(step, s + 14)
                        e_of = idf[:, :, :].rearrange("p g k -> p (g k)")
                        flat = lambda t: t.rearrange("p g k -> p (g k)")
                        nc.vector.tensor_tensor(chosen[:, par, :, :, :].rearrange("p g k e -> p (g k) e"),
                                                iota16[:, :].rearrange("p (a e) -> p a e", a=1).broadcast_to([T, 2 * GB, E16]),
                                                e_of.rearrange("p (q a) -> p q a", a=1).broadcast_to([T, 2 * GB, E16]),
                                                ALU.is_equal).then_inc(chosen_done, 1)
                        dve.wait_ge(chosen_done, n + 1)
                        dve.wait_ge(counted, n + 1)
                        nc.vector.tensor_tensor(ranks[:, :, :, :].rearrange("p g k e -> p (g k) e"),
                                                core.psum[:, COUNTS + par, 0:GB * 2 * E16].rearrange("p (q e) -> p q e", e=E16),
                                                chosen[:, par, :, :, :].rearrange("p g k e -> p (g k) e"), ALU.mult).then_inc(step, 1)
                        dve.wait_ge(step, s + 15)
                        nc.vector.tensor_reduce(flat(pos[:, :, :]), ranks[:, :, :, :].rearrange("p g k e -> p (g k) e"), X_AXIS, ALU.add).then_inc(step, 1)
                        nc.vector.tensor_scalar(flat(first_slot[:, :, :]), e_of, float(CAP), -1.0, ALU.mult, ALU.add).then_inc(step, 1)
                        dve.wait_ge(step, s + 17)
                        nc.vector.scalar_tensor_tensor(out=slot_read[:, bass.ds(n * GB, GB), :], in0=pos[:, :, :], scalar=float(CAP),
                                                       in1=first_slot[:, :, :], op0=ALU.min, op1=ALU.add).then_inc(step, 1)
                        nc.vector.tensor_scalar(flat(over[:, :, :]), flat(pos[:, :, :]), float(CAP), 4.0 * SLOTS, ALU.is_gt, ALU.mult).then_inc(half, 1)
                        dve.wait_ge(half, (2 + GB) * n + 1)
                        dve.wait_ge(step, s + 18)
                        nc.vector.tensor_tensor(slot_in[:, :, :], slot_read[:, bass.ds(n * GB, GB), :], over[:, :, :], ALU.add).then_inc(half, 1)
                        dve.wait_ge(half, (2 + GB) * n + 2)
                        for j in range(GB + 1):
                            if j < GB:
                                nc.vector.tensor_scalar(d1[:, j, :], iota256[:, :], slot_in[:, j, 0:1], None, ALU.is_equal).then_inc(half, 1)
                            if j > 0:
                                dve.wait_ge(half, (2 + GB) * n + 2 + j)
                                dve.wait_ge(xe_ready, GB * n + j - 1 + GB)
                                nc.vector.scalar_tensor_tensor(out=disp[:, (j - 1) % 2, :], in0=iota256[:, :], scalar=slot_in[:, j - 1, 1:2],
                                                               in1=d1[:, j - 1, :], op0=ALU.is_equal, op1=ALU.add).then_inc(disp_ready, 1)


def build_experts(core, taken):
    nc, inp = core.nc, core.inp
    GATE, UP, DOWN = 0, 2, 4
    N = B * CAP
    DEEP = 4
    with Stage(core, "experts") as st:
        wg = st.sb("wg", [C, DEEP, HID])
        wu = st.sb("wu", [C, DEEP, HID])
        wp = st.sb("wp", [HID, DEEP, C])
        sg = st.sb("sg", [HID, 2, N])
        gs = st.sb("gs", [HID, 2, N])
        hid = st.sb("hid", [HID, 2, N])
        loaded = [st.sem(f"loaded{k}") for k in range(DEEP)]
        up_ready, sig_done, gated, hid_ready, down_ready, down_done = (st.sem(n) for n in (
            "up_ready", "sig_done", "gated", "hid_ready", "down_ready", "down_done"))
        passed = st.sem("passed")
        with nc.Block() as block:
            @block.sync
            def _(sp):
                st.clear_retired(sp)

                def load(e, k):
                    sp.dma_start(wg[:, k, :], inp['L0_ffn_w_gate'].rearrange("e c h -> c e h")[:, e, :]).then_inc(loaded[k], 16)
                    sp.dma_start(wu[:, k, :], inp['L0_ffn_w_fc'].rearrange("e c h -> c e h")[:, e, :]).then_inc(loaded[k], 16)
                    sp.dma_start(wp[:, k, :], inp['L0_ffn_w_proj'].rearrange("e h c -> h e c")[:, e, :]).then_inc(loaded[k], 16)
                for k in range(DEEP):
                    load(k, k)
                with sp.Fori(1, E16 // DEEP) as i:
                    for k in range(DEEP):
                        sp.wait_ge(down_ready, DEEP * i + k - DEEP + 1)
                        load(DEEP * i + k, k)

            @block.tensor
            def _(pe):
                def up(i, k):
                    e, par = DEEP * i + k, k % 2
                    pe.wait_ge(loaded[k], 48 * i + 48)
                    pe.wait_ge(hid_ready, e)
                    rhs = taken[:, bass.ds(e, 1), :, :].rearrange("p a b s -> p (a b s)")
                    nc.tensor.matmul(core.psum[0:HID, GATE + par, :], wg[:, k, :], rhs, start=True, stop=True).then_inc(up_ready, 1)
                    nc.tensor.matmul(core.psum[0:HID, UP + par, :], wu[:, k, :], rhs, start=True, stop=True).then_inc(up_ready, 1)

                def down(e, k):
                    par = k % 2
                    pe.wait_ge(hid_ready, e + 2)
                    pe.wait_ge(down_done, e)
                    nc.tensor.matmul(core.psum[:, DOWN + par, :], wp[:, k, :], hid[:, par, :], start=True, stop=True).then_inc(down_ready, 1)

                def experts(i, first):
                    for k in range(DEEP):
                        up(i, k)
                        if not (first and k == 0):
                            down(DEEP * i + k - 1, (k - 1) % DEEP)
                experts(0, True)
                with pe.Fori(1, E16 // DEEP) as i:
                    experts(i, False)
                down(E16 - 1, DEEP - 1)

            @block.scalar
            def _(act):
                act.sem_inc(down_done, 1)

                def sigmoid(e, par):
                    act.wait_ge(up_ready, 2 * e + 1)
                    act.wait_ge(gated, e)
                    nc.scalar.activation(sg[:, par, :], core.psum[0:HID, GATE + par, :], ACT.Sigmoid).then_inc(sig_done, 1)

                def copy_down(e, par):
                    act.wait_ge(down_ready, e + 1)
                    nc.scalar.activation(taken[:, bass.ds(e, 1), :, :].rearrange("p a b s -> p (a b s)"), core.psum[:, DOWN + par, :],
                                         ACT.Identity).then_inc(down_done, 1)

                def pair(i, first):
                    for par in range(2):
                        sigmoid(2 * i + par, par)
                        if not (first and par == 0):
                            copy_down(2 * i + par - 1, 1 - par)
                pair(0, True)
                with act.Fori(1, E16 // 2) as i:
                    pair(i, False)
                copy_down(E16 - 1, 1)

            @block.vector
            def _(dve):
                dve.sem_inc(gated, 1)
                dve.sem_inc(hid_ready, 1)
                dve.wait_ge(gated, 1)
                with dve.Fori(0, E16 // 2) as i:
                    for par in range(2):
                        e = 2 * i + par
                        dve.wait_ge(sig_done, e + 1)
                        nc.vector.tensor_tensor(gs[:, par, :], core.psum[0:HID, GATE + par, :], sg[:, par, :], ALU.mult).then_inc(gated, 1)
                        dve.wait_ge(gated, e + 2)
                        dve.wait_ge(up_ready, 2 * e + 2)
                        nc.vector.tensor_tensor(hid[:, par, :], core.psum[0:HID, UP + par, :], gs[:, par, :], ALU.mult).then_inc(hid_ready, 1)


def build_combine(core, taken, slot_read, prob):
    nc = core.nc
    with Stage(core, "combine") as st:
        iota256 = st.sb("iota256", [T, SLOTS])
        c1 = st.sb("c1", [T, 2, SLOTS])
        c2 = st.sb("c2", [T, 2, SLOTS])
        cw = st.sb("cw", [T, 2, SLOTS])
        eo = st.sb("eo", [C, 2, SLOTS])
        cwT = st.sb("cwT", [128, 2, 2, T])
        eoT = st.sb("eoT", [128, 2, 2, C])
        consts, eo_ready, step, cw_ready, cwT_ready, eoT_ready, cwT_done, eoT_done, y_ready, y_done = (st.sem(n) for n in (
            "consts", "eo_ready", "step", "cw_ready", "cwT_ready", "eoT_ready", "cwT_done", "eoT_done", "y_ready", "y_done"))
        CW_BANK, EO_BANK, Y_BANK = 0, 2, 4
        passed = st.sem("passed")
        with nc.Block() as block:
            @block.gpsimd
            def _(pool):
                st.clear_retired(pool)
                nc.gpsimd.iota(iota256[:, :], pattern=[[1, SLOTS]], base=0, channel_multiplier=0, allow_small_or_imprecise_dtypes=True).then_inc(consts, 1)
                with pool.Fori(0, B // 2) as i:
                    for par in range(2):
                        b = 2 * i + par
                        pool.wait_ge(eoT_ready, b + 1)
                        nc.gpsimd.tensor_copy(eo[:, par, :].rearrange("p (e a s) -> p e a s", e=E16, a=1),
                                              taken[:, :, bass.ds(b, 1), :]).then_inc(eo_ready, 1)

            @block.tensor
            def _(pe):
                pe.sem_inc(eoT_ready, 2)
                pe.sem_inc(y_ready, 2)
                pe.sem_inc(cwT_ready, 1)

                def turn(b, par):
                    pe.wait_ge(cw_ready, b + 1)
                    pe.wait_ge(cwT_done, b)
                    for s in range(2):
                        mm = nc.tensor.transpose(core.psum[:, CW_BANK + par, s * T:(s + 1) * T], cw[:, par, s * 128:(s + 1) * 128], core.ident[:, :])
                    mm.then_inc(cwT_ready, 1)
                    pe.wait_ge(eo_ready, b + 1)
                    pe.wait_ge(eoT_done, b)
                    for s in range(2):
                        mm = nc.tensor.transpose(core.psum[:, EO_BANK + par, s * C:(s + 1) * C], eo[:, par, s * 128:(s + 1) * 128], core.ident[:, :])
                    mm.then_inc(eoT_ready, 1)

                def gather(b, par):
                    pe.wait_ge(cwT_done, b + 2)
                    pe.wait_ge(eoT_done, b + 2)
                    pe.wait_ge(y_done, b)
                    for s in range(2):
                        mm = nc.tensor.matmul(core.psum[:, Y_BANK + par, 0:C], cwT[:, par, s, :], eoT[:, par, s, :], start=(s == 0), stop=(s == 1))
                    mm.then_inc(y_ready, 1)

                def pair(i, first):
                    for par in range(2):
                        turn(2 * i + par, par)
                        if not first:
                            gather(2 * i + par - 2, par)
                pair(0, True)
                with pe.Fori(1, B // 2) as i:
                    pair(i, False)
                gather(B - 2, 0)
                gather(B - 1, 1)

            @block.scalar
            def _(act):
                act.sem_inc(cwT_done, 1)
                act.sem_inc(eoT_done, 1)
                with act.Fori(0, B // 2) as i:
                    for par in range(2):
                        b = 2 * i + par
                        act.wait_ge(cwT_ready, b + 2)
                        act.wait_ge(y_ready, b + 1)
                        nc.scalar.activation(cwT[:, par, :, :], core.psum[:, CW_BANK + par, 0:SLOTS].rearrange("p (s t) -> p s t", s=2),
                                             ACT.Identity).then_inc(cwT_done, 1)
                        act.wait_ge(eoT_ready, b + 3)
                        nc.scalar.activation(eoT[:, par, :, :], core.psum[:, EO_BANK + par, 0:SLOTS].rearrange("p (s c) -> p s c", s=2),
                                             ACT.Identity).then_inc(eoT_done, 1)

            @block.vector
            def _(dve):
                dve.wait_ge(consts, 1)
                dve.sem_inc(y_done, 1)

                def marks(b, par):
                    for k, dst in enumerate((c1, c2)):
                        nc.vector.tensor_scalar(dst[:, par, :], iota256[:, :], slot_read[:, b, k:k + 1], prob[:, b, k:k + 1],
                                                ALU.is_equal, ALU.mult).then_inc(step, 1)

                def weights(b, par):
                    dve.wait_ge(step, 2 * b + 2)
                    dve.wait_ge(cwT_ready, b)
                    nc.vector.tensor_tensor(cw[:, par, :], c1[:, par, :], c2[:, par, :], ALU.add).then_inc(cw_ready, 1)

                def keep(b, par):
                    dve.wait_ge(y_ready, b + 3)
                    stand_alone(dve, passed)
                    nc.vector.tensor_copy(core.branch[:, b, :], core.psum[:, Y_BANK + par, 0:C]).then_inc(y_done, 1)

                def pair(i, first, last_pair):
                    for par in range(2):
                        b = 2 * i + par
                        if not (last_pair and par == 1):
                            marks(b + 1, 1 - par)
                            weights(b + 1, 1 - par)
                        if not first:
                            keep(b - 2, par)

                marks(0, 0)
                weights(0, 0)
                pair(0, True, False)
                with dve.Fori(1, B // 2 - 1) as i:
                    pair(i, False, False)
                pair(B // 2 - 1, False, True)
                keep(B - 2, 0)
                keep(B - 1, 1)


def build_attention64(core, name, wq, wk, wv, wo, later=()):
    nc, inp = core.nc, core.inp
    scale = float(D64) ** -0.5
    nk = NCTX
    INNER = H * D64
    QK = 2 * T + 2 * nk
    S_BANK, T_BANK, OT_BANK, Y_BANK, QK_BANK, V_BANK = 0, 2, 4, 5, 6, 7
    with Stage(core, name) as st:
        xc = st.sb("xc", [C, 2, T])
        cc = st.sb("cc", [CC, 2, nk])
        qT = st.sb("qT", [128, NU, 2, T])
        keys_q = st.sb("keys_q", [128, NU, 2, 2, nk])
        va = st.sb("va", [nk, NU, QUAD, D64])
        sc = st.sb("sc", [T, NU, QUAD, nk])
        pT = st.sb("pT", [nk, 2, QUAD, T])
        oT = st.sb("oT", [128, 2, 2, T])
        negmax = st.sb("negmax", [T, 2, QUAD])
        total = st.sb("total", [T, 2, QUAD])
        rden = st.sb("rden", [T, 2, QUAD])
        arrived, consts, src_ready, qk_projected, v_projected = (
            st.sem(n) for n in ("arrived", "consts", "src_ready", "qk_projected", "v_projected"))
        qk_done, v_done, scored, max_step, shifted, p_ready, turned, pT_ready = (st.sem(n) for n in (
            "qk_done", "v_done", "scored", "max_step", "shifted", "p_ready", "turned", "pT_ready"))
        summed, recip_step, normed, weighed, oT_done, y_ready, y_done = (st.sem(n) for n in (
            "summed", "recip_step", "normed", "weighed", "oT_done", "y_ready", "y_done"))
        UNITS = NU * B

        passed = st.sem("passed")
        with nc.Block() as block:
            @block.sync
            def _(sp):
                prefetch(sp, later, arrived)

            @block.gpsimd
            def _(pool):
                st.clear_retired(pool)
                nc.gpsimd.memset(keys_q[:, :, :, :, :], 0.0).then_inc(consts, 1)
                with pool.Fori(0, B // 2) as i:
                    for par in range(2):
                        b = 2 * i + par
                        pool.wait_ge(v_projected, NU * b + 1)
                        nc.gpsimd.tensor_copy(xc[:, par, :], core.xT[:, b, :]).then_inc(src_ready, 1)
                        nc.gpsimd.tensor_copy(cc[:, par, :], core.ctxT[:, b, :]).then_inc(src_ready, 1)

            @block.tensor
            def _(pe):
                pe.sem_inc(v_projected, NU + 1)
                pe.wait_ge(consts, 1)

                def project_qk(b, par, g):
                    u = NU * b + g
                    if g == 0:
                        pe.wait_ge(src_ready, 2 * b + 2)
                    pe.wait_ge(qk_done, 3 * u)
                    for k in range(2):
                        cols = slice((2 * g + k) * 128, (2 * g + k + 1) * 128)
                        nc.tensor.matmul(core.psum[:, QK_BANK, k * T:(k + 1) * T], wq[:, cols], xc[:, par, :], start=True, stop=True)
                        mm = nc.tensor.matmul(core.psum[:, QK_BANK, 2 * T + k * nk:2 * T + (k + 1) * nk], wk[:, cols], cc[:, par, :],
                                              start=True, stop=True)
                    mm.then_inc(qk_projected, 1)

                def project_v(b, par, g):
                    pe.wait_ge(v_done, NU * b + g)
                    nc.tensor.matmul(core.psum[0:nk, V_BANK, 0:QUAD * D64], cc[:, par, :], wv[:, g * QUAD * D64:(g + 1) * QUAD * D64],
                                     start=True, stop=True).then_inc(v_projected, 1)

                def score(b, par, g):
                    u = NU * b + g
                    pe.wait_ge(qk_done, 3 * u + 3)
                    pe.wait_ge(shifted, u)
                    for k in range(2):
                        mm = nc.tensor.matmul(core.psum[:, S_BANK + g % 2, 2 * k * nk:2 * (k + 1) * nk], qT[:, g, k, :], keys_q[:, g, k, :, :],
                                              start=True, stop=True)
                    mm.then_inc(scored, 1)

                def turn(b, par, g):
                    u = NU * b + g
                    pe.wait_ge(normed, u + 1)
                    pe.wait_ge(pT_ready, u)
                    for j in range(QUAD):
                        mm = nc.tensor.transpose(core.psum[0:nk, T_BANK + g % 2, j * T:(j + 1) * T], sc[:, g, j, :], core.ident[:, :])
                    mm.then_inc(turned, 1)

                def weigh(b, par, g):
                    u = NU * b + g
                    pe.wait_ge(pT_ready, u + 2)
                    pe.wait_ge(v_done, u + 1)
                    pe.wait_ge(oT_done, u)
                    for j in range(QUAD):
                        rows = slice(D64 * (j % 2), D64 * (j % 2) + D64)
                        mm = nc.tensor.matmul(core.psum[rows, OT_BANK, (j // 2) * T:(j // 2 + 1) * T], va[:, g, j, :], pT[:, g % 2, j, :],
                                              start=True, stop=True, tile_position=(0, rows.start))
                    mm.then_inc(weighed, 1)

                def out_project(b, par, g):
                    u = NU * b + g
                    pe.wait_ge(oT_done, u + 1)
                    if g == 0:
                        pe.wait_ge(y_done, b)
                    for k in range(2):
                        mm = nc.tensor.matmul(core.psum[:, Y_BANK, 0:C], oT[:, g % 2, k, :], wo[:, 2 * g + k, :],
                                              start=(g == 0 and k == 0), stop=(g == NU - 1 and k == 1))
                    if g == NU - 1:
                        mm.then_inc(y_ready, 1)

                steps = [(score, 0), (turn, 2), (weigh, 3), (out_project, 4), (project_qk, -2), (project_v, -1)]

                def at(i, par, g, back):
                    t = NU * par + g - back
                    return 2 * i + t // NU, (t // NU) % 2, t % NU

                def pair(i, first, last):
                    for par in range(2):
                        for g in range(NU):
                            for step, back in steps:
                                t = NU * par + g - back
                                if (first and t < 0) or (last and t >= 2 * NU):
                                    continue
                                step(*at(i, par, g, back))

                project_qk(0, 0, 0)
                project_v(0, 0, 0)
                project_qk(0, 0, 1)
                pair(0, True, False)
                with pe.Fori(1, B // 2 - 1) as i:
                    pair(i, False, False)
                pair(B // 2 - 1, False, True)
                for over in range(4):
                    for step, back in steps:
                        t = 2 * NU + over - back
                        if back > over:
                            step(*at(B // 2 - 1, 0, 2 * NU + over, back))

            @block.scalar
            def _(act):
                act.sem_inc(pT_ready, 1)

                def copy_qk(u, g):
                    act.wait_ge(qk_projected, u + 1)
                    nc.scalar.activation(qT[:, g, :, :], core.psum[:, QK_BANK, 0:2 * T].rearrange("p (k t) -> p k t", k=2),
                                         ACT.Identity).then_inc(qk_done, 1)
                    for a in range(2):
                        rows = slice(D64 * a, D64 * a + D64)
                        nc.scalar.activation(keys_q[rows, g, :, a, :], core.psum[rows, QK_BANK, 2 * T:QK].rearrange("p (k n) -> p k n", k=2),
                                             ACT.Identity).then_inc(qk_done, 1)

                def exponential(u, g):
                    act.wait_ge(shifted, u + 2)
                    nc.scalar.activation(sc[:, g, :, :], sc[:, g, :, :], ACT.Exp, scale=scale).then_inc(p_ready, 1)

                def copy_pT(u, g):
                    act.wait_ge(turned, u + 1)
                    nc.scalar.activation(pT[:, g % 2, :, :], core.psum[0:nk, T_BANK + g % 2, :].rearrange("p (j t) -> p j t", j=QUAD),
                                         ACT.Identity).then_inc(pT_ready, 1)

                def copy_oT(u, g):
                    act.wait_ge(weighed, u + 1)
                    nc.scalar.activation(oT[:, g % 2, :, :], core.psum[:, OT_BANK, 0:2 * T].rearrange("p (k t) -> p k t", k=2),
                                         ACT.Identity).then_inc(oT_done, 1)

                steps = [(exponential, 0), (copy_pT, 2), (copy_oT, 3), (copy_qk, -2)]

                def pair(i, first, last):
                    for t0 in range(2 * NU):
                        for step, back in steps:
                            t = t0 - back
                            if (first and t < 0) or (last and t >= 2 * NU):
                                continue
                            step(2 * NU * i + t, t % NU)

                act.wait_ge(consts, 1)
                copy_qk(0, 0)
                copy_qk(1, 1)
                pair(0, True, False)
                with act.Fori(1, B // 2 - 1) as i:
                    pair(i, False, False)
                pair(B // 2 - 1, False, True)
                for over in range(3):
                    for step, back in steps:
                        if back > over:
                            step(UNITS + over - back, (over - back) % NU)

            @block.vector
            def _(dve):
                dve.sem_inc(shifted, 1)

                def copy_v(u, g, fresh=False):
                    dve.wait_ge(v_projected, u + 2 + NU)
                    if not fresh:
                        dve.wait_ge(weighed, u - NU + 1)
                    nc.vector.tensor_copy(va[:, g, :, :], core.psum[0:nk, V_BANK, 0:QUAD * D64].rearrange("p (j d) -> p j d", j=QUAD)).then_inc(v_done, 1)

                def scores(g):
                    return core.psum[:, S_BANK + g % 2, 0:QUAD * nk].rearrange("p (j n) -> p j n", j=QUAD)

                def maximum(u, g):
                    dve.wait_ge(scored, u + 1)
                    nc.vector.tensor_reduce(negmax[:, g % 2, :], scores(g), X_AXIS, ALU.max, negate=True).then_inc(max_step, 1)

                def shift(u, g, fresh):
                    dve.wait_ge(max_step, u + 1)
                    if not fresh:
                        dve.wait_ge(turned, u - NU + 1)
                    nm = negmax[:, g % 2, :].rearrange("p (q a) -> p q a", a=1).broadcast_to([T, QUAD, nk])
                    nc.vector.tensor_tensor(sc[:, g, :, :], scores(g), nm, ALU.add).then_inc(shifted, 1)

                def add_up(u, g):
                    dve.wait_ge(p_ready, u + 1)
                    nc.vector.tensor_reduce(total[:, g % 2, :], sc[:, g, :, :], X_AXIS, ALU.add).then_inc(summed, 1)

                def invert(u, g):
                    dve.wait_ge(summed, u + 1)
                    nc.vector.reciprocal(rden[:, g % 2, :], total[:, g % 2, :]).then_inc(recip_step, 1)

                def norm(u, g):
                    dve.wait_ge(recip_step, u + 1)
                    rd = rden[:, g % 2, :].rearrange("p (j a) -> p j a", a=1).broadcast_to([T, QUAD, nk])
                    nc.vector.tensor_tensor(sc[:, g, :, :], sc[:, g, :, :], rd, ALU.mult).then_inc(normed, 1)

                def keep_y(b):
                    dve.wait_ge(y_ready, b + 1)
                    stand_alone(dve, passed)
                    nc.vector.tensor_copy(core.branch[:, b, :], core.psum[:, Y_BANK, 0:C]).then_inc(y_done, 1)

                steps = [(maximum, 0), (add_up, 1), (shift, 0), (invert, 1), (norm, 1), (copy_v, -1)]

                def pair(i, first, last):
                    for t0 in range(2 * NU):
                        for step, back in steps:
                            t = t0 - back
                            if (first and t < 0) or (last and t >= 2 * NU):
                                continue
                            if step is copy_v or step is shift:
                                step(2 * NU * i + t, t % NU, first and t < NU)
                            else:
                                step(2 * NU * i + t, t % NU)
                        if t0 % NU == NU - 1 and not (first and t0 < NU):
                            keep_y(2 * i + t0 // NU - 1)

                copy_v(0, 0, True)
                pair(0, True, False)
                with dve.Fori(1, B // 2 - 1) as i:
                    pair(i, False, False)
                pair(B // 2 - 1, False, True)
                for step in (add_up, invert, norm):
                    step(UNITS - 1, NU - 1)
                keep_y(B - 1)


def build_gate(core, gate, mixed_bias):
    nc, inp = core.nc, core.inp
    E4, HG = 4, 128
    with Stage(core, "gate") as st:
        w1 = st.sb("w1", [C, HG])
        b1 = st.sb("b1", [HG, 1])
        w2 = st.sb("w2", [HG, E4])
        b2 = st.sb("b2", [1, E4])
        be = st.sb("be", [E4, 3, C])
        pooled = st.sb("pooled", [C, B])
        mean = st.sb("mean", [C, B])
        hid = st.sb("hid", [HG, B])
        lg = st.sb("lg", [B, 8])
        top = st.sb("top", [B, 8])
        idx = st.sb("idx", [B, 8], U32)
        idf = st.sb("idf", [B, 2])
        diff = st.sb("diff", [B, 2])
        ex = st.sb("ex", [B, 2])
        sm = st.sb("sm", [B, 2])
        total = st.sb("total", [B, 2])
        iota4 = st.sb("iota4", [B, E4])
        w_1 = st.sb("w_1", [B, E4])
        w_2 = st.sb("w_2", [B, E4])
        w = st.sb("w", [B, E4])
        wT = st.sb("wT", [E4, B])
        diag = st.sb("diag", [B, B, E4])
        loaded, consts, step, mm, acted = (st.sem(n) for n in ("loaded", "consts", "step", "mm", "acted"))
        passed = st.sem("passed")
        with nc.Block() as block:
            @block.sync
            def _(sp):
                n = 0
                for dst, src in ((w1[:, :], inp['L1_ffn_Wg1'][:, :]), (b1[:, :], col(inp['L1_ffn_bg1'])), (w2[:, :], inp['L1_ffn_Wg2'][:, :]),
                                 (b2[:, :], row(inp['L1_ffn_bg2'])), (be[:, 0, :], inp['L1_ffn_bq'][:, :]), (be[:, 1, :], inp['L1_ffn_bk'][:, :]),
                                 (be[:, 2, :], inp['L1_ffn_bv'][:, :])):
                    sp.dma_start(dst, src).then_inc(loaded, 16)
                    n += 1
                sp.wait_ge(loaded, 16 * n)

            @block.gpsimd
            def _(pool):
                st.clear_retired(pool)
                nc.gpsimd.iota(iota4[:, :], pattern=[[1, E4]], base=0, channel_multiplier=0, allow_small_or_imprecise_dtypes=True).then_inc(consts, 1)

            @block.tensor
            def _(pe):
                pe.wait_ge(loaded, 16 * 7)
                pe.wait_ge(step, 2)
                nc.tensor.matmul(core.psum[0:HG, 0, 0:B], w1[:, :], mean[:, :], start=True, stop=True).then_inc(mm, 1)
                pe.wait_ge(step, 3)
                nc.tensor.matmul(core.psum[0:B, 1, 0:E4], hid[:, :], w2[:, :], start=True, stop=False)
                nc.tensor.matmul(core.psum[0:B, 1, 0:E4], core.ones[0:1, 0:B], b2[:, :], start=False, stop=True).then_inc(mm, 1)
                pe.wait_ge(step, 14)
                nc.tensor.transpose(core.psum[0:E4, 2, 0:B], w[:, :], core.ident[0:B, 0:B]).then_inc(mm, 1)
                pe.wait_ge(step, 15)
                nc.tensor.matmul(core.psum[:, 3, 0:B * E4], core.ones[0:B, :], diag[:, :, :].rearrange("p b e -> p (b e)"), start=True, stop=True).then_inc(mm, 1)
                pe.wait_ge(step, 16)
                for k in range(3):
                    nc.tensor.matmul(core.psum[:, 4 + k, 0:B], be[:, k, :], wT[:, :], start=True, stop=True).then_inc(mm, 1)

            @block.scalar
            def _(act):
                act.wait_ge(step, 7)
                nc.scalar.activation(ex[:, :], diff[:, :], ACT.Exp).then_inc(acted, 1)

            @block.vector
            def _(dve):
                v = nc.vector
                dve.wait_ge(loaded, 16 * 7)
                dve.wait_ge(consts, 1)
                v.tensor_reduce(pooled[:, :], core.xT[:, :, :], X_AXIS, ALU.add).then_inc(step, 1)
                dve.wait_ge(step, 1)
                v.tensor_scalar(mean[:, :], pooled[:, :], 1.0 / T, None, ALU.mult).then_inc(step, 1)
                dve.wait_ge(mm, 1)
                v.tensor_scalar(hid[:, :], core.psum[0:HG, 0, 0:B], b1[:, :], 0.0, ALU.add, ALU.max).then_inc(step, 1)
                v.memset(lg[:, :], NEG).then_inc(step, 1)
                dve.wait_ge(mm, 2)
                dve.wait_ge(step, 4)
                v.tensor_copy(lg[:, 0:E4], core.psum[0:B, 1, 0:E4]).then_inc(step, 1)
                dve.wait_ge(step, 5)
                v.max(top[:, :], lg[:, :]).then_inc(step, 1)
                dve.wait_ge(step, 6)
                v.tensor_scalar(diff[:, :], top[:, 0:2], top[:, 0:1], None, ALU.subtract).then_inc(step, 1)
                v.max_index(idx[:, :], top[:, :], lg[:, :]).then_inc(step, 1)
                dve.wait_ge(step, 8)
                v.tensor_copy(idf[:, :], idx[:, 0:2]).then_inc(step, 1)
                dve.wait_ge(acted, 1)
                v.tensor_reduce(total[:, 0:1], ex[:, :], X_AXIS, ALU.add).then_inc(step, 1)
                dve.wait_ge(step, 10)
                v.reciprocal(total[:, 1:2], total[:, 0:1]).then_inc(step, 1)
                dve.wait_ge(step, 11)
                v.tensor_scalar(sm[:, :], ex[:, :], total[:, 1:2], None, ALU.mult).then_inc(step, 1)
                dve.wait_ge(step, 12)
                v.tensor_scalar(w_1[:, :], iota4[:, :], idf[:, 0:1], sm[:, 0:1], ALU.is_equal, ALU.mult).then_inc(step, 1)
                v.tensor_scalar(w_2[:, :], iota4[:, :], idf[:, 1:2], sm[:, 1:2], ALU.is_equal, ALU.mult).then_inc(acted, 1)
                dve.wait_ge(step, 13)
                dve.wait_ge(acted, 2)
                v.tensor_tensor(w[:, :], w_1[:, :], w_2[:, :], ALU.add).then_inc(step, 1)
                dve.wait_ge(step, 14)
                v.tensor_tensor(diag[:, :, :], core.ident[0:B, 0:B].rearrange("p (b a) -> p b a", a=1).broadcast_to([B, B, E4]),
                                w[:, :].rearrange("p (a e) -> p a e", a=1).broadcast_to([B, B, E4]), ALU.mult).then_inc(step, 1)
                dve.wait_ge(mm, 3)
                v.tensor_copy(wT[:, :], core.psum[0:E4, 2, 0:B]).then_inc(step, 1)
                dve.wait_ge(mm, 4)
                v.tensor_copy(gate[:, :], core.psum[:, 3, 0:B * E4]).then_inc(acted, 1)
                dve.wait_ge(mm, 7)
                v.tensor_copy(mixed_bias[:, :, :], core.psum[:, 4:7, 0:B]).then_inc(acted, 1)


def build(nc, inp, out, stages=None):
    with ExitStack() as ctx:
        core = Core(nc, ctx, inp, out)
        recip_all = core.sb("recip_all", [T, B, H])
        taken = core.sb("taken", [C, E16, B, CAP])
        slot_read = core.sb("slot_read", [T, B, 2])
        prob = core.sb("prob", [T, B, 2])
        gate = core.sb("gate", [128, B * 4])
        mixed_bias = core.sb("mixed_bias", [C, 3, B])
        experts = core.sb("experts", [C, 4, 3 * C])
        inner = H * D64
        w_q, w_k, w_v = core.sb("xattn1_wq", [C, inner]), core.sb("xattn1_wk", [CC, inner]), core.sb("xattn1_wv", [CC, inner])
        w_o = core.sb("xattn1_wo", [128, inner // 128, C])
        xattn1_weights = [(w_q[:, :], inp['L1_xattn_Wq'][:, :]), (w_k[:, :], inp['L1_xattn_Wk'][:, :]), (w_v[:, :], inp['L1_xattn_Wv'][:, :]),
                          (w_o[:, :, :], inp['L1_xattn_Wo'].rearrange("(t p) c -> p t c", p=128))]
        ffn1_weights = [(experts[:, :, k * C:(k + 1) * C], inp[name].rearrange("e c d -> c e d"))
                        for k, name in enumerate(('L1_ffn_Wq', 'L1_ffn_Wk', 'L1_ffn_Wv'))]
        steps = [
            lambda: build_setup(core),
            lambda: build_gru(core),
            lambda: build_close(core, "close0", turned=True),
            lambda: build_attention8(core, "xattn0", NCTX, inp['L0_xattn_Wq'][:, :], inp['L0_xattn_Wk'][:, :], inp['L0_xattn_Wv'][:, :],
                                     cross=True, b_q=inp['L0_xattn_bq'], b_k=inp['L0_xattn_bk'], clip=True, recip_all=recip_all),
            lambda: build_close(core, "close1", wo=inp['L0_xattn_Wo'][:, :], v_bias=inp['L0_xattn_bv'], out_bias=inp['L0_xattn_bo'], nan_guard=(recip_all, inp['L0_xattn_Wv'][:, :])),
            lambda: build_route(core, taken, slot_read, prob),
            lambda: build_experts(core, taken),
            lambda: build_combine(core, taken, slot_read, prob),
            lambda: build_close(core, "close2"),
            lambda: build_attention8(core, "attn1", T, None, None, None, transposed=(4, 5, 6), causal=True, guard=True,
                                     later=xattn1_weights),
            lambda: build_close(core, "close3", wo=core.wT[:, 7, :]),
            lambda: build_attention64(core, "xattn1", w_q, w_k, w_v, w_o, later=ffn1_weights),
            lambda: build_close(core, "close4", out_bias=inp['L1_xattn_bo']),
            lambda: build_gate(core, gate, mixed_bias),
            lambda: build_attention8(core, "ffn1", T, None, None, None, mixed=(gate, mixed_bias, experts)),
            lambda: build_close(core, "close5", wo=inp['L1_ffn_Wo'][:, :], v_bias_by_batch=mixed_bias[:, 2, :], out_bias=inp['L1_ffn_bo'],
                                last=True),
        ]
        n = len(steps) if stages is None else stages
        for step in steps[:n]:
            step()


def kernel(**inputs):
    import numpy as np
    import concourse.bacc as bacc
    from concourse.bass_utils import run_bass_kernel_spmd

    nc = bacc.Bacc("TRN2", target_bir_lowering=False, num_devices=1)
    arrays, inp = {}, {}
    for name in INS:
        a = np.ascontiguousarray(inputs[name])
        arrays[f"in_{name}_dram"] = a
        inp[name] = nc.dram_tensor(f"in_{name}_dram", a.shape, mybir.dt.from_np(a.dtype), kind="ExternalInput").ap()
    out = nc.dram_tensor("out_0_dram", (B, T, C), F32, kind="ExternalOutput").ap()
    build(nc, inp, out)
    return run_bass_kernel_spmd(nc, [arrays], core_ids=[0]).results[0]["out_0_dram"]
```
